# Optimizing a Trainium2 kernel written in Bass

```python
import numpy as np
import jax
import jax.numpy as jnp

def _softmax(x, axis=-1):
    return jax.nn.softmax(x, axis=axis)

def _gelu(x):
    return jax.nn.gelu(x, approximate=True)

def _silu(x):
    return jax.nn.silu(x)

def _sigmoid(x):
    return jax.nn.sigmoid(x)

def _layernorm(x, axis=-1, eps=1e-05):
    m = jnp.mean(x, axis=axis, keepdims=True)
    v = jnp.var(x, axis=axis, keepdims=True)
    return (x - m) / jnp.sqrt(v + eps)

def _scatter_add(tgt, idx, src, axis=0):
    return tgt.at[idx].add(src)

def _segment_sum(src, seg, n):
    return jax.ops.segment_sum(src, seg, n)
kernel_name = 'mk_flamingo_gated_d2_seqx_r4_d90d05'

def setup_inputs(seed: int=0):
    np.random.seed(seed)
    _w = jnp.asarray

    def _rec_inputs():
        import jax
        import jax.numpy as jnp
        _rk = jax.random.key(seed)
        x = -0.0005207 + 1.001 * jax.random.normal(jax.random.fold_in(_rk, 1), (16, 256, 256), jnp.float32)
        _lenS = 256 - jax.random.randint(jax.random.fold_in(_rk, 7), (16,), 0, max(1, 256 // 4) + 1, jnp.int32)
        _lenS2 = 256 - jax.random.randint(jax.random.fold_in(_rk, 8), (16,), 0, max(1, 256 // 4) + 1, jnp.int32)
        _ctx_1024P = jax.random.normal(jax.random.fold_in(_rk, 11), (16, 16, 256), jnp.float32)
        _ctx_1024c = jax.random.dirichlet(jax.random.fold_in(_rk, 511), 0.3 * jnp.ones((16,), jnp.float32), (16, 256))
        _ctx_1024t = jnp.einsum('bsk,bkd->bsd', _ctx_1024c, _ctx_1024P)
        _ctx_1024t = _ctx_1024t * jax.lax.rsqrt(jnp.mean(jnp.square(_ctx_1024t)) + 1e-12) * 0.953939
        ctx_1024 = -0.000514642 + 1.00011 * (_ctx_1024t + 0.3 * jax.random.normal(jax.random.fold_in(_rk, 611), (16, 256, 256), jnp.float32))
        _g = jax.random.normal(jax.random.fold_in(_rk, 9001), (2, 2), jnp.float32)
        _g = jnp.sign(_g) * jnp.maximum(jnp.abs(_g), 1.0) + (_g == 0) * 1.0
        g_xattn = _g[0]
        g_ffn = _g[1]
        return (x, ctx_1024, g_xattn, g_ffn)
    x, ctx_1024, g_xattn, g_ffn = _rec_inputs()

    def _L0_xattn_setup():
        import jax, jax.numpy as jnp
        import numpy as np
        B, S, NDIMS, NHEADS, NPOS = (1, 512, 256, 16, 64)
        PER_HEAD = NDIMS // NHEADS

        def cope(query, attn_logits, pos_emb):
            npos_max = pos_emb.shape[-1]
            gates = jax.nn.sigmoid(attn_logits)
            pos = jnp.flip(jnp.cumsum(jnp.flip(gates, axis=-1), axis=-1), axis=-1)
            pos = jnp.minimum(pos, npos_max - 1)
            pos_ceil = jnp.ceil(pos).astype(jnp.int32)
            pos_floor = jnp.floor(pos).astype(jnp.int32)
            logits_int = jnp.einsum('bhqd,dn->bhqn', query, pos_emb)
            logits_ceil = jnp.take_along_axis(logits_int, pos_ceil, axis=-1)
            logits_floor = jnp.take_along_axis(logits_int, pos_floor, axis=-1)
            w = pos - pos_floor
            return logits_ceil * w + logits_floor * (1.0 - w)
        key = jax.random.key(seed)
        ks = jax.random.split(key, 9)
        sc = 1.0 / np.sqrt(NDIMS)
        inp = {'q': jax.random.normal(ks[0], (B, S, NDIMS), jnp.float32), 'k': jax.random.normal(ks[1], (B, S, NDIMS), jnp.float32), 'v': jax.random.normal(ks[2], (B, S, NDIMS), jnp.float32), 'Wq_w': jax.random.normal(ks[3], (NDIMS, NDIMS), jnp.float32) * sc, 'Wq_b': jnp.zeros((NDIMS,), jnp.float32), 'Wk_w': jax.random.normal(ks[4], (NDIMS, NDIMS), jnp.float32) * sc, 'Wk_b': jnp.zeros((NDIMS,), jnp.float32), 'Wv_w': jax.random.normal(ks[5], (NDIMS, NDIMS), jnp.float32) * sc, 'Wv_b': jnp.zeros((NDIMS,), jnp.float32), 'Wo_w': jax.random.normal(ks[6], (NDIMS, NDIMS), jnp.float32) * sc, 'Wo_b': jnp.zeros((NDIMS,), jnp.float32), 'pos_emb': jax.random.normal(ks[7], (PER_HEAD, NPOS), jnp.float32) * 0.02, 'nheads': NHEADS}
        return inp
    _L0_xattn_all = _L0_xattn_setup()
    _L0_xattn_in = {k: v for k, v in _L0_xattn_all.items() if k in ('Wq_w', 'Wq_b', 'Wk_w', 'Wk_b', 'Wv_w', 'Wv_b', 'Wo_w', 'Wo_b', 'pos_emb')}
    del _L0_xattn_all

    def _L0_ffn_setup():
        import jax, jax.numpy as jnp
        import numpy as np
        E = 8
        TOP_K = 2
        ROUTE_SCALE = 1.0
        ALPHA = 1.702
        LIMIT = 7.0
        D = 256
        F = 256
        B, S = (2, 256)

        def swiglu(h):
            g = jnp.minimum(h[..., ::2], LIMIT)
            l = jnp.clip(h[..., 1::2], -LIMIT, LIMIT)
            return g * jax.nn.sigmoid(ALPHA * g) * (l + 1.0)
        if __name__ == '__main__':
            out = reference(**setup_inputs())
            print(out.shape, out.dtype)
        key = jax.random.key(seed)
        ks = jax.random.split(key, 16)
        sd = 1.0 / np.sqrt(D)
        sf = 1.0 / np.sqrt(F)
        return {'x': jax.random.normal(ks[0], (B, S, D), jnp.float32), 'gate_w': jax.random.normal(ks[1], (E, D), jnp.float32) * sd, 'gate_b': jax.random.normal(ks[2], (E,), jnp.float32) * 0.01, 'w1': jax.random.normal(ks[3], (E, 2 * F, D), jnp.float32) * sd, 'b1': jax.random.normal(ks[4], (E, 2 * F), jnp.float32) * 0.01, 'w3': jax.random.normal(ks[5], (E, 2 * F, D), jnp.float32) * sd, 'b3': jax.random.normal(ks[6], (E, 2 * F), jnp.float32) * 0.01, 'w2': jax.random.normal(ks[7], (E, D, F), jnp.float32) * sf, 'b2': jax.random.normal(ks[8], (E, D), jnp.float32) * 0.01, 'sw1': jax.random.normal(ks[9], (2 * F, D), jnp.float32) * sd, 'sb1': jax.random.normal(ks[10], (2 * F,), jnp.float32) * 0.01, 'sw3': jax.random.normal(ks[11], (2 * F, D), jnp.float32) * sd, 'sb3': jax.random.normal(ks[12], (2 * F,), jnp.float32) * 0.01, 'sw2': jax.random.normal(ks[13], (D, F), jnp.float32) * sf, 'sb2': jax.random.normal(ks[14], (D,), jnp.float32) * 0.01}
    _L0_ffn_all = _L0_ffn_setup()
    _L0_ffn_in = {k: v for k, v in _L0_ffn_all.items() if k in ('gate_w', 'gate_b', 'w1', 'b1', 'w3', 'b3', 'w2', 'b2', 'sw1', 'sb1', 'sw3', 'sb3', 'sw2', 'sb2')}
    del _L0_ffn_all

    def _L1_xattn_setup():
        import jax, jax.numpy as jnp
        import numpy as np
        EMBED_DIM = 256
        NUM_HEADS = 16
        HEAD_DIM = EMBED_DIM // NUM_HEADS
        SCALE = HEAD_DIM ** (-0.5)
        key = jax.random.key(seed)
        ks = jax.random.split(key, 8)
        B, Nq, Nkv, C = (2, 512, 512, EMBED_DIM)
        s = C ** (-0.5)
        return {'q': jax.random.normal(ks[0], (B, Nq, C), dtype=jnp.float32), 'kv': jax.random.normal(ks[1], (B, Nkv, C), dtype=jnp.float32), 'w_q': jax.random.normal(ks[2], (C, C), dtype=jnp.float32) * s, 'b_q': jnp.zeros((C,), dtype=jnp.float32), 'w_kv': jax.random.normal(ks[3], (C, 2 * C), dtype=jnp.float32) * s, 'b_kv': jnp.zeros((2 * C,), dtype=jnp.float32), 'w_out': jax.random.normal(ks[4], (C, C), dtype=jnp.float32) * s, 'b_out': jnp.zeros((C,), dtype=jnp.float32)}
    _L1_xattn_all = _L1_xattn_setup()
    _L1_xattn_in = {k: v for k, v in _L1_xattn_all.items() if k in ('w_q', 'b_q', 'w_kv', 'b_kv', 'w_out', 'b_out')}
    del _L1_xattn_all

    def _L1_ffn_setup():
        import jax, jax.numpy as jnp
        import numpy as np
        import math
        DIM = 256
        NUM_HEADS = 16
        SHARED_HEADS = 1
        ROUTED_HEADS = 3
        HEAD_DIM = DIM // NUM_HEADS
        B, N = (2, 512)
        key = jax.random.key(seed)
        ks = jax.random.split(key, 16)
        s = 1.0 / math.sqrt(DIM)
        inp = {'x': jax.random.normal(ks[0], (B, N, DIM), dtype=jnp.float32), 'Wq': jax.random.uniform(ks[1], (DIM, DIM), minval=-s, maxval=s), 'bq': jax.random.uniform(ks[2], (DIM,), minval=-s, maxval=s), 'Wk': jax.random.uniform(ks[3], (DIM, DIM), minval=-s, maxval=s), 'bk': jax.random.uniform(ks[4], (DIM,), minval=-s, maxval=s), 'Wv': jax.random.uniform(ks[5], (DIM, DIM), minval=-s, maxval=s), 'bv': jax.random.uniform(ks[6], (DIM,), minval=-s, maxval=s), 'Wp': jax.random.uniform(ks[7], (DIM, DIM), minval=-s, maxval=s), 'bp': jax.random.uniform(ks[8], (DIM,), minval=-s, maxval=s), 'Wr': jax.random.uniform(ks[9], (NUM_HEADS - SHARED_HEADS, DIM), minval=-s, maxval=s), 'br': jax.random.uniform(ks[10], (NUM_HEADS - SHARED_HEADS,), minval=-s, maxval=s), 'Ws': jax.random.uniform(ks[11], (2, DIM), minval=-s, maxval=s), 'bs': jax.random.uniform(ks[12], (2,), minval=-s, maxval=s), 'temperature': jnp.full((NUM_HEADS, 1, 1), float(np.log(np.expm1(1.0 / 0.24))), dtype=jnp.float32), 'query_embedding': 0.02 * jax.random.normal(ks[13], (NUM_HEADS, 1, HEAD_DIM), dtype=jnp.float32)}
        return inp
    _L1_ffn_all = _L1_ffn_setup()
    _L1_ffn_in = {k: v for k, v in _L1_ffn_all.items() if k in ('Wq', 'bq', 'Wk', 'bk', 'Wv', 'bv', 'Wp', 'bp', 'Wr', 'br', 'Ws', 'bs', 'temperature', 'query_embedding')}
    del _L1_ffn_all
    return {'x': x, 'ctx_1024': ctx_1024, 'g_xattn': g_xattn, 'g_ffn': g_ffn, 'L0_xattn_Wq_w': _L0_xattn_in['Wq_w'], 'L0_xattn_Wq_b': _L0_xattn_in['Wq_b'], 'L0_xattn_Wk_w': _L0_xattn_in['Wk_w'], 'L0_xattn_Wk_b': _L0_xattn_in['Wk_b'], 'L0_xattn_Wv_w': _L0_xattn_in['Wv_w'], 'L0_xattn_Wv_b': _L0_xattn_in['Wv_b'], 'L0_xattn_Wo_w': _L0_xattn_in['Wo_w'], 'L0_xattn_Wo_b': _L0_xattn_in['Wo_b'], 'L0_xattn_pos_emb': _L0_xattn_in['pos_emb'], 'L0_ffn_gate_w': _L0_ffn_in['gate_w'], 'L0_ffn_gate_b': _L0_ffn_in['gate_b'], 'L0_ffn_w1': _L0_ffn_in['w1'], 'L0_ffn_b1': _L0_ffn_in['b1'], 'L0_ffn_w3': _L0_ffn_in['w3'], 'L0_ffn_b3': _L0_ffn_in['b3'], 'L0_ffn_w2': _L0_ffn_in['w2'], 'L0_ffn_b2': _L0_ffn_in['b2'], 'L0_ffn_sw1': _L0_ffn_in['sw1'], 'L0_ffn_sb1': _L0_ffn_in['sb1'], 'L0_ffn_sw3': _L0_ffn_in['sw3'], 'L0_ffn_sb3': _L0_ffn_in['sb3'], 'L0_ffn_sw2': _L0_ffn_in['sw2'], 'L0_ffn_sb2': _L0_ffn_in['sb2'], 'L1_xattn_w_q': _L1_xattn_in['w_q'], 'L1_xattn_b_q': _L1_xattn_in['b_q'], 'L1_xattn_w_kv': _L1_xattn_in['w_kv'], 'L1_xattn_b_kv': _L1_xattn_in['b_kv'], 'L1_xattn_w_out': _L1_xattn_in['w_out'], 'L1_xattn_b_out': _L1_xattn_in['b_out'], 'L1_ffn_Wq': _L1_ffn_in['Wq'], 'L1_ffn_bq': _L1_ffn_in['bq'], 'L1_ffn_Wk': _L1_ffn_in['Wk'], 'L1_ffn_bk': _L1_ffn_in['bk'], 'L1_ffn_Wv': _L1_ffn_in['Wv'], 'L1_ffn_bv': _L1_ffn_in['bv'], 'L1_ffn_Wp': _L1_ffn_in['Wp'], 'L1_ffn_bp': _L1_ffn_in['bp'], 'L1_ffn_Wr': _L1_ffn_in['Wr'], 'L1_ffn_br': _L1_ffn_in['br'], 'L1_ffn_Ws': _L1_ffn_in['Ws'], 'L1_ffn_bs': _L1_ffn_in['bs'], 'L1_ffn_temperature': _L1_ffn_in['temperature'], 'L1_ffn_query_embedding': _L1_ffn_in['query_embedding']}

def reference(x, ctx_1024, g_xattn, g_ffn, L0_xattn_Wq_w, L0_xattn_Wq_b, L0_xattn_Wk_w, L0_xattn_Wk_b, L0_xattn_Wv_w, L0_xattn_Wv_b, L0_xattn_Wo_w, L0_xattn_Wo_b, L0_xattn_pos_emb, L0_ffn_gate_w, L0_ffn_gate_b, L0_ffn_w1, L0_ffn_b1, L0_ffn_w3, L0_ffn_b3, L0_ffn_w2, L0_ffn_b2, L0_ffn_sw1, L0_ffn_sb1, L0_ffn_sw3, L0_ffn_sb3, L0_ffn_sw2, L0_ffn_sb2, L1_xattn_w_q, L1_xattn_b_q, L1_xattn_w_kv, L1_xattn_b_kv, L1_xattn_w_out, L1_xattn_b_out, L1_ffn_Wq, L1_ffn_bq, L1_ffn_Wk, L1_ffn_bk, L1_ffn_Wv, L1_ffn_bv, L1_ffn_Wp, L1_ffn_bp, L1_ffn_Wr, L1_ffn_br, L1_ffn_Ws, L1_ffn_bs, L1_ffn_temperature, L1_ffn_query_embedding):
    import jax
    import jax.numpy as jnp

    def _L0_xattn_ref(q, k, v, Wq_w, Wq_b, Wk_w, Wk_b, Wv_w, Wv_b, Wo_w, Wo_b, pos_emb, nheads):
        import jax, jax.numpy as jnp
        import numpy as np
        B, S, NDIMS, NHEADS, NPOS = (1, 512, 256, 16, 64)
        PER_HEAD = NDIMS // NHEADS

        def cope(query, attn_logits, pos_emb):
            npos_max = pos_emb.shape[-1]
            gates = jax.nn.sigmoid(attn_logits)
            pos = jnp.flip(jnp.cumsum(jnp.flip(gates, axis=-1), axis=-1), axis=-1)
            pos = jnp.minimum(pos, npos_max - 1)
            pos_ceil = jnp.ceil(pos).astype(jnp.int32)
            pos_floor = jnp.floor(pos).astype(jnp.int32)
            logits_int = jnp.einsum('bhqd,dn->bhqn', query, pos_emb)
            logits_ceil = jnp.take_along_axis(logits_int, pos_ceil, axis=-1)
            logits_floor = jnp.take_along_axis(logits_int, pos_floor, axis=-1)
            w = pos - pos_floor
            return logits_ceil * w + logits_floor * (1.0 - w)
        b, s, ndims = q.shape
        d = ndims // nheads

        def heads(x, W, bb):
            y = x @ W.T + bb
            return y.reshape(b, s, nheads, d).transpose(0, 2, 1, 3)
        Q = heads(q, Wq_w, Wq_b)
        K = heads(k, Wk_w, Wk_b)
        V = heads(v, Wv_w, Wv_b)
        logits = jnp.einsum('bhqd,bhkd->bhqk', Q, K) / jnp.sqrt(jnp.asarray(d, Q.dtype))
        scores = jax.nn.softmax(logits + cope(Q, logits, pos_emb), axis=-1)
        out = jnp.einsum('bhqk,bhkd->bhqd', scores, V)
        out = out.transpose(0, 2, 1, 3).reshape(b, s, ndims)
        return out @ Wo_w.T + Wo_b

    def _L0_ffn_ref(x, gate_w, gate_b, w1, b1, w3, b3, w2, b2, sw1, sb1, sw3, sb3, sw2, sb2):
        import jax, jax.numpy as jnp
        import numpy as np
        E = 8
        TOP_K = 2
        ROUTE_SCALE = 1.0
        ALPHA = 1.702
        LIMIT = 7.0
        D = 256
        F = 256
        B, S = (2, 256)

        def swiglu(h):
            g = jnp.minimum(h[..., ::2], LIMIT)
            l = jnp.clip(h[..., 1::2], -LIMIT, LIMIT)
            return g * jax.nn.sigmoid(ALPHA * g) * (l + 1.0)
        if __name__ == '__main__':
            out = reference(**setup_inputs())
            print(out.shape, out.dtype)
        inp_shape = x.shape
        xt = x.reshape(-1, D)
        logits = xt @ gate_w.T
        scores = jax.nn.softmax(logits.astype(jnp.float32), axis=-1)
        biased = scores + gate_b.astype(jnp.float32)
        idx = jax.lax.top_k(biased, TOP_K)[1]
        weights = (jnp.take_along_axis(scores, idx, axis=-1) * ROUTE_SCALE).astype(x.dtype)
        cw = jnp.sum(jax.nn.one_hot(idx, E, dtype=x.dtype) * weights[..., None], axis=1)
        h1 = jnp.einsum('td,efd->etf', xt, w1) + b1[:, None, :]
        h3 = jnp.einsum('td,efd->etf', xt, w3) + b3[:, None, :]
        a = swiglu(h1 * h3)
        y = jnp.einsum('etf,edf->etd', a, w2) + b2[:, None, :]
        routed = jnp.einsum('te,etd->td', cw, y)
        sh = swiglu((xt @ sw1.T + sb1) * (xt @ sw3.T + sb3))
        shared = sh @ sw2.T + sb2
        return (routed + shared).reshape(inp_shape)

    def _L1_xattn_ref(q, kv, w_q, b_q, w_kv, b_kv, w_out, b_out):
        import jax, jax.numpy as jnp
        import numpy as np
        EMBED_DIM = 256
        NUM_HEADS = 16
        HEAD_DIM = EMBED_DIM // NUM_HEADS
        SCALE = HEAD_DIM ** (-0.5)
        B, Nq, C = q.shape
        _, Nkv, _ = kv.shape
        H, D = (NUM_HEADS, HEAD_DIM)
        qp = (q @ w_q + b_q).reshape(B, Nq, H, D).transpose(0, 2, 1, 3)
        kvp = (kv @ w_kv + b_kv).reshape(B, Nkv, 2, H, D).transpose(2, 0, 3, 1, 4)
        kp, vp = (kvp[0], kvp[1])
        attn = jnp.einsum('bhqd,bhkd->bhqk', qp, kp) * SCALE
        attn = jax.nn.softmax(attn, axis=-1)
        out = jnp.einsum('bhqk,bhkd->bhqd', attn, vp)
        out = out.transpose(0, 2, 1, 3).reshape(B, Nq, C)
        return out @ w_out + b_out

    def _L1_ffn_ref(x, Wq, bq, Wk, bk, Wv, bv, Wp, bp, Wr, br, Ws, bs, temperature, query_embedding):
        import jax, jax.numpy as jnp
        import numpy as np
        import math
        DIM = 256
        NUM_HEADS = 16
        SHARED_HEADS = 1
        ROUTED_HEADS = 3
        HEAD_DIM = DIM // NUM_HEADS
        B, N = (2, 512)
        Bsz, Nn, C = x.shape
        H, hd = (NUM_HEADS, HEAD_DIM)

        def heads(W, b):
            y = x @ W.T + b
            return y.reshape(Bsz, Nn, H, hd).transpose(0, 2, 1, 3)
        q = heads(Wq, bq)
        k = heads(Wk, bk)
        v = heads(Wv, bv)
        q_norm = q / jnp.linalg.norm(q, axis=-1, keepdims=True)
        q_scaled = (q_norm + query_embedding[None]) * jax.nn.softplus(temperature)[None]
        attn = jnp.einsum('bhqd,bhkd->bhqk', q_scaled, k) / math.sqrt(hd)
        attn = jax.nn.softmax(attn, axis=-1)
        h = jnp.einsum('bhqk,bhkd->bhqd', attn, v)
        h = h.transpose(0, 2, 1, 3).reshape(Bsz, Nn, C)
        gates = jax.nn.softmax(h @ Wr.T + br, axis=-1)
        _, idx = jax.lax.top_k(gates, ROUTED_HEADS)
        mask = jax.nn.one_hot(idx, H - SHARED_HEADS, dtype=gates.dtype).sum(axis=-2)
        routed_gates = gates * mask * ROUTED_HEADS
        sw = jax.nn.softmax(h @ Ws.T + bs, axis=-1)
        shared_gates = sw * SHARED_HEADS
        weight_0 = sw * 2.0
        shared_gates = weight_0[..., 0:1] * shared_gates
        routed_gates = weight_0[..., 1:2] * routed_gates
        masked_gates = jnp.concatenate([shared_gates, routed_gates], axis=-1)
        out = h * masked_gates.sum(axis=-1, keepdims=True)
        return out @ Wp.T + bp
    x = x + jnp.tanh(g_xattn[0]) * _L0_xattn_ref(_layernorm(x, axis=-1), ctx_1024, ctx_1024, L0_xattn_Wq_w, L0_xattn_Wq_b, L0_xattn_Wk_w, L0_xattn_Wk_b, L0_xattn_Wv_w, L0_xattn_Wv_b, L0_xattn_Wo_w, L0_xattn_Wo_b, L0_xattn_pos_emb, 16)
    x = x + jnp.tanh(g_ffn[0]) * _L0_ffn_ref(_layernorm(x, axis=-1), L0_ffn_gate_w, L0_ffn_gate_b, L0_ffn_w1, L0_ffn_b1, L0_ffn_w3, L0_ffn_b3, L0_ffn_w2, L0_ffn_b2, L0_ffn_sw1, L0_ffn_sb1, L0_ffn_sw3, L0_ffn_sb3, L0_ffn_sw2, L0_ffn_sb2)
    x = x + jnp.tanh(g_xattn[1]) * _L1_xattn_ref(_layernorm(x, axis=-1), ctx_1024, L1_xattn_w_q, L1_xattn_b_q, L1_xattn_w_kv, L1_xattn_b_kv, L1_xattn_w_out, L1_xattn_b_out)
    x = x + jnp.tanh(g_ffn[1]) * _L1_ffn_ref(_layernorm(x, axis=-1), L1_ffn_Wq, L1_ffn_bq, L1_ffn_Wk, L1_ffn_bk, L1_ffn_Wv, L1_ffn_bv, L1_ffn_Wp, L1_ffn_bp, L1_ffn_Wr, L1_ffn_br, L1_ffn_Ws, L1_ffn_bs, L1_ffn_temperature, L1_ffn_query_embedding)
    return x

_drawn_inputs = setup_inputs


def setup_inputs(seed=0):
    import zlib

    import numpy as np

    out = dict(_drawn_inputs(seed))
    spreads = {'g_ffn': (-1.0, 0.6),
     'L0_xattn_Wq_b': (0.0, 0.294),
     'L0_xattn_Wk_b': (0.0, 0.8),
     'L0_xattn_Wv_b': (0.0, 0.1),
     'L0_xattn_Wo_b': (0.0, 0.1),
     'L1_xattn_b_q': (0.0, 0.546),
     'L1_xattn_b_kv': (0.0, 0.1),
     'L1_xattn_b_out': (0.0, 0.1),
     'L1_ffn_temperature': (4.151041507720947, 0.6)}
    factors = {'L0_xattn_pos_emb': 6.482,
     'L0_ffn_b1': 8.0,
     'L0_ffn_b3': 8.0,
     'L0_ffn_b2': 8.0,
     'L0_ffn_sb1': 8.0,
     'L0_ffn_sb3': 8.0,
     'L0_ffn_sb2': 8.0,
     'L1_ffn_Wq': 3.536,
     'L1_ffn_bq': 8.0,
     'L1_ffn_Wk': 3.513,
     'L1_ffn_bk': 64.0,
     'L1_ffn_bv': 2.888,
     'L1_ffn_bp': 2.851,
     'L1_ffn_Wr': 8.0,
     'L1_ffn_br': 8.0,
     'L1_ffn_Ws': 8.0,
     'L1_ffn_bs': 41.162,
     'L1_ffn_query_embedding': 8.0}
    for name, (base, spread) in spreads.items():
        noise = np.random.default_rng([zlib.crc32(name.encode()), seed]).standard_normal(out[name].shape)
        drawn = base * np.exp(spread * noise) if base else spread * noise
        out[name] = jnp.asarray(drawn.astype(out[name].dtype))
    for name, factor in factors.items():
        out[name] = (out[name] * factor).astype(out[name].dtype)
    return out
```

```python
from contextlib import ExitStack

import concourse.bass as bass
from concourse import mybir

F32 = mybir.dt.float32
I16 = mybir.dt.int16
U32 = mybir.dt.uint32
ALU = mybir.AluOpType
ACT = mybir.ActivationFunctionType
AX = mybir.AxisListType

P = 128
D = 256
S = 256
B = 16
H = 16
HD = D // H
HP = 32
G4 = H // 4
NC = D // P
NT = S // P
E = 8
NE = E + 1
F = 256
NPOS = 64
EPS = 1e-5
ALPHA = 1.702
LIMIT = 7.0
ROUND = 12582912.0
TINY = 1e-30
RESET = -1e9
INV_SQRT_HD = HD ** -0.5
TOP = 3
NG = H + 1

SEMS = ["loads", "stores", "transposed", "evacuated", "dve_step", "act_step", "pool_step",
        "var_ready", "rstd_ready", "xn_ready", "xT_psum", "xT_ready", "ctxT_psum", "ctxT_ready",
        "proj_done", "k_ready", "v_ready", "q_ready", "q_padded", "q_psum",
        "scores_done", "table_done", "gates_ready", "z_ready", "exp_done", "pT_psum", "pT_ready",
        "pv_done", "o_ready", "oT_psum", "oT_ready", "y_done", "x_ready", "max_ready",
        "maxT_psum", "scoresT_done", "logits_done", "gate_exp", "cw_ready", "cwT_psum", "cwT_ready",
        "h_done", "h1_ready", "u_used", "g_ready", "tanh_ready", "a_ready", "acc_used", "consts"]


class Kernel:
    pass


class Attention:

    def __init__(self, wq, wk, wv, wo, bq, bk, bv, tbo):
        self.wq, self.wk, self.wv, self.wo = wq, wk, wv, wo
        self.bq, self.bk, self.bv, self.tbo = bq, bk, bv, tbo


def zero(nc, k):
    for name in SEMS:
        nc.gpsimd.sem_clear(k.sem[name])
    nc.all_engine_barrier()


def transpose_weights(nc, k, blocks, small_loads=()):
    sem = k.sem
    with nc.Block() as block:
        @block.sync
        def _(sp):
            for n, (src, _, _) in enumerate(blocks):
                sp.dma_start(k.stage[:, n, :], src).then_inc(sem["loads"], 16)

        @block.tensor
        def _(pe):
            for n in range(len(blocks)):
                if n == 0:
                    pe.wait_ge(sem["loads"], 16 * len(blocks))
                if n >= 8:
                    pe.wait_ge(sem["evacuated"], n - 7)
                for c in range(NC):
                    last = nc.tensor.transpose(k.bank[n % 8][:, c * P:(c + 1) * P],
                                               k.stage[:, n, c * P:(c + 1) * P], k.ident[:])
                last.then_inc(sem["transposed"], 1)

        @block.vector
        def _(dve):
            for n, (_, dst, view) in enumerate(blocks):
                dve.wait_ge(sem["transposed"], n + 1)
                src = k.bank[n % 8][:, 0:D].rearrange("p (c r) -> p c r", c=NC)
                if view == "parity":
                    src = src.rearrange("p c (j t) -> p c t j", t=2)
                if view == "heads":
                    src = src.rearrange("p c (h d) -> p c h d", d=HD)
                if view == "half":
                    nc.vector.tensor_scalar(dst, src, 0.5, None, ALU.mult).then_inc(sem["evacuated"], 1)
                else:
                    nc.vector.tensor_copy(dst, src).then_inc(sem["evacuated"], 1)
    zero(nc, k)


def layer_norm(nc, k, xT_bank):
    sem = k.sem

    def on_dve(dve, step):
        for t in range(NT):
            step(nc.vector.bn_stats(k.bn[:, t, :], k.x[:, t, :]))
            step(nc.vector.bn_aggr(k.mv[:, t, :], k.bn[:, t, :]))
        nc.vector.tensor_scalar(k.var[:, 0:NT], k.mv[:, :, 1], EPS, None, ALU.add)\
            .then_inc(sem["var_ready"], 1)
        dve.wait_ge(sem["rstd_ready"], 1)
        for t in range(NT):
            nc.vector.tensor_scalar(k.xn[:, t, :], k.x[:, t, :], k.mv[:, t, 0:1], k.rstd[:, t:t + 1],
                                    ALU.subtract, ALU.mult).then_inc(sem["xn_ready"], 1)

    def on_pool(pool):
        pool.wait_ge(sem["var_ready"], 1)
        nc.gpsimd.tensor_tensor(k.rstd[:, 0:NT], k.var[:, 0:NT], k.neghalf[:, 0:NT], ALU.pow)\
            .then_inc(sem["rstd_ready"], 1)

    def on_pe(pe):
        pe.wait_ge(sem["xn_ready"], NT)
        for c in range(NC):
            for t in range(NT):
                last = nc.tensor.transpose(k.bank[xT_bank][:, c * S + t * P:c * S + (t + 1) * P],
                                           k.xn[:, t, c * P:(c + 1) * P], k.ident[:])
        last.then_inc(sem["xT_psum"], 1)

    def on_act(act):
        act.wait_ge(sem["xT_psum"], 1)
        nc.scalar.activation(k.xT[:].rearrange("p c s -> p (c s)"), k.bank[xT_bank][:], ACT.Copy)\
            .then_inc(sem["xT_ready"], 1)

    return on_dve, on_pool, on_pe, on_act


def stepper(eng, sem):
    count = [0]

    def step(ins):
        count[0] += 1
        ins.then_inc(sem, 1)
        eng.wait_ge(sem, count[0])
    return step


def head_projection(nc, k, g, w, src, bank):
    for half in range(2):
        for c in range(NC):
            last = nc.tensor.matmul(bank[:, half * S:(half + 1) * S],
                                    w[:, c, (g + half) * P:(g + half + 1) * P], src[:, c, :],
                                    start=(c == 0), stop=(c == NC - 1))
    return last


def token_projection(nc, w, src, bank):
    for t in range(NT):
        for c in range(NC):
            last = nc.tensor.matmul(bank[:, t * D:(t + 1) * D], src[:, c, t * P:(t + 1) * P], w[:, c, :],
                                    start=(c == 0), stop=(c == NC - 1))
    return last


def attention_inputs(nc, k, kind, i):
    sem = k.sem
    w = k.att[kind]
    with nc.Block() as block:
        ln_dve, ln_pool, ln_pe, ln_act = layer_norm(nc, k, 0)
        kv_src = k.xT if kind == "gated" else k.ctxT

        if kind == "cope":
            @block.sync
            def _(sp):
                for t in range(NT):
                    sp.dma_start(k.x[:, t, :], k.x_rows(i, t)).then_inc(sem["loads"], 16)
                for t in range(NT):
                    sp.dma_start(k.ctx[:, t, :], k.ctx_rows(i, t)).then_inc(sem["loads"], 16)

        @block.gpsimd
        def _(pool):
            ln_pool(pool)
            if kind == "gated":
                pool.wait_ge(sem["var_ready"], 2)
                nc.gpsimd.tensor_tensor(k.rnorm[:], k.sumsq[:], k.neghalf[:], ALU.pow)\
                    .then_inc(sem["rstd_ready"], 1)

        @block.vector
        def _(dve):
            step = stepper(dve, sem["dve_step"])
            if kind == "cope":
                dve.wait_ge(sem["loads"], 16 * 2 * NT)
            ln_dve(dve, step)
            dve.wait_ge(sem["proj_done"], 3)
            nc.vector.tensor_tensor(k.v[:, :, :, 0:HD],
                                    k.bank[4][:].rearrange("p (t h d) -> p t h d", t=NT, h=H),
                                    w.bv[:].rearrange("p (h d) -> p h d", h=H).unsqueeze(1)
                                    .broadcast_to([P, NT, H, HD]), ALU.add).then_inc(sem["v_ready"], 1)
            if kind == "gated":
                dve.wait_ge(sem["proj_done"], 4)
                q = k.qn[:].rearrange("p t n -> p (t n)")
                step(nc.vector.tensor_tensor(k.qn[:], k.bank[5][:].rearrange("p (t n) -> p t n", t=NT),
                                             w.bq[:].unsqueeze(1).broadcast_to([P, NT, D]), ALU.add))
                step(nc.vector.tensor_tensor(k.qsq, q, q, ALU.mult))
                nc.vector.tensor_reduce(k.sumsq[:], k.qsq.rearrange("p (m d) -> p m d", d=HD),
                                        axis=AX.X, op=ALU.add).then_inc(sem["var_ready"], 1)
                dve.wait_ge(sem["rstd_ready"], 2)
                qh = k.qn[:].rearrange("p t (h d) -> p (t h) d", d=HD)
                step(nc.vector.tensor_tensor(qh, qh, k.rnorm[:].unsqueeze(2)
                                             .broadcast_to([P, NT * H, HD]), ALU.mult))
                step(nc.vector.tensor_tensor(k.qn[:], k.qn[:], k.qe_row[:].unsqueeze(1)
                                             .broadcast_to([P, NT, D]), ALU.add))
                nc.vector.tensor_tensor(
                    k.qpad[:, :, :, 0:HD], k.qn[:].rearrange("p t (h d) -> p t h d", d=HD),
                    k.temp_row[:].unsqueeze(2).unsqueeze(1).broadcast_to([P, NT, H, HD]),
                    ALU.mult).then_inc(sem["q_padded"], 1)

        @block.tensor
        def _(pe):
            if kind == "cope":
                pe.wait_ge(sem["loads"], 16 * 2 * NT)
                for c in range(NC):
                    for t in range(NT):
                        last = nc.tensor.transpose(k.bank[1][:, c * S + t * P:c * S + (t + 1) * P],
                                                   k.ctx[:, t, c * P:(c + 1) * P], k.ident[:])
                last.then_inc(sem["ctxT_psum"], 1)
            if kind == "gated":
                ln_pe(pe)
                pe.wait_ge(sem["xT_ready"], 1)
            elif kind == "cope":
                pe.wait_ge(sem["ctxT_ready"], 1)
            head_projection(nc, k, 0, w.wk, kv_src, k.bank[2]).then_inc(sem["proj_done"], 1)
            head_projection(nc, k, 2, w.wk, kv_src, k.bank[3]).then_inc(sem["proj_done"], 1)
            token_projection(nc, w.wv, kv_src, k.bank[4]).then_inc(sem["proj_done"], 1)
            if kind != "gated":
                ln_pe(pe)
                pe.wait_ge(sem["xT_ready"], 1)
                head_projection(nc, k, 0, w.wq, k.xT, k.bank[5]).then_inc(sem["proj_done"], 1)
                head_projection(nc, k, 2, w.wq, k.xT, k.bank[6]).then_inc(sem["proj_done"], 1)
            else:
                token_projection(nc, w.wq, k.xT, k.bank[5]).then_inc(sem["proj_done"], 1)
                pe.wait_ge(sem["q_padded"], 1)
                for g in range(G4):
                    for t in range(NT):
                        last = nc.tensor.transpose(
                            k.bank[6 + g // 2][:, (g % 2) * S + t * P:(g % 2) * S + (t + 1) * P],
                            k.qpad[:, t, 4 * g:4 * g + 4, :].rearrange("p h d -> p (h d)"), k.ident[:])
                last.then_inc(sem["q_psum"], 1)

        @block.scalar
        def _(act):
            if kind == "cope":
                act.wait_ge(sem["ctxT_psum"], 1)
                nc.scalar.activation(k.ctxT[:].rearrange("p c s -> p (c s)"), k.bank[1][:], ACT.Copy)\
                    .then_inc(sem["ctxT_ready"], 1)
            if kind == "gated":
                ln_act(act)
            for g in range(G4):
                act.wait_ge(sem["proj_done"], g // 2 + 1)
                nc.scalar.activation(k.kT[:, g, :], k.bank[2 + g // 2][:, (g % 2) * S:(g % 2 + 1) * S],
                                     ACT.Identity, bias=w.bk[:, g:g + 1]).then_inc(sem["k_ready"], 1)
            if kind != "gated":
                ln_act(act)
                for g in range(G4):
                    act.wait_ge(sem["proj_done"], 4 + g // 2)
                    nc.scalar.activation(k.qT[:, g, :], k.bank[5 + g // 2][:, (g % 2) * S:(g % 2 + 1) * S],
                                         ACT.Identity, bias=w.bq[:, g:g + 1]).then_inc(sem["q_ready"], 1)
            else:
                act.wait_ge(sem["q_psum"], 1)
                for n in range(2):
                    nc.scalar.activation(k.qT[:, 2 * n:2 * n + 2, :].rearrange("p g s -> p (g s)"),
                                         k.bank[6 + n][:], ACT.Copy).then_inc(sem["q_ready"], 1)
    zero(nc, k)


def head_rows(h):
    return slice(HP * (h % 4), HP * (h % 4 + 1))


def scores(nc, k, h, out):
    r, g = head_rows(h), h // 4
    for t in range(NT):
        last = nc.tensor.matmul(out[:, t * S:(t + 1) * S], k.qT[r, g, t * P:(t + 1) * P], k.kT[r, g, :],
                                start=True, stop=True)
    return last


def cope_attention(nc, k):
    sem = k.sem
    with nc.Block() as block:
        @block.tensor
        def _(pe):
            def transpose_probs(h):
                pe.wait_ge(sem["exp_done"], NT * (h + 1))
                if h >= 1:
                    pe.wait_ge(sem["pT_ready"], h)
                for c in range(NT):
                    for t in range(NT):
                        last = nc.tensor.transpose(k.bank[6][:, c * S + t * P:c * S + (t + 1) * P],
                                                   k.prob[:, h % 2, t, c * P:(c + 1) * P], k.ident[:])
                last.then_inc(sem["pT_psum"], 1)

            def weigh_values(h):
                pe.wait_ge(sem["pT_ready"], h + 1)
                for t in range(NT):
                    for c in range(NT):
                        last = nc.tensor.matmul(k.bank[7][:, t * D + h * HD:t * D + (h + 1) * HD],
                                                k.pT[:, h % 2, c, t * P:(t + 1) * P], k.v[:, c, h, 0:HD],
                                                start=(c == 0), stop=(c == NT - 1))
                last.then_inc(sem["pv_done"], 1)

            for h in range(H + 2):
                if h < H:
                    if h >= 2:
                        pe.wait_ge(sem["z_ready"], h - 1)
                    scores(nc, k, h, k.bank[h % 2]).then_inc(sem["scores_done"], 1)
                    for t in range(NT):
                        last = nc.tensor.matmul(k.bank[2 + 2 * (h % 2) + t][:],
                                                k.qT[head_rows(h), h // 4, t * P:(t + 1) * P],
                                                k.table[head_rows(h), :], start=True, stop=True)
                    last.then_inc(sem["table_done"], 1)
                if h >= 1 and h - 1 < H:
                    transpose_probs(h - 1)
                if h >= 2:
                    weigh_values(h - 2)
            pe.wait_ge(sem["o_ready"], 1)
            for c in range(NC):
                for t in range(NT):
                    last = nc.tensor.transpose(k.bank[0][:, c * S + t * P:c * S + (t + 1) * P],
                                               k.o[:, t, c * P:(c + 1) * P], k.ident[:])
            last.then_inc(sem["oT_psum"], 1)
            pe.wait_ge(sem["oT_ready"], 1)
            token_projection(nc, k.att["cope"].wo, k.oT, k.bank[1]).then_inc(sem["y_done"], 1)

        @block.scalar
        def _(act):
            step = stepper(act, sem["act_step"])

            def gates(h):
                act.wait_ge(sem["scores_done"], h + 1)
                if h >= 1:
                    act.wait_ge(sem["gates_ready"], h)
                step(nc.scalar.activation(k.th[:], k.bank[h % 2][:], ACT.Tanh, scale=-0.5 * INV_SQRT_HD))
                nc.scalar.activation(k.gate[:, h % 2, :, 0:S], k.th[:].rearrange("p (t s) -> p t s", t=NT),
                                     ACT.Identity, scale=0.5, bias=k.half[:]).then_inc(sem["gates_ready"], 1)

            for h in range(H + 2):
                if h < H:
                    gates(h)
                if h >= 1 and h - 1 < H:
                    n = h - 1
                    act.wait_ge(sem["z_ready"], n + 1)
                    if n >= 2:
                        act.wait_ge(sem["pT_psum"], n - 1)
                    for t in range(NT):
                        nc.scalar.activation(k.prob[:, n % 2, t, :], k.z[:, n % 2, t, :], ACT.Exp,
                                             bias=k.negmax[:, n % 2, t:t + 1],
                                             accum_out=k.sums[:, t, n:n + 1]).then_inc(sem["exp_done"], 1)
                if h >= 1 and h - 1 < H:
                    n = h - 1
                    act.wait_ge(sem["pT_psum"], n + 1)
                    if n >= 2:
                        act.wait_ge(sem["pv_done"], n - 1)
                    nc.scalar.activation(k.pT[:, n % 2, :, :].rearrange("p c s -> p (c s)"), k.bank[6][:],
                                         ACT.Copy).then_inc(sem["pT_ready"], 1)
            act.wait_ge(sem["oT_psum"], 1)
            nc.scalar.activation(k.oT[:].rearrange("p c s -> p (c s)"), k.bank[0][:], ACT.Copy)\
                .then_inc(sem["oT_ready"], 1)

        @block.vector
        def _(dve):
            step = stepper(dve, sem["dve_step"])
            flat = "p t s -> p (t s)"
            for h in range(H):
                dve.wait_ge(sem["gates_ready"], h + 1)
                step(nc.vector.tensor_tensor_scan(
                    k.c[:].rearrange(flat)[:, ::-1], k.gate[:, h % 2].rearrange(flat)[:, ::-1],
                    k.cap[:].rearrange(flat)[:, ::-1], 0.0, ALU.add, ALU.max))
                c = k.c[:, :, 0:S]
                step(nc.vector.tensor_scalar(k.low[:], c, ROUND, ROUND + 1.0, ALU.add, ALU.subtract))
                step(nc.vector.tensor_tensor(k.diff[:], c, k.low[:], ALU.subtract))
                step(nc.vector.scalar_tensor_tensor(k.shift[:], k.diff[:], 1.0, k.low[:], ALU.is_gt, ALU.add))
                step(nc.vector.scalar_tensor_tensor(k.negw[:], k.diff[:], 1.0, k.diff[:], ALU.is_gt,
                                                    ALU.subtract))
                dve.wait_ge(sem["table_done"], h + 1)
                tab = k.banks[:, 2 + 2 * (h % 2):4 + 2 * (h % 2), :].rearrange("p t (a s) -> p t a s", a=2)
                for n, b in enumerate((32, 16, 8, 4, 2, 1)):
                    m = k.mask[:, n % 2]
                    step(nc.vector.tensor_scalar(m, k.shift[:], b, None, ALU.bitwise_and))
                    step(nc.vector.copy_predicated(
                        tab[:, :, :, 0:S - b], m[:, :, 0:S - b].unsqueeze(2).broadcast_to([P, NT, 2, S - b]),
                        tab[:, :, :, b:S]))
                step(nc.vector.tensor_tensor(k.bias[:], k.negw[:], tab[:, :, 1, :], ALU.mult))
                step(nc.vector.tensor_tensor(k.bias[:], k.bias[:], tab[:, :, 0, :], ALU.add))
                if h >= 2:
                    dve.wait_ge(sem["exp_done"], NT * (h - 1))
                step(nc.vector.scalar_tensor_tensor(
                    k.z[:, h % 2], k.bank[h % 2][:].rearrange("p (t s) -> p t s", t=NT), INV_SQRT_HD,
                    k.bias[:], ALU.mult, ALU.add))
                nc.vector.tensor_reduce(k.negmax[:, h % 2], k.z[:, h % 2], axis=AX.X, op=ALU.max,
                                        negate=True).then_inc(sem["z_ready"], 1)
            dve.wait_ge(sem["exp_done"], NT * H)
            step(nc.vector.reciprocal(k.rsum[:], k.sums[:]))
            dve.wait_ge(sem["pv_done"], H)
            nc.vector.tensor_tensor(k.o[:].rearrange("p t (h d) -> p t h d", d=HD),
                                    k.bank[7][:].rearrange("p (t h d) -> p t h d", t=NT, h=H),
                                    k.rsum[:].unsqueeze(3).broadcast_to([P, NT, H, HD]), ALU.mult)\
                .then_inc(sem["o_ready"], 1)
            dve.wait_ge(sem["y_done"], 1)
            add_to_x(nc, k, step, k.bank[1], k.tanh_g[:, 0:1], k.att["cope"].tbo)
    zero(nc, k)


def add_to_x(nc, k, step, bank, scale, bias_row):
    x = k.x[:].rearrange("p t n -> p (t n)")
    step(nc.vector.scalar_tensor_tensor(x, bank[:], scale, x, ALU.mult, ALU.add))
    step(nc.vector.tensor_tensor(k.x[:], k.x[:], bias_row[:].unsqueeze(1).broadcast_to([P, NT, D]),
                                 ALU.add))


def plain_attention(nc, k, kind, i):
    sem = k.sem
    w = k.att[kind]
    with nc.Block() as block:
        @block.tensor
        def _(pe):
            for h in range(H):
                if h >= 2:
                    pe.wait_ge(sem["max_ready"], h - 1)
                scores(nc, k, h, k.bank[h % 2]).then_inc(sem["scores_done"], 1)
            pe.wait_ge(sem["max_ready"], H)
            for g in range(G4):
                for t in range(NT):
                    last = nc.tensor.transpose(
                        k.bank[2 + g // 2][:, (g % 2) * S + t * P:(g % 2) * S + (t + 1) * P],
                        k.maxpad[:, t, 4 * g:4 * g + 4, :].rearrange("p h d -> p (h d)"), k.ident[:])
            last.then_inc(sem["maxT_psum"], 1)
            pe.wait_ge(sem["q_ready"], 1)

            def weigh_values(h):
                pe.wait_ge(sem["pT_ready"], h + 1)
                for t in range(NT):
                    for c in range(NT):
                        last = nc.tensor.matmul(k.bank[4 + t][:, h * (HD + 1):(h + 1) * (HD + 1)],
                                                k.pT[:, h % 2, c, t * P:(t + 1) * P], k.v[:, c, h, :],
                                                start=(c == 0), stop=(c == NT - 1))
                last.then_inc(sem["pv_done"], 1)

            for h in range(H):
                if h >= 2:
                    pe.wait_ge(sem["pT_ready"], h - 1)
                r, g = head_rows(h), h // 4
                for c in range(NT):
                    last = nc.tensor.matmul(k.bank[h % 2][:, c * S:(c + 1) * S],
                                            k.kT[r, g, c * P:(c + 1) * P], k.qT[r, g, :],
                                            start=True, stop=True)
                last.then_inc(sem["scoresT_done"], 1)
                if h >= 1:
                    weigh_values(h - 1)
            weigh_values(H - 1)
            pe.wait_ge(sem["o_ready"], NT)
            for c in range(NC):
                for t in range(NT):
                    last = nc.tensor.transpose(k.bank[0][:, c * S + t * P:c * S + (t + 1) * P],
                                               k.o[:, t, c * P:(c + 1) * P], k.ident[:])
            last.then_inc(sem["oT_psum"], 1)
            pe.wait_ge(sem["oT_ready"], 1)
            if kind == "gated":
                for t in range(NT):
                    for c in range(NC):
                        last = nc.tensor.matmul(k.bank[6][:, t * NG:(t + 1) * NG],
                                                k.oT[:, c, t * P:(t + 1) * P], k.wrs[:, c, :],
                                                start=(c == 0), stop=(c == NC - 1))
                last.then_inc(sem["logits_done"], 1)
            token_projection(nc, w.wo, k.oT, k.bank[1]).then_inc(sem["y_done"], 1)

        @block.scalar
        def _(act):
            for h in range(H):
                act.wait_ge(sem["scoresT_done"], h + 1)
                if h >= 2:
                    act.wait_ge(sem["pv_done"], h - 1)
                nc.scalar.activation(k.pT[:, h % 2, :, :].rearrange("p c s -> p (c s)"), k.bank[h % 2][:],
                                     ACT.Exp, scale=INV_SQRT_HD).then_inc(sem["pT_ready"], 1)
            act.wait_ge(sem["oT_psum"], 1)
            nc.scalar.activation(k.oT[:].rearrange("p c s -> p (c s)"), k.bank[0][:], ACT.Copy)\
                .then_inc(sem["oT_ready"], 1)
            if kind == "gated":
                act.wait_ge(sem["cw_ready"], 1)
                nc.scalar.activation(k.gexp[:].rearrange("p t n -> p (t n)"),
                                     k.glog[:].rearrange("p t n -> p (t n)"), ACT.Exp)\
                    .then_inc(sem["gate_exp"], 1)

        @block.vector
        def _(dve):
            step = stepper(dve, sem["dve_step"])
            for h in range(H):
                dve.wait_ge(sem["scores_done"], h + 1)
                nc.vector.tensor_reduce(k.maxpad[:, :, h, HD], k.bank[h % 2][:].rearrange("p (t s) -> p t s", t=NT),
                                        axis=AX.X, op=ALU.max, negate=True).then_inc(sem["max_ready"], 1)
            dve.wait_ge(sem["maxT_psum"], 1)
            step(nc.vector.tensor_tensor(k.qT[:, 0:2, :].rearrange("p g s -> p (g s)"),
                                         k.qT[:, 0:2, :].rearrange("p g s -> p (g s)"), k.bank[2][:], ALU.add))
            nc.vector.tensor_tensor(k.qT[:, 2:4, :].rearrange("p g s -> p (g s)"),
                                    k.qT[:, 2:4, :].rearrange("p g s -> p (g s)"), k.bank[3][:], ALU.add)\
                .then_inc(sem["q_ready"], 1)
            dve.wait_ge(sem["pv_done"], H)
            for t in range(NT):
                ov = k.bank[4 + t][:, 0:H * (HD + 1)].rearrange("p (h d) -> p h d", h=H)
                step(nc.vector.reciprocal(k.rsum[:, t, :], ov[:, :, HD]))
                nc.vector.tensor_tensor(k.o[:, t, :].rearrange("p (h d) -> p h d", d=HD), ov[:, :, 0:HD],
                                        k.rsum[:, t, :].unsqueeze(2).broadcast_to([P, H, HD]), ALU.mult)\
                    .then_inc(sem["o_ready"], 1)
            scale = k.tanh_g[:, 1:2]
            if kind == "gated":
                dve.wait_ge(sem["logits_done"], 1)
                step(nc.vector.tensor_tensor(k.glog[:], k.bank[6][:, 0:NT * NG].rearrange("p (t n) -> p t n", t=NT),
                                             k.brs_row[:].unsqueeze(1).broadcast_to([P, NT, NG]), ALU.add))
                parts = ((0, H - 1), (H - 1, NG))
                for n, (a, b) in enumerate(parts):
                    step(nc.vector.tensor_reduce(k.gmax[:, n, :], k.glog[:, :, a:b], axis=AX.X, op=ALU.max))
                for n, (a, b) in enumerate(parts):
                    last = nc.vector.tensor_tensor(k.glog[:, :, a:b], k.glog[:, :, a:b],
                                                   k.gmax[:, n, :].unsqueeze(2).broadcast_to([P, NT, b - a]),
                                                   ALU.subtract)
                    if n == 0:
                        step(last)
                last.then_inc(sem["cw_ready"], 1)
                dve.wait_ge(sem["gate_exp"], 1)
                for n, (a, b) in enumerate(parts):
                    step(nc.vector.tensor_reduce(k.gsum[:, n, :], k.gexp[:, :, a:b], axis=AX.X, op=ALU.add))
                step(nc.vector.reciprocal(k.gsum[:], k.gsum[:]))
                for n, (a, b) in enumerate(parts):
                    step(nc.vector.tensor_tensor(k.gexp[:, :, a:b], k.gexp[:, :, a:b],
                                                 k.gsum[:, n, :].unsqueeze(2).broadcast_to([P, NT, b - a]),
                                                 ALU.mult))
                for t in range(NT):
                    step(nc.vector.max(k.top8[:, t, :], k.gexp[:, t, 0:H - 1]))
                step(nc.vector.tensor_reduce(k.gscale[:, 0, :], k.top8[:, :, 0:TOP], axis=AX.X, op=ALU.add))
                step(nc.vector.tensor_reduce(k.gscale[:, 1, :], k.gexp[:, :, H - 1:NG], axis=AX.X, op=ALU.add))
                step(nc.vector.scalar_tensor_tensor(k.gscale[:, 0, :], k.gscale[:, 0, :], 2.0 * TOP,
                                                    k.gexp[:, :, NG - 1], ALU.mult, ALU.mult))
                step(nc.vector.scalar_tensor_tensor(k.gscale[:, 1, :], k.gscale[:, 1, :], 2.0,
                                                    k.gexp[:, :, NG - 2], ALU.mult, ALU.mult))
                step(nc.vector.tensor_tensor(k.gscale[:, 0, :], k.gscale[:, 0, :], k.gscale[:, 1, :], ALU.add))
                step(nc.vector.tensor_scalar(k.gscale[:, 0, :], k.gscale[:, 0, :], k.tanh_g[:, 3:4], None,
                                             ALU.mult))
                dve.wait_ge(sem["y_done"], 1)
                for t in range(NT):
                    step(nc.vector.scalar_tensor_tensor(k.x[:, t, :], k.bank[1][:, t * D:(t + 1) * D],
                                                        k.gscale[:, 0, t:t + 1], k.x[:, t, :],
                                                        ALU.mult, ALU.add))
                nc.vector.tensor_tensor(k.x[:], k.x[:], w.tbo[:].unsqueeze(1).broadcast_to([P, NT, D]),
                                        ALU.add).then_inc(sem["x_ready"], 1)
            else:
                dve.wait_ge(sem["y_done"], 1)
                add_to_x(nc, k, step, k.bank[1], scale, w.tbo)

        if kind == "gated":
            @block.sync
            def _(sp):
                sp.wait_ge(sem["x_ready"], 1)
                for t in range(NT):
                    sp.dma_start(k.out_rows(i, t), k.x[:, t, :]).then_inc(sem["stores"], 16)
                sp.wait_ge(sem["stores"], 16 * NT)
    zero(nc, k)


def experts(nc, k):
    sem = k.sem
    with nc.Block() as block:
        ln_dve, ln_pool, ln_pe, ln_act = layer_norm(nc, k, 6)

        @block.gpsimd
        def _(pool):
            ln_pool(pool)

        @block.tensor
        def _(pe):
            ln_pe(pe)
            pe.wait_ge(sem["xT_ready"], 1)
            for t in range(NT):
                for c in range(NC):
                    last = nc.tensor.matmul(k.bank[7][:, t * E:(t + 1) * E], k.xT[:, c, t * P:(t + 1) * P],
                                            k.wgate[:, c, :], start=(c == 0), stop=(c == NC - 1))
            last.then_inc(sem["logits_done"], 1)

            def up(n):
                e, par = divmod(n, 2)
                if n >= 2:
                    pe.wait_ge(sem["u_used"], 2 * (n - 1))
                for w, b in ((k.w1, 0), (k.w3, 1)):
                    for f in range(2):
                        for c in range(NC):
                            last = nc.tensor.matmul(k.bank[2 * (n % 2) + b][:, f * S:(f + 1) * S],
                                                    w[:, e, c, par, f * P:(f + 1) * P], k.xT[:, c, :],
                                                    start=(c == 0), stop=(c == NC - 1))
                last.then_inc(sem["h_done"], 1)

            def down(e):
                pe.wait_ge(sem["a_ready"], e + 1)
                if e >= 2:
                    pe.wait_ge(sem["acc_used"], 2 * (e - 1))
                for t in range(NT):
                    for f in range(2):
                        last = nc.tensor.matmul(k.bank[4 + e % 2][:, t * D:(t + 1) * D],
                                                k.a[:, e % 2, f, t * P:(t + 1) * P], k.w2[:, e, f, :],
                                                start=(f == 0), stop=(f == 1))
                last.then_inc(sem["y_done"], 1)

            up(0)
            up(1)
            pe.wait_ge(sem["cw_ready"], 1)
            for t in range(NT):
                last = nc.tensor.transpose(k.bank[6][0:NE, t * P:(t + 1) * P], k.cw[:, t, :], k.ident[:])
            last.then_inc(sem["cwT_psum"], 1)
            pe.wait_ge(sem["cwT_ready"], 1)
            for t in range(NT):
                last = nc.tensor.matmul(k.bank[7][:, t * D:(t + 1) * D], k.cwT[0:NE, t * P:(t + 1) * P],
                                        k.b2[0:NE, :], start=True, stop=True)
            last.then_inc(sem["cwT_psum"], 1)
            for e in range(1, NE):
                up(2 * e)
                down(e - 1)
                up(2 * e + 1)
            down(NE - 1)

        @block.scalar
        def _(act):
            ln_act(act)
            act.wait_ge(sem["max_ready"], 1)
            for t in range(NT):
                nc.scalar.activation(k.escore[:, t, :], k.bank[7][:, t * E:(t + 1) * E], ACT.Exp,
                                     bias=k.enegmax[:, t:t + 1], accum_out=k.esum[:, t:t + 1])\
                    .then_inc(sem["gate_exp"], 1)

            def first_linear(n):
                e, par = divmod(n, 2)
                act.wait_ge(sem["h_done"], n + 1)
                if n >= 2:
                    act.wait_ge(sem["u_used"], 2 * (n - 1))
                for f in range(2):
                    nc.scalar.activation(k.h1[:, n % 2, f, :], k.bank[2 * (n % 2)][:, f * S:(f + 1) * S],
                                         ACT.Identity, bias=k.b1[:, par, f, e:e + 1]).then_inc(sem["h1_ready"], 1)

            for e in range(NE):
                first_linear(2 * e)
                if e == 0:
                    act.wait_ge(sem["cwT_psum"], 1)
                    nc.scalar.activation(k.cwT[0:NE, :], k.bank[6][0:NE, 0:S], ACT.Copy)\
                        .then_inc(sem["cwT_ready"], 1)
                act.wait_ge(sem["g_ready"], e + 1)
                nc.scalar.activation(k.eth, k.eg, ACT.Tanh, scale=0.5 * ALPHA)\
                    .then_inc(sem["tanh_ready"], 1)
                first_linear(2 * e + 1)

        @block.vector
        def _(dve):
            step = stepper(dve, sem["dve_step"])
            ln_dve(dve, step)
            dve.wait_ge(sem["logits_done"], 1)
            logits = k.bank[7][:, 0:NT * E].rearrange("p (t e) -> p t e", t=NT)
            nc.vector.tensor_reduce(k.enegmax[:], logits, axis=AX.X, op=ALU.max, negate=True)\
                .then_inc(sem["max_ready"], 1)
            dve.wait_ge(sem["gate_exp"], NT)
            step(nc.vector.reciprocal(k.esum[:], k.esum[:]))
            step(nc.vector.tensor_tensor(k.escore[:], k.escore[:],
                                         k.esum[:].unsqueeze(2).broadcast_to([P, NT, E]), ALU.mult))
            step(nc.vector.tensor_tensor(k.ebiased[:], k.escore[:],
                                         k.gate_b[:].unsqueeze(1).broadcast_to([P, NT, E]), ALU.add))
            for t in range(NT):
                step(nc.vector.max(k.etop[:, t, :], k.ebiased[:, t, :]))
                step(nc.vector.max_index(k.eidx[:, t, :], k.etop[:, t, :], k.ebiased[:, t, :]))
                step(nc.vector.tensor_copy(k.eidxf[:, t, :], k.eidx[:, t, :]))
                step(nc.vector.tensor_scalar(k.ehot[:], k.expert_no[:], k.eidxf[:, t, 1:2], None, ALU.is_equal))
                step(nc.vector.scalar_tensor_tensor(k.ehot[:], k.expert_no[:], k.eidxf[:, t, 0:1], k.ehot[:],
                                                    ALU.is_equal, ALU.add))
                last = nc.vector.tensor_tensor(k.cw[:, t, 0:E], k.escore[:, t, :], k.ehot[:], ALU.mult)
                if t < NT - 1:
                    step(last)
            last.then_inc(sem["cw_ready"], 1)

            def hidden(n):
                e, par = divmod(n, 2)
                for f in range(2):
                    dve.wait_ge(sem["h1_ready"], 2 * n + f + 1)
                    nc.vector.scalar_tensor_tensor(k.u[:, par, f, :], k.bank[2 * (n % 2) + 1][:, f * S:(f + 1) * S],
                                                   k.b3[:, par, f, e:e + 1], k.h1[:, n % 2, f, :],
                                                   ALU.add, ALU.mult).then_inc(sem["u_used"], 1)
                dve.wait_ge(sem["u_used"], 2 * n + 2)

            def accumulate(e):
                dve.wait_ge(sem["y_done"], e + 1)
                for t in range(NT):
                    nc.vector.scalar_tensor_tensor(k.acc[:, t, :], k.bank[4 + e % 2][:, t * D:(t + 1) * D],
                                                   k.cw[:, t, e:e + 1], k.acc[:, t, :], ALU.mult, ALU.add)\
                        .then_inc(sem["acc_used"], 1)

            both = "p f s -> p (f s)"
            for e in range(NE):
                hidden(2 * e)
                if e >= 1:
                    dve.wait_ge(sem["a_ready"], e)
                nc.vector.tensor_scalar(k.eg, k.u[:, 0].rearrange(both), LIMIT, None, ALU.min)\
                    .then_inc(sem["g_ready"], 1)
                if e == 0:
                    dve.wait_ge(sem["cwT_psum"], 2)
                    step(nc.vector.tensor_copy(k.acc[:].rearrange("p t n -> p (t n)"), k.bank[7][:]))
                hidden(2 * e + 1)
                step(nc.vector.tensor_scalar(k.el, k.u[:, 1].rearrange(both), -LIMIT, LIMIT, ALU.max, ALU.min))
                dve.wait_ge(sem["tanh_ready"], e + 1)
                step(nc.vector.scalar_tensor_tensor(k.eg, k.eth, 1.0, k.eg, ALU.add, ALU.mult))
                if e >= 2:
                    dve.wait_ge(sem["y_done"], e - 1)
                nc.vector.scalar_tensor_tensor(k.a[:, e % 2].rearrange(both), k.el, 1.0, k.eg,
                                               ALU.add, ALU.mult).then_inc(sem["a_ready"], 1)
                if e >= 1:
                    accumulate(e - 1)
                    dve.wait_ge(sem["acc_used"], 2 * e)
            accumulate(NE - 1)
            dve.wait_ge(sem["acc_used"], 2 * NE)
            x = k.x[:].rearrange("p t n -> p (t n)")
            step(nc.vector.scalar_tensor_tensor(x, k.acc[:].rearrange("p t n -> p (t n)"), k.tanh_g[:, 2:3], x,
                                                ALU.mult, ALU.add))
    zero(nc, k)


def build(nc, x, ctx_in, g_xattn, g_ffn, Wq0, bq0, Wk0, bk0, Wv0, bv0, Wo0, bo0, pos_emb,
          gate_w, gate_b, w1, b1, w3, b3, w2, b2, sw1, sb1, sw3, sb3, sw2, sb2,
          wq1, bq1, wkv1, bkv1, wo1, bo1, Wq2, bq2, Wk2, bk2, Wv2, bv2, Wp2, bp2, Wr, br, Ws, bs,
          temperature, query_emb, out):
    with ExitStack() as ctx:
        k = Kernel()
        k.stack = ctx

        def sb(name, shape, dt=F32):
            return k.stack.enter_context(nc.sbuf_tensor(name, shape, dt))

        k.sem = {name: ctx.enter_context(nc.semaphore(name)) for name in SEMS}
        k.banks = ctx.enter_context(nc.psum_tensor("banks", [P, 8, 512], F32))
        k.bank = [k.banks[:, n, :] for n in range(8)]

        k.wq_cope = sb("wq_cope", [P, NC, H * HP])
        k.wk_cope = sb("wk_cope", [P, NC, H * HP])
        k.wq_cross = sb("wq_cross", [P, NC, H * HP])
        k.wk_cross = sb("wk_cross", [P, NC, H * HP])
        k.wk_gated = sb("wk_gated", [P, NC, H * HP])
        k.wv_cope = sb("wv_cope", [P, NC, D])
        k.wo_cope = sb("wo_cope", [P, NC, D])
        k.wv_cross = sb("wv_cross", [P, NC, D])
        k.wo_cross = sb("wo_cross", [P, NC, D])
        k.wq_gated = sb("wq_gated", [P, NC, D])
        k.wv_gated = sb("wv_gated", [P, NC, D])
        k.wo_gated = sb("wo_gated", [P, NC, D])
        k.w1 = sb("w1", [P, NE, NC, 2, F])
        k.w3 = sb("w3", [P, NE, NC, 2, F])
        k.w2 = sb("w2", [P, NE, 2, D])
        k.b1 = sb("b1", [P, 2, 2, NE])
        k.b3 = sb("b3", [P, 2, 2, NE])
        k.b2 = sb("b2", [NE, D])
        k.wgate = sb("wgate", [P, NC, E])
        k.wrs = sb("wrs", [P, NC, NG])
        k.table = sb("table", [P, 2 * S])
        k.bq_cope = sb("bq_cope", [P, G4])
        k.bk_cope = sb("bk_cope", [P, G4])
        k.bq_cross = sb("bq_cross", [P, G4])
        k.bk_cross = sb("bk_cross", [P, G4])
        k.bk_gated = sb("bk_gated", [P, G4])
        k.bv_cope = sb("bv_cope", [P, D])
        k.bo_cope = sb("bo_cope", [P, D])
        k.bv_cross = sb("bv_cross", [P, D])
        k.bo_cross = sb("bo_cross", [P, D])
        k.bq_gated = sb("bq_gated", [P, D])
        k.bv_gated = sb("bv_gated", [P, D])
        k.bo_gated = sb("bo_gated", [P, D])
        k.qe_row = sb("qe_row", [P, D])
        k.temp_row = sb("temp_row", [P, H])
        k.gate_b = sb("gate_b", [P, E])
        k.brs_row = sb("brs_row", [P, NG])
        k.g_raw = sb("g_raw", [P, 4])
        k.tanh_g = sb("tanh_g", [P, 4])
        k.ident = sb("ident", [P, P])
        k.neghalf = sb("neghalf", [P, NT * H])
        k.half = sb("half", [P, 1])
        k.cap = sb("cap", [P, NT, S + 1])
        k.expert_no = sb("expert_no", [P, E])
        k.v = sb("v", [P, NT, H, HD + 1])
        k.qpad = sb("qpad", [P, NT, H, HP])
        k.maxpad = sb("maxpad", [P, NT, H, HP])
        k.gate = sb("gate", [P, 2, NT, S + 1])
        k.c = sb("c", [P, NT, S + 1])
        k.cw = sb("cw", [P, NT, NE])
        preamble = ctx.enter_context(ExitStack())
        k.stack = preamble
        k.temp_tmp = sb("temp_tmp", [P, 3, H])
        k.stage = sb("stage", [P, 10, D])
        k.bias_rows = sb("bias_rows", [NE, 2, 2 * F])
        k.bias_pad = sb("bias_pad", [1, 5, H, HP])
        k.bias_flat = sb("bias_flat", [1, 5, D])
        k.small_rows = sb("small_rows", [32, D])
        k.emb = sb("emb", [P, NPOS + 1])
        k.emb_step = sb("emb_step", [P, NPOS])

        k.att = {
            "cope": Attention(wq=k.wq_cope, wk=k.wk_cope, wv=k.wv_cope, wo=k.wo_cope, bq=k.bq_cope,
                                    bk=k.bk_cope, bv=k.bv_cope, tbo=k.bo_cope),
            "cross": Attention(wq=k.wq_cross, wk=k.wk_cross, wv=k.wv_cross, wo=k.wo_cross,
                                     bq=k.bq_cross, bk=k.bk_cross, bv=k.bv_cross, tbo=k.bo_cross),
            "gated": Attention(wq=k.wq_gated, wk=k.wk_gated, wv=k.wv_gated, wo=k.wo_gated,
                                     bq=k.bq_gated, bk=k.bk_gated, bv=k.bv_gated, tbo=k.bo_gated),
        }
        k.x_rows = lambda i, t: x[bass.ds(i, 1), t * P:(t + 1) * P, :].rearrange("a p n -> p (a n)")
        k.ctx_rows = lambda i, t: ctx_in[bass.ds(i, 1), t * P:(t + 1) * P, :].rearrange("a p n -> p (a n)")
        k.out_rows = lambda i, t: out[bass.ds(i, 1), t * P:(t + 1) * P, :].rearrange("a p n -> p (a n)")
        sem = k.sem

        padded = (k.wq_cope, k.wk_cope, k.wq_cross, k.wk_cross, k.wk_gated)
        with nc.Block() as block:
            @block.gpsimd
            def _(pool):
                nc.gpsimd.memset(k.ident[:], 0.0).then_inc(sem["consts"], 1)
                pool.wait_ge(sem["consts"], 1)
                nc.gpsimd.affine_select(out=k.ident[:], in_=k.ident[:], compare_op=ALU.not_equal, fill=1.0,
                                        base=0, pattern=[[-1, P]], channel_multiplier=1)\
                    .then_inc(sem["consts"], 1)
                nc.gpsimd.iota(k.c[:], pattern=[[0, NT], [-1, S + 1]], base=S - NPOS + 1, channel_multiplier=0,
                               allow_small_or_imprecise_dtypes=True).then_inc(sem["pool_step"], 1)
                nc.gpsimd.iota(k.expert_no[:], pattern=[[1, E]], base=0, channel_multiplier=0,
                               allow_small_or_imprecise_dtypes=True).then_inc(sem["pool_step"], 1)

            @block.vector
            def _(dve):
                dve.wait_ge(sem["pool_step"], 1)
                nc.vector.tensor_scalar(k.cap[:], k.c[:], TINY, None, ALU.max).then_inc(sem["dve_step"], 1)
                dve.wait_ge(sem["dve_step"], 1)
                nc.vector.memset(k.cap[:, :, S:S + 1], TINY)
                nc.vector.memset(k.gate[:, :, :, S:S + 1], RESET)
                nc.vector.memset(k.neghalf[:], -0.5)
                nc.vector.memset(k.half[:], 0.5)
                for w in padded:
                    nc.vector.memset(w[:], 0.0)
                nc.vector.memset(k.qpad[:], 0.0)
                nc.vector.memset(k.maxpad[:], 0.0)
                nc.vector.memset(k.bias_pad[:], 0.0)
                nc.vector.memset(k.v[:, :, :, HD:HD + 1], 1.0)
                nc.vector.memset(k.cw[:, :, E:NE], 1.0)
                nc.vector.memset(k.emb[:], 0.0)
                nc.vector.memset(k.small_rows[:], 0.0)
        zero(nc, k)

        def expert_blocks(e, a1, a3, a2, at):
            blocks = []
            for dst, src in ((k.w1, a1), (k.w3, a3)):
                for r in range(2 * F // P):
                    n = P // 2
                    blocks.append((src[r * P:(r + 1) * P, :],
                                   dst[:, at, :, :, r * n:(r + 1) * n].rearrange("p e c t j -> p (e c) t j"),
                                   "parity"))
            for r in range(D // P):
                blocks.append((a2[r * P:(r + 1) * P, :],
                               k.w2[:, at, :, r * P:(r + 1) * P].rearrange("p e f n -> p (e f) n"), "half"))
            return blocks

        flat = "e r n -> (e r) n"
        with nc.Fori(0, E) as e:
            transpose_weights(nc, k, expert_blocks(e, w1[bass.ds(e, 1)].rearrange(flat),
                                                   w3[bass.ds(e, 1)].rearrange(flat),
                                                   w2[bass.ds(e, 1)].rearrange(flat), bass.ds(e, 1)))
        transpose_weights(nc, k, expert_blocks(E, sw1, sw3, sw2, slice(E, NE)))

        def padded_block(dst, src, r):
            h = P // HD
            return (src[r * P:(r + 1) * P, :],
                    dst[:].rearrange("p c (h d) -> p c h d", d=HP)[:, :, r * h:(r + 1) * h, 0:HD], "heads")

        def plain_block(dst, src, r):
            return (src[r * P:(r + 1) * P, :], dst[:, :, r * P:(r + 1) * P], "plain")

        transpose_weights(nc, k, [padded_block(k.wq_cope, Wq0, r) for r in range(2)]
                          + [padded_block(k.wk_cope, Wk0, r) for r in range(2)]
                          + [plain_block(k.wv_cope, Wv0, r) for r in range(2)]
                          + [plain_block(k.wo_cope, Wo0, r) for r in range(2)])
        transpose_weights(nc, k, [padded_block(k.wk_gated, Wk2, r) for r in range(2)]
                          + [plain_block(k.wq_gated, Wq2, r) for r in range(2)]
                          + [plain_block(k.wv_gated, Wv2, r) for r in range(2)]
                          + [plain_block(k.wo_gated, Wp2, r) for r in range(2)])

        row = lambda a: a.rearrange("(o n) -> o n", o=1)
        with nc.Block() as block:
            rows = [(k.bv_cope, bv0), (k.bo_cope, bo0), (k.bo_cross, bo1), (k.bq_gated, bq2),
                    (k.bv_gated, bv2), (k.bo_gated, bp2), (k.gate_b, gate_b)]
            flats = [bq0, bk0, bq1, bkv1[0:D], bk2]

            @block.sync
            def _(sp):
                def load(dst, src):
                    sp.dma_start(dst, src).then_inc(sem["loads"], 16)
                for c in range(NC):
                    load(k.stage[:, c, :], wq1[c * P:(c + 1) * P, :])
                    load(k.stage[:, 2 + c, :], wkv1[c * P:(c + 1) * P, 0:D])
                    load(k.wv_cross[:, c, :], wkv1[c * P:(c + 1) * P, D:2 * D])
                    load(k.wo_cross[:, c, :], wo1[c * P:(c + 1) * P, :])
                load(k.bias_rows[0:E, 0, :], b1)
                load(k.bias_rows[E:NE, 0, :], row(sb1))
                load(k.bias_rows[0:E, 1, :], b3)
                load(k.bias_rows[E:NE, 1, :], row(sb3))
                load(k.b2[0:E, :], b2)
                load(k.b2[E:NE, :], row(sb2))
                for n, src in enumerate(flats):
                    load(k.bias_flat[0:1, n, :], row(src))
                load(k.small_rows[0:E, :], gate_w)
                load(k.small_rows[E:E + H - 1, :], Wr)
                load(k.small_rows[E + H - 1:E + NG, :], Ws)

            @block.scalar
            def _(act):
                def load(dst, src):
                    act.dma_start(dst, src).then_inc(sem["loads"], 16)
                for dst, src in rows:
                    load(dst[:], row(src).broadcast_to([P, src.shape[0]]))
                load(k.bv_cross[:], row(bkv1[D:2 * D]).broadcast_to([P, D]))
                load(k.qe_row[:], query_emb.rearrange("h o d -> o (h d)").broadcast_to([P, D]))
                load(k.temp_row[:], temperature.rearrange("h a b -> (a b) h").broadcast_to([P, H]))
                load(k.brs_row[:, 0:H - 1], row(br).broadcast_to([P, H - 1]))
                load(k.brs_row[:, H - 1:NG], row(bs).broadcast_to([P, 2]))
                load(k.g_raw[:, 0:2], row(g_xattn).broadcast_to([P, 2]))
                load(k.g_raw[:, 2:4], row(g_ffn).broadcast_to([P, 2]))
                for j in range(4):
                    load(k.emb[HP * j:HP * j + HD, 0:NPOS], pos_emb)
                step = stepper(act, sem["act_step"])
                act.wait_ge(sem["loads"], 16 * 40)
                step(nc.scalar.activation(k.tanh_g[:], k.g_raw[:], ACT.Tanh))
                act.wait_ge(sem["consts"], 1)
                step(nc.scalar.activation(k.temp_tmp[:, 1, :], k.temp_tmp[:, 0, :], ACT.Exp, scale=-1.0))
                step(nc.scalar.activation(k.temp_tmp[:, 2, :], k.temp_tmp[:, 1, :], ACT.Ln, bias=1.0))

            @block.vector
            def _(dve):
                step = stepper(dve, sem["dve_step"])
                dve.wait_ge(sem["loads"], 16 * 40)
                nc.vector.scalar_tensor_tensor(k.temp_tmp[:, 0, :], k.temp_row[:], -1.0, k.temp_row[:],
                                               ALU.mult, ALU.max)\
                    .then_inc(sem["consts"], 1)
                heads = "p c (h d) -> p c h d"
                for n, w in ((0, k.wq_cross), (2, k.wk_cross)):
                    step(nc.vector.tensor_copy(w[:].rearrange(heads, d=HP)[:, :, :, 0:HD],
                                               k.stage[:, n:n + 2, :].rearrange(heads, d=HD)))
                step(nc.vector.tensor_copy(k.bias_pad[:, :, :, 0:HD],
                                           k.bias_flat[:].rearrange("o n (h d) -> o n h d", d=HD)))
                for n in (1, 3, 4):
                    step(nc.vector.memset(k.bias_pad[:, n, :, HD:HD + 1], 1.0))
                step(nc.vector.tensor_copy(k.emb[:, NPOS:NPOS + 1], k.emb[:, NPOS - 1:NPOS]))
                step(nc.vector.tensor_tensor(k.emb_step[:], k.emb[:, 1:NPOS + 1], k.emb[:, 0:NPOS], ALU.subtract))
                rep = S // NPOS
                for n, src in enumerate((k.emb[:, 1:NPOS + 1], k.emb_step[:])):
                    step(nc.vector.tensor_copy(
                        k.table[:, n * S:(n + 1) * S].rearrange("p (r b) -> p r b", b=NPOS),
                        src[:, ::-1].unsqueeze(1).broadcast_to([P, rep, NPOS])))
                dve.wait_ge(sem["act_step"], 3)
                step(nc.vector.scalar_tensor_tensor(k.temp_row[:], k.temp_row[:], 0.0, k.temp_tmp[:, 2, :],
                                                    ALU.max, ALU.add))
                for n, b in ((0, k.bo_cope), (1, k.bo_cross), (3, k.bo_gated)):
                    step(nc.vector.tensor_scalar(b[:], b[:], k.tanh_g[:, n:n + 1], None, ALU.mult))
        zero(nc, k)
        with nc.Block() as block:
            @block.tensor
            def _(pe):
                for n in range(2):
                    for par in range(2):
                        for f in range(2):
                            at = (2 * n + par) * 2 + f
                            src = k.bias_rows[:, n, :].rearrange("e (f j t) -> e t f j", f=2, t=2)[:, par, f, :]
                            nc.tensor.transpose(k.bank[0][:, at * 16:at * 16 + NE], src, k.ident[0:NE, 0:NE])
                for n in range(5):
                    for g in range(G4):
                        src = k.bias_pad[0:1, n, 4 * g:4 * g + 4, :].rearrange("o h d -> o (h d)")
                        nc.tensor.transpose(k.bank[1][:, n * G4 + g:n * G4 + g + 1], src, k.ident[0:1, 0:1])
                for c in range(NC):
                    last = nc.tensor.transpose(k.bank[2][:, c * 32:(c + 1) * 32],
                                               k.small_rows[:, c * P:(c + 1) * P], k.ident[0:32, 0:32])
                last.then_inc(sem["transposed"], 1)

            @block.vector
            def _(dve):
                dve.wait_ge(sem["transposed"], 1)
                src = k.bank[0][:, 0:128].rearrange("p (m e) -> p m e", e=16)
                for n, dst in enumerate((k.b1, k.b3)):
                    nc.vector.tensor_copy(dst[:].rearrange("p t f e -> p (t f) e"), src[:, 4 * n:4 * n + 4, 0:NE])
                for n, dst in enumerate((k.bq_cope, k.bk_cope, k.bq_cross, k.bk_cross, k.bk_gated)):
                    nc.vector.tensor_copy(dst[:], k.bank[1][:, n * G4:(n + 1) * G4])
                src = k.bank[2][:, 0:64].rearrange("p (c n) -> p c n", c=NC)
                nc.vector.tensor_copy(k.wgate[:], src[:, :, 0:E])
                nc.vector.tensor_copy(k.wrs[:], src[:, :, E:E + NG])
        zero(nc, k)

        preamble.close()
        k.stack = ctx
        k.x = sb("x", [P, NT, D])
        k.ctx = sb("ctx", [P, NT, D])
        k.xn = sb("xn", [P, NT, D])
        k.bn = sb("bn", [P, NT, 6])
        k.mv = sb("mv", [P, NT, 2])
        k.var = sb("var", [P, NT])
        k.rstd = sb("rstd", [P, NT])
        k.xT = sb("xT", [P, NC, S])
        k.ctxT = sb("ctxT", [P, NC, S])
        k.qT = sb("qT", [P, G4, S])
        k.kT = sb("kT", [P, G4, S])
        k.sumsq = sb("sumsq", [P, NT * H])
        k.rnorm = sb("rnorm", [P, NT * H])
        k.th = sb("th", [P, NT * S])
        k.low = sb("low", [P, NT, S])
        k.diff = sb("diff", [P, NT, S])
        k.negw = sb("negw", [P, NT, S])
        k.shift = sb("shift", [P, NT, S], I16)
        k.mask = sb("mask", [P, 2, NT, S], I16)
        k.bias = sb("bias", [P, NT, S])
        k.z = sb("z", [P, 2, NT, S])
        k.negmax = sb("negmax", [P, 2, NT])
        k.prob = sb("prob", [P, 2, NT, S])
        k.sums = sb("sums", [P, NT, H])
        k.rsum = sb("rsum", [P, NT, H])
        k.pT = sb("pT", [P, 2, NT, S])
        k.o = sb("o", [P, NT, D])
        k.oT = sb("oT", [P, NC, S])
        k.glog = sb("glog", [P, NT, NG])
        k.gexp = sb("gexp", [P, NT, NG])
        k.gmax = sb("gmax", [P, 2, NT])
        k.gsum = sb("gsum", [P, 2, NT])
        k.gscale = sb("gscale", [P, 2, NT])
        k.top8 = sb("top8", [P, NT, 8])
        k.escore = sb("escore", [P, NT, E])
        k.ebiased = sb("ebiased", [P, NT, E])
        k.enegmax = sb("enegmax", [P, NT])
        k.esum = sb("esum", [P, NT])
        k.etop = sb("etop", [P, NT, 8])
        k.eidx = sb("eidx", [P, NT, 8], U32)
        k.eidxf = sb("eidxf", [P, NT, 8])
        k.ehot = sb("ehot", [P, E])
        k.cwT = sb("cwT", [NE, S])
        flat2 = "p t s -> p (t s)"
        k.h1, k.u, k.a, k.acc, k.qn = k.z, k.prob, k.pT, k.bias, k.low
        k.eg, k.el, k.eth = (b[:].rearrange(flat2) for b in (k.low, k.diff, k.negw))
        k.qsq = k.diff[:].rearrange(flat2)

        with nc.Fori(0, B) as i:
            attention_inputs(nc, k, "cope", i)
            cope_attention(nc, k)
            experts(nc, k)
            attention_inputs(nc, k, "cross", i)
            plain_attention(nc, k, "cross", i)
            attention_inputs(nc, k, "gated", i)
            plain_attention(nc, k, "gated", i)


_INS = ['x', 'ctx_1024', 'g_xattn', 'g_ffn', 'L0_xattn_Wq_w', 'L0_xattn_Wq_b', 'L0_xattn_Wk_w', 'L0_xattn_Wk_b',
        'L0_xattn_Wv_w', 'L0_xattn_Wv_b', 'L0_xattn_Wo_w', 'L0_xattn_Wo_b', 'L0_xattn_pos_emb', 'L0_ffn_gate_w',
        'L0_ffn_gate_b', 'L0_ffn_w1', 'L0_ffn_b1', 'L0_ffn_w3', 'L0_ffn_b3', 'L0_ffn_w2', 'L0_ffn_b2',
        'L0_ffn_sw1', 'L0_ffn_sb1', 'L0_ffn_sw3', 'L0_ffn_sb3', 'L0_ffn_sw2', 'L0_ffn_sb2', 'L1_xattn_w_q',
        'L1_xattn_b_q', 'L1_xattn_w_kv', 'L1_xattn_b_kv', 'L1_xattn_w_out', 'L1_xattn_b_out', 'L1_ffn_Wq',
        'L1_ffn_bq', 'L1_ffn_Wk', 'L1_ffn_bk', 'L1_ffn_Wv', 'L1_ffn_bv', 'L1_ffn_Wp', 'L1_ffn_bp', 'L1_ffn_Wr',
        'L1_ffn_br', 'L1_ffn_Ws', 'L1_ffn_bs', 'L1_ffn_temperature', 'L1_ffn_query_embedding']


def kernel(**inputs):
    import numpy as _np
    import concourse.bacc as _bacc
    from concourse import mybir as _mybir
    from concourse.bass_utils import run_bass_kernel_spmd as _run

    nc = _bacc.Bacc("TRN2", target_bir_lowering=False, num_devices=1)
    arrays, args = {}, []
    for name in _INS:
        a = _np.ascontiguousarray(inputs[name])
        arrays[f"in_{name}"] = a
        args.append(nc.dram_tensor(f"in_{name}", a.shape, _mybir.dt.from_np(a.dtype), kind="ExternalInput").ap())
    out = nc.dram_tensor("out_0", (B, S, D), F32, kind="ExternalOutput").ap()
    build(nc, *args, out)
    return _run(nc, [arrays], core_ids=[0]).results[0]["out_0"]
```

```python
from contextlib import ExitStack

import concourse.bass as bass
from concourse import mybir

F32 = mybir.dt.float32
BF16 = mybir.dt.bfloat16
I16 = mybir.dt.int16
U32 = mybir.dt.uint32
ALU = mybir.AluOpType
ACT = mybir.ActivationFunctionType
AX = mybir.AxisListType

P = 128
D = 256
S = 256
B = 16
H = 16
HD = D // H
HB = 2 * HD
HG = P // HD
NC = D // P
NT = S // P
E = 8
NE = E + 1
F = 256
NPOS = 64
EPS = 1e-5
ALPHA = 1.702
LIMIT = 7.0
ROUND = 12582912.0
TINY = 1e-30
RESET = -1e9
INV_SQRT_HD = HD ** -0.5
TOP = 3
NG = H + 1

ATT = ("qT_psum", "kv_src", "k_psum", "k_ready", "v_psum", "v_ready", "q_psum", "q_ready",
       "scores", "max_ready", "maxT_psum", "maxT_ready", "scoresT", "pT_ready", "pv_done",
       "o_ready", "oT_psum", "oT_ready", "y_done")
LN = ("loads", "var_ready", "rstd_ready", "xn_ready", "xT_psum", "xT_ready")
SEMS = (["loads", "stores", "transposed", "evacuated", "consts", "step", "pool_step", "dve_core", "dve_side"]
        + ["core_" + n for n in LN + (
            "ctxT_psum", "ctxT_ready", "k_psum", "k_ready", "v_psum", "v_ready", "q_psum", "q_ready",
            "offset_psum", "offset_ready", "scores", "scores_copied", "gates", "low", "diff", "shift", "shift_copied",
            "pool_shift", "table", "moved", "slope", "steps", "partial", "z_ready", "exp", "pT_psum",
            "pT_ready", "pv_done", "o_ready")]
        + ["tail_" + n for n in ("ctxT_psum", "ctxT_ready", "oT_psum", "oT_ready", "y_done")]
        + ["ffn_" + n for n in LN[1:] + (
            "logits", "max_ready", "exp", "cw_ready", "cwT_psum", "cwT_ready", "init", "h1_done",
            "h3_done", "h1_ready", "u_ready", "g_ready", "tanh", "a_ready", "y_done", "acc")]
        + ["cross_" + n for n in LN[1:] + ATT]
        + ["gated_" + n for n in LN[1:] + ATT + ("norm_ready", "rnorm_ready", "q_done", "logits", "glog", "gexp",
                                                 "x_ready")])
PIECES = 6


class Kernel:
    pass


class Norm:
    pass


class Attention:

    def __init__(self, wq, wk, wv, wo, bq, bk, bv, tbo):
        self.wq, self.wk, self.wv, self.wo = wq, wk, wv, wo
        self.bq, self.bk, self.bv, self.tbo = bq, bk, bv, tbo


def zero(nc, k):
    nc.gpsimd.sem_clear(range(k.sem[SEMS[0]].num, k.sem[SEMS[-1]].num + 1))
    nc.all_engine_barrier()


def stepper(eng, sem):
    count = [0]

    def step(ins):
        count[0] += 1
        ins.then_inc(sem, 1)
        eng.wait_ge(sem, count[0])
    return step


def transpose_weights(nc, k, blocks, small_loads=()):
    sem = k.sem
    with nc.Block() as block:
        @block.sync
        def _(sp):
            for n, (src, _, _) in enumerate(blocks):
                sp.dma_start(k.stage[:, n, :], src).then_inc(sem["loads"], 16)

        @block.tensor
        def _(pe):
            for n in range(len(blocks)):
                if n == 0:
                    pe.wait_ge(sem["loads"], 16 * len(blocks))
                if n >= 8:
                    pe.wait_ge(sem["evacuated"], n - 7)
                for c in range(NC):
                    last = nc.tensor.transpose(k.bank[n % 8][:, c * P:(c + 1) * P],
                                               k.stage[:, n, c * P:(c + 1) * P], k.ident[:])
                last.then_inc(sem["transposed"], 1)

        @block.vector
        def _(dve):
            for n, (_, dst, view) in enumerate(blocks):
                dve.wait_ge(sem["transposed"], n + 1)
                src = k.bank[n % 8][:, 0:D].rearrange("p (c r) -> p c r", c=NC)
                if view == "parity":
                    src = src.rearrange("p c (j t) -> p c t j", t=2)
                if view == "half":
                    nc.vector.tensor_scalar(dst, src, 0.5, None, ALU.mult).then_inc(sem["evacuated"], 1)
                else:
                    nc.vector.tensor_copy(dst, src).then_inc(sem["evacuated"], 1)
    zero(nc, k)



def norm_vector(nc, k, dve, step, n, p):
    sem = k.sem
    for t in range(NT):
        step(nc.vector.bn_stats(n.stats[:, t, :], n.x[:, t, :]))
        step(nc.vector.bn_aggr(n.mean_var[:, t, :], n.stats[:, t, :]))
    nc.vector.tensor_scalar(n.var[:], n.mean_var[:, :, 1], EPS, None, ALU.add).then_inc(sem[p + "var_ready"], 1)
    dve.wait_ge(sem[p + "rstd_ready"], 1)
    for t in range(NT):
        nc.vector.tensor_scalar(n.xn[:, t, :], n.x[:, t, :], n.mean_var[:, t, 0:1], n.rstd[:, t:t + 1],
                                ALU.subtract, ALU.mult).then_inc(sem[p + "xn_ready"], 1)


def norm_pool(nc, k, pool, n, p):
    pool.wait_ge(k.sem[p + "var_ready"], 1)
    nc.gpsimd.tensor_tensor(n.rstd[:], n.var[:], k.neghalf[:, 0:NT], ALU.pow)\
        .then_inc(k.sem[p + "rstd_ready"], 1)


def transpose_tokens(nc, k, bank, src):
    for c in range(NC):
        for t in range(NT):
            last = nc.tensor.transpose(bank[:, c * S + t * P:c * S + (t + 1) * P],
                                       src[:, t, c * P:(c + 1) * P], k.ident[:])
    return last


def whole(tile):
    return tile[:, :, :].rearrange("p a b -> p (a b)")


def feature_projection(nc, w, src, bank):
    for g in range(NC):
        for c in range(NC):
            last = nc.tensor.matmul(bank[:, g * S:(g + 1) * S], w[:, c, g * P:(g + 1) * P], src[:, c, :],
                                    start=(c == 0), stop=(c == NC - 1))
    return last


def token_projection(nc, w, src, bank):
    for t in range(NT):
        for c in range(NC):
            last = nc.tensor.matmul(bank[:, t * D:(t + 1) * D], src[:, c, t * P:(t + 1) * P], w[:, c, :],
                                    start=(c == 0), stop=(c == NC - 1))
    return last


def copy_keys(nc, k, bank, kT, bias, signal):
    for par in range(2):
        for g in range(NC):
            nc.scalar.activation(kT[:, par, g, :], bank[:, g * S:(g + 1) * S], ACT.Identity,
                                 bias=bias[:, par, g:g + 1], scale=k.parity[:, par:par + 1]).then_inc(signal, 1)


def copy_queries(nc, bank, qT, bias, signal):
    for g in range(NC):
        nc.scalar.activation(qT[:, g, :], bank[:, g * S:(g + 1) * S], ACT.Identity,
                             bias=bias[:, g:g + 1]).then_inc(signal, 1)


def block_of(h):
    b = h % HG // 2
    return h // HG, slice(HB * b, HB * (b + 1)), h % 2


def scores(nc, h, qT, kT, bank):
    g, r, par = block_of(h)
    for t in range(NT):
        last = nc.tensor.matmul(bank[:, t * S:(t + 1) * S], qT[r, g, t * P:(t + 1) * P], kT[r, par, g, :],
                                start=True, stop=True)
    return last



def core_tensor(nc, k, pe, side):
    sem = k.sem
    pe.wait_ge(sem["core_loads"], 16 * 2 * NT)
    transpose_tokens(nc, k, k.bank[0], k.core_ctx).then_inc(sem["core_ctxT_psum"], 1)
    pe.wait_ge(sem["core_ctxT_ready"], 1)
    feature_projection(nc, k.wk_cope, k.core_ctxT, k.bank[2]).then_inc(sem["core_k_psum"], 1)
    token_projection(nc, k.wv_cope, k.core_ctxT, k.bank[0]).then_inc(sem["core_v_psum"], 1)
    pe.wait_ge(sem["core_xn_ready"], NT)
    transpose_tokens(nc, k, k.bank[1], k.core_norm.xn).then_inc(sem["core_xT_psum"], 1)
    pe.wait_ge(sem["core_xT_ready"], 1)
    feature_projection(nc, k.wq_cope, k.core_norm.xT, k.bank[3]).then_inc(sem["core_q_psum"], 1)
    pe.wait_ge(sem["core_q_ready"], NC)
    for t in range(NT):
        for g in range(NC):
            last = nc.tensor.matmul(k.bank[1][:, t * H + g * HG:t * H + (g + 1) * HG],
                                    k.core_qT[:, g, t * P:(t + 1) * P], k.first[:], start=True, stop=True)
    last.then_inc(sem["core_offset_psum"], 1)

    def raw(h):
        if h == 0:
            pe.wait_ge(sem["core_k_ready"], 2 * NC)
            pe.wait_ge(sem["core_v_ready"], 1)
        else:
            pe.wait_ge(sem["core_scores_copied"], (NT + 1) * h)
        scores(nc, h, k.core_qT, k.core_kT, k.bank[0]).then_inc(sem["core_scores"], 1)

    def table(h):
        if h == 0:
            pe.wait_ge(sem["core_offset_ready"], 1)
        else:
            pe.wait_ge(sem["core_slope"], h)
        g, r, par = block_of(h)
        for t in range(NT):
            last = nc.tensor.matmul(k.bank[1][:, t * S:(t + 1) * S], k.core_qT[r, g, t * P:(t + 1) * P],
                                    k.table[r, par, :], start=True, stop=True)
        last.then_inc(sem["core_table"], 1)

    raw(0)
    table(0)
    raw(1)
    for s in range(H + 3):
        if s + 2 < H:
            raw(s + 2)
        for _ in range(PIECES // 2):
            next(side, None)
        h = s - 2
        if 0 <= h < H:
            pe.wait_ge(sem["core_exp"], NT * (h + 1))
            if h >= 1:
                pe.wait_ge(sem["core_pT_ready"], h)
            transpose_tokens(nc, k, k.bank[2], k.core_prob).then_inc(sem["core_pT_psum"], 1)
        for _ in range(PIECES - PIECES // 2):
            next(side, None)
        h = s - 3
        if 0 <= h < H:
            pe.wait_ge(sem["core_pT_ready"], h + 1)
            for t in range(NT):
                for c in range(NT):
                    last = nc.tensor.matmul(k.bank[3][:, t * D + h * HD:t * D + (h + 1) * HD],
                                            k.core_pT[:, h % 2, c, t * P:(t + 1) * P],
                                            k.core_v[:, c, h * HD:(h + 1) * HD],
                                            start=(c == 0), stop=(c == NT - 1))
            last.then_inc(sem["core_pv_done"], 1)
        if s + 1 < H:
            table(s + 1)


def core_scalar(nc, k, act, side):
    sem = k.sem
    act.wait_ge(sem["core_ctxT_psum"], 1)
    nc.scalar.activation(whole(k.core_ctxT), k.bank[0][:], ACT.Copy).then_inc(sem["core_ctxT_ready"], 1)
    act.wait_ge(sem["core_k_psum"], 1)
    copy_keys(nc, k, k.bank[2], k.core_kT, k.bk_cope, sem["core_k_ready"])
    act.wait_ge(sem["core_xT_psum"], 1)
    nc.scalar.activation(whole(k.core_norm.xT), k.bank[1][:], ACT.Copy).then_inc(sem["core_xT_ready"], 1)
    act.wait_ge(sem["core_q_psum"], 1)
    copy_queries(nc, k.bank[3], k.core_qT, k.bq_cope, sem["core_q_ready"])
    act.wait_ge(sem["core_offset_psum"], 1)
    nc.scalar.activation(k.core_offset[:], k.bank[1][:, 0:NT * H], ACT.Copy).then_inc(sem["core_offset_ready"], 1)
    act.wait_ge(sem["core_offset_ready"], 1)

    def gates(h):
        act.wait_ge(sem["core_scores"], h + 1)
        if h >= 1:
            act.wait_ge(sem["core_low"], h)
            act.wait_ge(sem["core_gates"], h)
        gate = k.gate[:, :, 0:S]
        nc.scalar.activation(gate, k.bank[0][:].rearrange("p (t s) -> p t s", t=NT), ACT.Tanh,
                             scale=-0.5 * INV_SQRT_HD).then_inc(sem["core_scores_copied"], 1)
        if h >= 2:
            act.wait_ge(sem["core_partial"], h - 1)
        for t in range(NT):
            nc.scalar.activation(k.core_scores[:, h % 2, t, :], k.bank[0][:, t * S:(t + 1) * S], ACT.Identity,
                                 bias=k.core_offset[:, t * H + h:t * H + h + 1])\
                .then_inc(sem["core_scores_copied"], 1)
        act.wait_ge(sem["core_scores_copied"], (NT + 1) * (h + 1))
        nc.scalar.activation(gate, gate, ACT.Identity, scale=0.5, bias=k.half[:]).then_inc(sem["core_gates"], 1)

    gates(0)
    for s in range(H + 3):
        if s < H:
            act.wait_ge(sem["core_shift"], s + 1)
            if s >= 1:
                act.wait_ge(sem["core_pool_shift"], 3 * s)
            nc.scalar.activation(k.shift16[:], k.shift[:], ACT.Copy).then_inc(sem["core_shift_copied"], 1)
        h = s - 2
        if 0 <= h < H:
            act.wait_ge(sem["core_z_ready"], h + 1)
            if h >= 1:
                act.wait_ge(sem["core_pT_psum"], h)
            for t in range(NT):
                nc.scalar.activation(k.core_prob[:, t, :], k.z[:, h % 2, t, :], ACT.Exp,
                                     bias=k.negmax[:, h % 2, t:t + 1], scale=INV_SQRT_HD,
                                     accum_out=k.core_sums[:, t, h:h + 1]).then_inc(sem["core_exp"], 1)
        if s + 1 < H:
            gates(s + 1)
        for _ in range(PIECES // 2):
            next(side, None)
        if 0 <= h < H:
            act.wait_ge(sem["core_pT_psum"], h + 1)
            if h >= 2:
                act.wait_ge(sem["core_pv_done"], h - 1)
            nc.scalar.activation(whole(k.core_pT[:, h % 2]), k.bank[2][:], ACT.Copy)\
                .then_inc(sem["core_pT_ready"], 1)
        for _ in range(PIECES - PIECES // 2):
            next(side, None)
        if s < H:
            act.wait_ge(sem["core_moved"], s + 1)
            if s >= 1:
                act.wait_ge(sem["core_steps"], 2 * s)
            nc.scalar.activation(whole(k.slope), k.bank[1][:], ACT.Copy).then_inc(sem["core_slope"], 1)


def core_pool(nc, k, pool, side):
    sem = k.sem
    norm_pool(nc, k, pool, k.core_norm, "core_")

    def diff(h):
        pool.wait_ge(sem["core_low"], h + 1)
        nc.gpsimd.tensor_tensor(k.diff[:], k.c[:, :, 0:S], k.low[:], ALU.subtract)\
            .then_inc(sem["core_diff"], 1)

    diff(0)
    for s in range(H + 3):
        if s < H:
            b = s % 2
            pool.wait_ge(sem["core_shift_copied"], s + 1)
            nc.gpsimd.tensor_tensor(k.minus_u[:], k.shift16[:], k.t_row[:].unsqueeze(1)
                                    .broadcast_to([P, NT, S + 1]), ALU.subtract).then_inc(sem["core_pool_shift"], 1)
            nc.gpsimd.tensor_tensor(k.neg_rest[:], k.shift16[:, :, 0:S], k.c[:, :, 0:S], ALU.subtract)\
                .then_inc(sem["core_pool_shift"], 1)
            pool.wait_ge(sem["core_pool_shift"], 3 * s + 2)
            nc.gpsimd.tensor_tensor(k.rises[:], k.minus_u[:, :, 1:S + 1], k.minus_u[:, :, 0:S], ALU.subtract)\
                .then_inc(sem["core_pool_shift"], 1)
            pool.wait_ge(sem["core_pool_shift"], 3 * s + 3)
        for _ in range(PIECES):
            next(side, None)
        if s + 1 < H:
            diff(s + 1)
        if s < H:
            pool.wait_ge(sem["core_slope"], s + 1)
            if s >= 1:
                pool.wait_ge(sem["core_z_ready"], s)
            nc.gpsimd.tensor_tensor(k.steps[:], k.slope[:], k.rises[:], ALU.mult).then_inc(sem["core_steps"], 1)
            nc.gpsimd.tensor_tensor(k.partial[:], k.slope[:], k.neg_rest[:], ALU.mult).then_inc(sem["core_steps"], 1)
            pool.wait_ge(sem["core_steps"], 2 * s + 2)
            nc.gpsimd.tensor_tensor(k.partial[:], k.partial[:], k.core_scores[:, b], ALU.add)\
                .then_inc(sem["core_partial"], 1)
            pool.wait_ge(sem["core_partial"], s + 1)


def core_vector(nc, k, dve, step, side):
    sem = k.sem
    dve.wait_ge(sem["core_loads"], 16 * 2 * NT)
    norm_vector(nc, k, dve, step, k.core_norm, "core_")
    dve.wait_ge(sem["core_v_psum"], 1)
    nc.vector.tensor_tensor(k.core_v[:], k.bank[0][:].rearrange("p (t n) -> p t n", t=NT),
                            k.bv_cope[:].unsqueeze(1).broadcast_to([P, NT, D]), ALU.add)\
        .then_inc(sem["core_v_ready"], 1)
    flat = "p t s -> p (t s)"

    def scan(h):
        dve.wait_ge(sem["core_gates"], h + 1)
        if h >= 1:
            dve.wait_ge(sem["core_pool_shift"], 3 * h - 1)
        step(nc.vector.tensor_tensor_scan(
            k.c[:].rearrange(flat)[:, ::-1], k.gate[:].rearrange(flat)[:, ::-1],
            k.cap[:].rearrange(flat)[:, ::-1], 0.0, ALU.add, ALU.max))
        nc.vector.tensor_scalar(k.low[:], k.c[:, :, 0:S], ROUND, ROUND + 1.0, ALU.add, ALU.subtract)\
            .then_inc(sem["core_low"], 1)

    tab = k.bank[1][:].rearrange("p (t s) -> p t s", t=NT)
    scan(0)
    for s in range(H + 3):
        if s < H:
            dve.wait_ge(sem["core_diff"], s + 1)
            if s >= 1:
                dve.wait_ge(sem["core_shift_copied"], s)
            nc.vector.scalar_tensor_tensor(k.shift[:, :, 0:S], k.diff[:], 1.0, k.low[:], ALU.is_gt,
                                           ALU.add).then_inc(sem["core_shift"], 1)
            dve.wait_ge(sem["core_shift"], s + 1)
            for n, b in enumerate((32, 16, 8, 4, 2, 1)):
                step(nc.vector.tensor_scalar(k.mask[:], k.shift[:, :, 0:S], b, None, ALU.bitwise_and))
                if n == 0:
                    dve.wait_ge(sem["core_table"], s + 1)
                move = nc.vector.copy_predicated(tab[:, :, 0:S - b], k.mask[:, :, 0:S - b], tab[:, :, b:S])
                if b > 1:
                    step(move)
                    next(side, None)
                else:
                    move.then_inc(sem["core_moved"], 1)
                    dve.wait_ge(sem["core_moved"], s + 1)
        else:
            for _ in range(PIECES - 1):
                next(side, None)
        if s + 1 < H:
            scan(s + 1)
        next(side, None)
        h = s - 1
        if 0 <= h < H:
            dve.wait_ge(sem["core_steps"], 2 * h + 1)
            if h >= 2:
                dve.wait_ge(sem["core_exp"], NT * (h - 1))
            for t in range(NT):
                step(nc.vector.tensor_tensor_scan(k.z[:, h % 2, t, ::-1], k.steps[:, t, ::-1],
                                                  k.steps[:, t, ::-1], 0.0, ALU.add, ALU.bypass))
            dve.wait_ge(sem["core_partial"], h + 1)
            for t in range(NT):
                step(nc.vector.tensor_tensor_reduce(
                    out=k.z[:, h % 2, t, :], in0=k.z[:, h % 2, t, :], in1=k.partial[:, t, :], scale=1.0,
                    scalar=-3e38, op0=ALU.add, op1=ALU.max, accum_out=k.rowmax[:, t:t + 1]))
            nc.vector.tensor_scalar(k.negmax[:, h % 2], k.rowmax[:], -INV_SQRT_HD, None, ALU.mult)\
                .then_inc(sem["core_z_ready"], 1)
            dve.wait_ge(sem["core_z_ready"], h + 1)


def core_tail(nc, k, dve, step):
    sem = k.sem
    dve.wait_ge(sem["core_exp"], NT * H)
    step(nc.vector.reciprocal(k.core_rsum[:], k.core_sums[:]))
    dve.wait_ge(sem["core_pv_done"], H)
    step(nc.vector.tensor_tensor(k.core_o[:].rearrange("p t (h d) -> p t h d", d=HD),
                                 k.bank[3][:].rearrange("p (t h d) -> p t h d", t=NT, h=H),
                                 k.core_rsum[:].unsqueeze(3).broadcast_to([P, NT, H, HD]), ALU.mult))



def side_tensor(nc, k, pe):
    sem = k.sem
    n = k.norm
    pe.wait_ge(sem["loads"], 16 * 2 * NT)
    transpose_tokens(nc, k, k.bank[4], k.ctx).then_inc(sem["tail_ctxT_psum"], 1)
    transpose_tokens(nc, k, k.bank[5], k.core_o).then_inc(sem["tail_oT_psum"], 1)
    yield
    pe.wait_ge(sem["tail_oT_ready"], 1)
    token_projection(nc, k.wo_cope, k.oT, k.bank[6]).then_inc(sem["tail_y_done"], 1)
    yield
    yield
    pe.wait_ge(sem["ffn_xn_ready"], NT)
    pe.wait_ge(sem["tail_ctxT_ready"], 1)
    transpose_tokens(nc, k, k.bank[4], n.xn).then_inc(sem["ffn_xT_psum"], 1)
    pe.wait_ge(sem["ffn_xT_ready"], 1)
    for t in range(NT):
        for c in range(NC):
            last = nc.tensor.matmul(k.bank[7][:, t * E:(t + 1) * E], n.xT[:, c, t * P:(t + 1) * P],
                                    k.wgate[:, c, :], start=(c == 0), stop=(c == NC - 1))
    last.then_inc(sem["ffn_logits"], 1)

    def up(m):
        e, par = divmod(m, 2)
        for w, bank, signal in ((k.w1, 4, "ffn_h1_done"), (k.w3, 5 + m % 2, "ffn_h3_done")):
            if bank == 4 and m >= 1:
                pe.wait_ge(sem["ffn_h1_ready"], 2 * m)
            if bank != 4 and m >= 2:
                pe.wait_ge(sem["ffn_u_ready"], 2 * (m - 1))
            for f in range(2):
                for c in range(NC):
                    last = nc.tensor.matmul(k.bank[bank][:, f * S:(f + 1) * S],
                                            w[:, e, c, par, f * P:(f + 1) * P], n.xT[:, c, :],
                                            start=(c == 0), stop=(c == NC - 1))
            last.then_inc(sem[signal], 1)

    def down(e):
        pe.wait_ge(sem["ffn_a_ready"], e + 1)
        if e == 0:
            pe.wait_ge(sem["ffn_init"], 2)
        else:
            pe.wait_ge(sem["ffn_acc"], 2 * e)
        for t in range(NT):
            for f in range(2):
                last = nc.tensor.matmul(k.bank[7][:, t * D:(t + 1) * D], k.a[:, e % 2, f, t * P:(t + 1) * P],
                                        k.w2[:, e, f, :], start=(f == 0), stop=(f == 1))
        last.then_inc(sem["ffn_y_done"], 1)

    yield
    up(0)
    yield
    up(1)
    pe.wait_ge(sem["ffn_cw_ready"], 1)
    for t in range(NT):
        last = nc.tensor.transpose(k.bank[7][0:NE, t * P:(t + 1) * P], k.cw[:, t, :], k.ident[:])
    last.then_inc(sem["ffn_cwT_psum"], 1)
    yield
    up(2)
    pe.wait_ge(sem["ffn_cwT_ready"], 1)
    for t in range(NT):
        last = nc.tensor.matmul(k.bank[7][:, t * D:(t + 1) * D], k.cwT[0:NE, t * P:(t + 1) * P],
                                k.b2[0:NE, :], start=True, stop=True)
    last.then_inc(sem["ffn_init"], 1)
    yield
    up(3)
    down(0)
    yield
    for e in range(2, NE):
        up(2 * e)
        yield
        up(2 * e + 1)
        down(e - 1)
        yield
    down(NE - 1)
    yield
    yield
    yield from attention_tensor(nc, k, pe, "cross")
    yield from attention_tensor(nc, k, pe, "gated")


def side_scalar(nc, k, act):
    sem = k.sem
    n = k.norm
    act.wait_ge(sem["tail_ctxT_psum"], 1)
    nc.scalar.activation(whole(k.ctxT), k.bank[4][:], ACT.Copy).then_inc(sem["tail_ctxT_ready"], 1)
    act.wait_ge(sem["tail_oT_psum"], 1)
    nc.scalar.activation(whole(k.oT), k.bank[5][:], ACT.Copy).then_inc(sem["tail_oT_ready"], 1)
    yield
    yield
    yield
    act.wait_ge(sem["ffn_xT_psum"], 1)
    nc.scalar.activation(whole(n.xT), k.bank[4][:], ACT.Copy).then_inc(sem["ffn_xT_ready"], 1)
    yield

    def first_linear(m):
        e, par = divmod(m, 2)
        act.wait_ge(sem["ffn_h1_done"], m + 1)
        if m >= 2:
            act.wait_ge(sem["ffn_u_ready"], 2 * (m - 1))
        for f in range(2):
            nc.scalar.activation(k.h1[:, m % 2, f, :], k.bank[4][:, f * S:(f + 1) * S], ACT.Identity,
                                 bias=k.b1[:, par, f, e:e + 1]).then_inc(sem["ffn_h1_ready"], 1)

    act.wait_ge(sem["ffn_max_ready"], 1)
    for t in range(NT):
        nc.scalar.activation(k.escore[:, t, :], k.bank[7][:, t * E:(t + 1) * E], ACT.Exp,
                             bias=k.enegmax[:, t:t + 1], accum_out=k.esum[:, t:t + 1])\
            .then_inc(sem["ffn_exp"], 1)
    first_linear(0)
    yield
    for e in range(NE):
        if e >= 1:
            first_linear(2 * e)
            if e == 1:
                act.wait_ge(sem["ffn_cwT_psum"], 1)
                nc.scalar.activation(k.cwT[0:NE, :], k.bank[7][0:NE, 0:S], ACT.Copy)\
                    .then_inc(sem["ffn_cwT_ready"], 1)
            yield
        act.wait_ge(sem["ffn_g_ready"], e + 1)
        nc.scalar.activation(k.eth, k.eg, ACT.Tanh, scale=0.5 * ALPHA).then_inc(sem["ffn_tanh"], 1)
        first_linear(2 * e + 1)
        yield
    yield
    yield
    yield from attention_scalar(nc, k, act, "cross")
    yield from attention_scalar(nc, k, act, "gated")


def side_pool(nc, k, pool):
    yield
    yield
    norm_pool(nc, k, pool, k.norm, "ffn_")
    yield
    yield
    for _ in range(2 * NE):
        yield
    yield
    yield
    yield from attention_pool(nc, k, pool, "cross")
    yield from attention_pool(nc, k, pool, "gated")


def side_vector(nc, k, dve):
    sem = k.sem
    step = stepper(dve, sem["dve_side"])
    yield
    dve.wait_ge(sem["tail_y_done"], 1)
    add_to_x(nc, k, step, k.bank[6], k.tanh_g[:, 0:1], k.bo_cope)
    yield
    norm_vector(nc, k, dve, step, k.norm, "ffn_")
    yield
    yield
    dve.wait_ge(sem["ffn_logits"], 1)
    logits = k.bank[7][:, 0:NT * E].rearrange("p (t e) -> p t e", t=NT)
    nc.vector.tensor_reduce(k.enegmax[:], logits, axis=AX.X, op=ALU.max, negate=True)\
        .then_inc(sem["ffn_max_ready"], 1)

    def hidden(m):
        e, par = divmod(m, 2)
        dve.wait_ge(sem["ffn_h3_done"], m + 1)
        for f in range(2):
            dve.wait_ge(sem["ffn_h1_ready"], 2 * m + f + 1)
            nc.vector.scalar_tensor_tensor(k.u[:, par, f, :], k.bank[5 + m % 2][:, f * S:(f + 1) * S],
                                           k.b3[:, par, f, e:e + 1], k.h1[:, m % 2, f, :],
                                           ALU.add, ALU.mult).then_inc(sem["ffn_u_ready"], 1)
        dve.wait_ge(sem["ffn_u_ready"], 2 * m + 2)

    both = "p f s -> p (f s)"

    def gate_part(e):
        hidden(2 * e)
        if e >= 1:
            dve.wait_ge(sem["ffn_a_ready"], e)
        nc.vector.tensor_scalar(k.eg, k.u[:, 0].rearrange(both), LIMIT, None, ALU.min)\
            .then_inc(sem["ffn_g_ready"], 1)

    def linear_part(e):
        hidden(2 * e + 1)
        step(nc.vector.tensor_scalar(k.el, k.u[:, 1].rearrange(both), -LIMIT, LIMIT, ALU.max, ALU.min))
        dve.wait_ge(sem["ffn_tanh"], e + 1)
        step(nc.vector.scalar_tensor_tensor(k.eg, k.eth, 1.0, k.eg, ALU.add, ALU.mult))
        if e >= 2:
            dve.wait_ge(sem["ffn_y_done"], e - 1)
        nc.vector.scalar_tensor_tensor(k.a[:, e % 2].rearrange(both), k.el, 1.0, k.eg,
                                       ALU.add, ALU.mult).then_inc(sem["ffn_a_ready"], 1)

    def accumulate(e):
        dve.wait_ge(sem["ffn_y_done"], e + 1)
        for t in range(NT):
            nc.vector.scalar_tensor_tensor(k.acc[:, t, :], k.bank[7][:, t * D:(t + 1) * D],
                                           k.cw[:, t, e:e + 1], k.acc[:, t, :], ALU.mult, ALU.add)\
                .then_inc(sem["ffn_acc"], 1)
        dve.wait_ge(sem["ffn_acc"], 2 * e + 2)

    dve.wait_ge(sem["ffn_exp"], NT)
    step(nc.vector.reciprocal(k.esum[:], k.esum[:]))
    step(nc.vector.tensor_tensor(k.escore[:], k.escore[:],
                                 k.esum[:].unsqueeze(2).broadcast_to([P, NT, E]), ALU.mult))
    step(nc.vector.tensor_tensor(k.ebiased[:], k.escore[:],
                                 k.gate_b[:].unsqueeze(1).broadcast_to([P, NT, E]), ALU.add))
    for t in range(NT):
        step(nc.vector.max(k.etop[:, t, :], k.ebiased[:, t, :]))
        step(nc.vector.max_index(k.eidx[:, t, :], k.etop[:, t, :], k.ebiased[:, t, :]))
        step(nc.vector.tensor_copy(k.eidxf[:, t, :], k.eidx[:, t, :]))
        step(nc.vector.tensor_scalar(k.ehot[:], k.expert_no[:], k.eidxf[:, t, 1:2], None, ALU.is_equal))
        step(nc.vector.scalar_tensor_tensor(k.ehot[:], k.expert_no[:], k.eidxf[:, t, 0:1], k.ehot[:],
                                            ALU.is_equal, ALU.add))
        last = nc.vector.tensor_tensor(k.cw[:, t, 0:E], k.escore[:, t, :], k.ehot[:], ALU.mult)
        if t < NT - 1:
            step(last)
    last.then_inc(sem["ffn_cw_ready"], 1)
    gate_part(0)
    yield
    linear_part(0)
    yield
    gate_part(1)
    dve.wait_ge(sem["ffn_init"], 1)
    nc.vector.tensor_copy(whole(k.acc), k.bank[7][:]).then_inc(sem["ffn_init"], 1)
    dve.wait_ge(sem["ffn_init"], 2)
    yield
    linear_part(1)
    accumulate(0)
    yield
    for e in range(2, NE):
        gate_part(e)
        yield
        linear_part(e)
        accumulate(e - 1)
        yield
    accumulate(NE - 1)
    step(nc.vector.scalar_tensor_tensor(whole(k.norm.x), whole(k.acc), k.tanh_g[:, 2:3], whole(k.norm.x),
                                        ALU.mult, ALU.add))
    yield
    yield
    yield from attention_vector(nc, k, dve, step, "cross")
    yield from attention_vector(nc, k, dve, step, "gated")


def add_to_x(nc, k, step, bank, scale, bias_row):
    x = k.norm.x
    step(nc.vector.scalar_tensor_tensor(whole(x), bank[:], scale, whole(x), ALU.mult, ALU.add))
    step(nc.vector.tensor_tensor(x[:], x[:], bias_row[:].unsqueeze(1).broadcast_to([P, NT, D]), ALU.add))



def attention_tensor(nc, k, pe, kind):
    sem = k.sem
    p = kind + "_"
    w = k.att[kind]
    n = k.norm
    pe.wait_ge(sem[p + "xn_ready"], NT)
    transpose_tokens(nc, k, k.bank[4], n.xn).then_inc(sem[p + "xT_psum"], 1)
    yield
    pe.wait_ge(sem[p + "xT_ready"], 1)
    src = n.xT if kind == "gated" else k.ctxT
    feature_projection(nc, w.wk, src, k.bank[5]).then_inc(sem[p + "k_psum"], 1)
    yield
    token_projection(nc, w.wv, src, k.bank[6]).then_inc(sem[p + "v_psum"], 1)
    yield
    if kind == "gated":
        token_projection(nc, w.wq, n.xT, k.bank[7]).then_inc(sem[p + "q_psum"], 1)
        yield
        pe.wait_ge(sem[p + "q_done"], 1)
        transpose_tokens(nc, k, k.bank[4], k.qn).then_inc(sem[p + "qT_psum"], 1)
    else:
        feature_projection(nc, w.wq, n.xT, k.bank[7]).then_inc(sem[p + "q_psum"], 1)
        yield
    yield
    pe.wait_ge(sem[p + "k_ready"], 2 * NC)
    pe.wait_ge(sem[p + "q_ready"], NC)
    pe.wait_ge(sem[p + "v_ready"], 1)
    for h in range(H):
        if h >= 2:
            pe.wait_ge(sem[p + "max_ready"], h - 1)
        scores(nc, h, k.qT, k.kT, k.bank[6 + h % 2]).then_inc(sem[p + "scores"], 1)
        yield
    pe.wait_ge(sem[p + "max_ready"], H + 1)
    maxT = k.bank[6].bitcast(BF16)
    for t in range(NT):
        last = nc.tensor.transpose(maxT[:, t * P:(t + 1) * P],
                                   k.max_parts[:, t].rearrange("p r m h -> p (r m h)"), k.ident16[:])
    last.then_inc(sem[p + "maxT_psum"], 1)
    yield

    def weigh_values(h):
        pe.wait_ge(sem[p + "pT_ready"], h + 1)
        for t in range(NT):
            for c in range(NT):
                last = nc.tensor.matmul(k.bank[4 + t][:, h * (HD + 1):(h + 1) * (HD + 1)],
                                        k.pT[:, h % 2, c, t * P:(t + 1) * P], k.v[:, c, h, :],
                                        start=(c == 0), stop=(c == NT - 1))
        last.then_inc(sem[p + "pv_done"], 1)

    pe.wait_ge(sem[p + "maxT_ready"], 1)
    for h in range(H):
        if h >= 2:
            pe.wait_ge(sem[p + "pT_ready"], h - 1)
        g, r, par = block_of(h)
        for c in range(NT):
            out = k.bank[6 + h % 2][:, c * S:(c + 1) * S]
            nc.tensor.matmul(out, k.kT[r, par, g, c * P:(c + 1) * P], k.qT[r, g, :], start=True, stop=False)
            last = nc.tensor.matmul(out, k.pick[r, h:h + 1].broadcast_to([HB, P]), k.maxT[r, :],
                                    start=False, stop=True)
        last.then_inc(sem[p + "scoresT"], 1)
        if h >= 1:
            weigh_values(h - 1)
        yield
    weigh_values(H - 1)
    yield
    pe.wait_ge(sem[p + "o_ready"], NT)
    pe.wait_ge(sem[p + "pT_ready"], H)
    transpose_tokens(nc, k, k.bank[6], k.o).then_inc(sem[p + "oT_psum"], 1)
    pe.wait_ge(sem[p + "oT_ready"], 1)
    if kind == "gated":
        for t in range(NT):
            for c in range(NC):
                last = nc.tensor.matmul(k.bank[4][:, t * NG:(t + 1) * NG], k.oT[:, c, t * P:(t + 1) * P],
                                        k.wrs[:, c, :], start=(c == 0), stop=(c == NC - 1))
        last.then_inc(sem[p + "logits"], 1)
    token_projection(nc, w.wo, k.oT, k.bank[7]).then_inc(sem[p + "y_done"], 1)
    yield
    yield


def attention_scalar(nc, k, act, kind):
    sem = k.sem
    p = kind + "_"
    w = k.att[kind]
    act.wait_ge(sem[p + "xT_psum"], 1)
    nc.scalar.activation(whole(k.norm.xT), k.bank[4][:], ACT.Copy).then_inc(sem[p + "xT_ready"], 1)
    yield
    act.wait_ge(sem[p + "k_psum"], 1)
    copy_keys(nc, k, k.bank[5], k.kT, w.bk, sem[p + "k_ready"])
    yield
    yield
    if kind == "gated":
        yield
        act.wait_ge(sem[p + "qT_psum"], 1)
        for g in range(NC):
            nc.scalar.activation(k.qT[:, g, :], k.bank[4][:, g * S:(g + 1) * S], ACT.Copy)\
                .then_inc(sem[p + "q_ready"], 1)
    else:
        act.wait_ge(sem[p + "q_psum"], 1)
        copy_queries(nc, k.bank[7], k.qT, w.bq, sem[p + "q_ready"])
        yield
    yield
    for h in range(H):
        yield
    act.wait_ge(sem[p + "maxT_psum"], 1)
    nc.scalar.activation(k.maxT[:], k.bank[6].bitcast(BF16)[:, 0:S], ACT.Copy)\
        .then_inc(sem[p + "maxT_ready"], 1)
    yield
    for h in range(H):
        act.wait_ge(sem[p + "scoresT"], h + 1)
        if h >= 2:
            act.wait_ge(sem[p + "pv_done"], h - 1)
        nc.scalar.activation(whole(k.pT[:, h % 2]), k.bank[6 + h % 2][:], ACT.Exp, scale=INV_SQRT_HD)\
            .then_inc(sem[p + "pT_ready"], 1)
        yield
    yield
    act.wait_ge(sem[p + "oT_psum"], 1)
    nc.scalar.activation(whole(k.oT), k.bank[6][:], ACT.Copy).then_inc(sem[p + "oT_ready"], 1)
    if kind == "gated":
        act.wait_ge(sem[p + "glog"], 1)
        nc.scalar.activation(whole(k.gexp), whole(k.glog), ACT.Exp).then_inc(sem[p + "gexp"], 1)
    yield
    yield


def attention_pool(nc, k, pool, kind):
    sem = k.sem
    p = kind + "_"
    norm_pool(nc, k, pool, k.norm, p)
    yield
    yield
    yield
    yield
    if kind == "gated":
        pool.wait_ge(sem[p + "norm_ready"], 1)
        nc.gpsimd.tensor_tensor(k.rnorm[:], k.sumsq[:], k.neghalf[:], ALU.pow).then_inc(sem[p + "rnorm_ready"], 1)
    yield
    for _ in range(2 * H + 1):
        yield
    yield
    yield
    yield


def attention_vector(nc, k, dve, step, kind):
    sem = k.sem
    p = kind + "_"
    w = k.att[kind]
    norm_vector(nc, k, dve, step, k.norm, p)
    yield
    yield
    dve.wait_ge(sem[p + "v_psum"], 1)
    nc.vector.tensor_tensor(k.v[:, :, :, 0:HD], k.bank[6][:].rearrange("p (t h d) -> p t h d", t=NT, h=H),
                            w.bv[:].rearrange("p (h d) -> p h d", h=H).unsqueeze(1)
                            .broadcast_to([P, NT, H, HD]), ALU.add).then_inc(sem[p + "v_ready"], 1)
    yield
    yield
    if kind == "gated":
        dve.wait_ge(sem[p + "q_psum"], 1)
        q = whole(k.qn)
        heads = k.qn.rearrange("p t (h d) -> p (t h) d", d=HD)
        step(nc.vector.tensor_tensor(k.qn, k.bank[7][:].rearrange("p (t n) -> p t n", t=NT),
                                     w.bq[:].unsqueeze(1).broadcast_to([P, NT, D]), ALU.add))
        step(nc.vector.tensor_tensor(whole(k.qsq), q, q, ALU.mult))
        nc.vector.tensor_reduce(k.sumsq[:], whole(k.qsq).rearrange("p (m d) -> p m d", d=HD),
                                axis=AX.X, op=ALU.add).then_inc(sem[p + "norm_ready"], 1)
        dve.wait_ge(sem[p + "rnorm_ready"], 1)
        step(nc.vector.tensor_tensor(heads, heads, k.rnorm[:].unsqueeze(2).broadcast_to([P, NT * H, HD]),
                                     ALU.mult))
        step(nc.vector.tensor_tensor(k.qn, k.qn, k.qe_row[:].unsqueeze(1).broadcast_to([P, NT, D]), ALU.add))
        nc.vector.tensor_tensor(k.qn.rearrange("p t (h d) -> p t h d", d=HD),
                                k.qn.rearrange("p t (h d) -> p t h d", d=HD),
                                k.temp_row[:].unsqueeze(2).unsqueeze(1).broadcast_to([P, NT, H, HD]),
                                ALU.mult).then_inc(sem[p + "q_done"], 1)
    yield
    for h in range(H):
        dve.wait_ge(sem[p + "scores"], h + 1)
        nc.vector.tensor_reduce(k.row_negmax[:, :, h], k.bank[6 + h % 2][:].rearrange("p (t s) -> p t s", t=NT),
                                axis=AX.X, op=ALU.max, negate=True).then_inc(sem[p + "max_ready"], 1)
        yield
    dve.wait_ge(sem[p + "max_ready"], H)
    for t in range(NT):
        negmax = k.row_negmax[:, t, :].unsqueeze(1).broadcast_to([P, P // HB, H])
        step(nc.vector.tensor_copy(k.max_parts[:, t, :, 0, :], negmax))
        last = nc.vector.tensor_tensor(k.max_parts[:, t, :, 1, :], negmax, k.max_parts[:, t, :, 0, :],
                                       ALU.subtract)
        if t < NT - 1:
            step(last)
    last.then_inc(sem[p + "max_ready"], 1)
    yield
    for h in range(H):
        yield
    yield
    dve.wait_ge(sem[p + "pv_done"], H)
    for t in range(NT):
        ov = k.bank[4 + t][:, 0:H * (HD + 1)].rearrange("p (h d) -> p h d", h=H)
        step(nc.vector.reciprocal(k.rsum[:, t, :], ov[:, :, HD]))
        nc.vector.tensor_tensor(k.o[:, t, :].rearrange("p (h d) -> p h d", d=HD), ov[:, :, 0:HD],
                                k.rsum[:, t, :].unsqueeze(2).broadcast_to([P, H, HD]), ALU.mult)\
            .then_inc(sem[p + "o_ready"], 1)
    if kind == "cross":
        yield
        dve.wait_ge(sem[p + "y_done"], 1)
        add_to_x(nc, k, step, k.bank[7], k.tanh_g[:, 1:2], w.tbo)
        yield
        return
    dve.wait_ge(sem[p + "logits"], 1)
    step(nc.vector.tensor_tensor(k.glog[:], k.bank[4][:, 0:NT * NG].rearrange("p (t n) -> p t n", t=NT),
                                 k.brs_row[:].unsqueeze(1).broadcast_to([P, NT, NG]), ALU.add))
    parts = ((0, H - 1), (H - 1, NG))
    for m, (a, b) in enumerate(parts):
        step(nc.vector.tensor_reduce(k.gmax[:, m, :], k.glog[:, :, a:b], axis=AX.X, op=ALU.max))
    for m, (a, b) in enumerate(parts):
        last = nc.vector.tensor_tensor(k.glog[:, :, a:b], k.glog[:, :, a:b],
                                       k.gmax[:, m, :].unsqueeze(2).broadcast_to([P, NT, b - a]), ALU.subtract)
        if m == 0:
            step(last)
    last.then_inc(sem[p + "glog"], 1)
    yield
    dve.wait_ge(sem[p + "gexp"], 1)
    for m, (a, b) in enumerate(parts):
        step(nc.vector.tensor_reduce(k.gsum[:, m, :], k.gexp[:, :, a:b], axis=AX.X, op=ALU.add))
    step(nc.vector.reciprocal(k.gsum[:], k.gsum[:]))
    for m, (a, b) in enumerate(parts):
        step(nc.vector.tensor_tensor(k.gexp[:, :, a:b], k.gexp[:, :, a:b],
                                     k.gsum[:, m, :].unsqueeze(2).broadcast_to([P, NT, b - a]), ALU.mult))
    for t in range(NT):
        step(nc.vector.max(k.top8[:, t, :], k.gexp[:, t, 0:H - 1]))
    step(nc.vector.tensor_reduce(k.gscale[:, 0, :], k.top8[:, :, 0:TOP], axis=AX.X, op=ALU.add))
    step(nc.vector.tensor_reduce(k.gscale[:, 1, :], k.gexp[:, :, H - 1:NG], axis=AX.X, op=ALU.add))
    step(nc.vector.scalar_tensor_tensor(k.gscale[:, 0, :], k.gscale[:, 0, :], 2.0 * TOP,
                                        k.gexp[:, :, NG - 1], ALU.mult, ALU.mult))
    step(nc.vector.scalar_tensor_tensor(k.gscale[:, 1, :], k.gscale[:, 1, :], 2.0,
                                        k.gexp[:, :, NG - 2], ALU.mult, ALU.mult))
    step(nc.vector.tensor_tensor(k.gscale[:, 0, :], k.gscale[:, 0, :], k.gscale[:, 1, :], ALU.add))
    step(nc.vector.tensor_scalar(k.gscale[:, 0, :], k.gscale[:, 0, :], k.tanh_g[:, 3:4], None, ALU.mult))
    dve.wait_ge(sem[p + "y_done"], 1)
    x = k.norm.x
    for t in range(NT):
        step(nc.vector.scalar_tensor_tensor(x[:, t, :], k.bank[7][:, t * D:(t + 1) * D],
                                            k.gscale[:, 0, t:t + 1], x[:, t, :], ALU.mult, ALU.add))
    nc.vector.tensor_tensor(x[:], x[:], w.tbo[:].unsqueeze(1).broadcast_to([P, NT, D]), ALU.add)\
        .then_inc(sem[p + "x_ready"], 1)
    yield


def run_pass(nc, k, core, rest):
    sem = k.sem
    with nc.Block() as block:
        @block.sync
        def _(sp):
            if rest is not None:
                for t in range(NT):
                    sp.dma_start(k.ctx[:, t, :], k.ctx_rows(rest, t)).then_inc(sem["loads"], 16)
                    sp.dma_start(k.norm.x[:, t, :], k.x_rows(rest, t)).then_inc(sem["loads"], 16)
                sp.wait_ge(sem["gated_x_ready"], 1)
                for t in range(NT):
                    sp.dma_start(k.out_rows(rest, t), k.norm.x[:, t, :]).then_inc(sem["stores"], 16)
                sp.wait_ge(sem["stores"], 16 * NT)

        @block.gpsimd
        def _(pool):
            side = side_pool(nc, k, pool) if rest is not None else iter(())
            if core is not None:
                core_pool(nc, k, pool, side)
            for _ in side:
                pass

        @block.tensor
        def _(pe):
            side = side_tensor(nc, k, pe) if rest is not None else iter(())
            if core is not None:
                core_tensor(nc, k, pe, side)
            for _ in side:
                pass

        @block.scalar
        def _(act):
            if core is not None:
                for t in range(NT):
                    act.dma_start(k.core_ctx[:, t, :], k.ctx_rows(core, t)).then_inc(sem["core_loads"], 16)
                    act.dma_start(k.core_norm.x[:, t, :], k.x_rows(core, t)).then_inc(sem["core_loads"], 16)
            side = side_scalar(nc, k, act) if rest is not None else iter(())
            if core is not None:
                core_scalar(nc, k, act, side)
            for _ in side:
                pass

        @block.vector
        def _(dve):
            side = side_vector(nc, k, dve) if rest is not None else iter(())
            if core is not None:
                step = stepper(dve, sem["dve_core"])
                core_vector(nc, k, dve, step, side)
            for _ in side:
                pass
            if core is not None:
                core_tail(nc, k, dve, step)
    zero(nc, k)


def build(nc, x, ctx_in, g_xattn, g_ffn, Wq0, bq0, Wk0, bk0, Wv0, bv0, Wo0, bo0, pos_emb,
          gate_w, gate_b, w1, b1, w3, b3, w2, b2, sw1, sb1, sw3, sb3, sw2, sb2,
          wq1, bq1, wkv1, bkv1, wo1, bo1, Wq2, bq2, Wk2, bk2, Wv2, bv2, Wp2, bp2, Wr, br, Ws, bs,
          temperature, query_emb, out):
    with ExitStack() as ctx:
        k = Kernel()
        k.stack = ctx

        def sb(name, shape, dt=F32):
            return k.stack.enter_context(nc.sbuf_tensor(name, shape, dt))

        k.sem = {name: ctx.enter_context(nc.semaphore(name)) for name in SEMS}
        k.banks = ctx.enter_context(nc.psum_tensor("banks", [P, 8, 512], F32))
        k.bank = [k.banks[:, n, :] for n in range(8)]

        k.wq_cope = sb("wq_cope", [P, NC, D])
        k.wk_cope = sb("wk_cope", [P, NC, D])
        k.wv_cope = sb("wv_cope", [P, NC, D])
        k.wo_cope = sb("wo_cope", [P, NC, D])
        k.wq_cross = sb("wq_cross", [P, NC, D])
        k.wk_cross = sb("wk_cross", [P, NC, D])
        k.wv_cross = sb("wv_cross", [P, NC, D])
        k.wo_cross = sb("wo_cross", [P, NC, D])
        k.wq_gated = sb("wq_gated", [P, NC, D])
        k.wk_gated = sb("wk_gated", [P, NC, D])
        k.wv_gated = sb("wv_gated", [P, NC, D])
        k.wo_gated = sb("wo_gated", [P, NC, D])
        k.w1 = sb("w1", [P, NE, NC, 2, F])
        k.w3 = sb("w3", [P, NE, NC, 2, F])
        k.w2 = sb("w2", [P, NE, 2, D])
        k.b1 = sb("b1", [P, 2, 2, NE])
        k.b3 = sb("b3", [P, 2, 2, NE])
        k.b2 = sb("b2", [NE, D])
        k.wgate = sb("wgate", [P, NC, E])
        k.wrs = sb("wrs", [P, NC, NG])
        k.table = sb("table", [P, 2, S])
        k.first = sb("first", [P, HG])
        k.parity = sb("parity", [P, 2])
        k.bq_cope = sb("bq_cope", [P, NC])
        k.bk_cope = sb("bk_cope", [P, 2, NC])
        k.bq_cross = sb("bq_cross", [P, NC])
        k.bk_cross = sb("bk_cross", [P, 2, NC])
        k.bk_gated = sb("bk_gated", [P, 2, NC])
        k.bv_cope = sb("bv_cope", [P, D])
        k.bo_cope = sb("bo_cope", [P, D])
        k.bv_cross = sb("bv_cross", [P, D])
        k.bo_cross = sb("bo_cross", [P, D])
        k.bq_gated = sb("bq_gated", [P, D])
        k.bv_gated = sb("bv_gated", [P, D])
        k.bo_gated = sb("bo_gated", [P, D])
        k.qe_row = sb("qe_row", [P, D])
        k.temp_row = sb("temp_row", [P, H])
        k.gate_b = sb("gate_b", [P, E])
        k.brs_row = sb("brs_row", [P, NG])
        k.g_raw = sb("g_raw", [P, 4])
        k.tanh_g = sb("tanh_g", [P, 4])
        k.ident = sb("ident", [P, P])
        k.ident16 = sb("ident16", [P, P], BF16)
        k.pick = sb("pick", [P, H], BF16)
        k.neghalf = sb("neghalf", [P, NT * H])
        k.half = sb("half", [P, 1])
        k.cap = sb("cap", [P, NT, S + 1])
        k.t_row = sb("t_row", [P, S + 1], BF16)
        k.expert_no = sb("expert_no", [P, E])
        preamble = ctx.enter_context(ExitStack())
        k.stack = preamble
        k.temp_tmp = sb("temp_tmp", [P, 3, H])
        k.stage = sb("stage", [P, 10, D])
        k.bias_rows = sb("bias_rows", [NE, 2, 2 * F])
        k.small_rows = sb("small_rows", [32, D])
        k.emb = sb("emb", [P, NPOS + 1])
        k.emb_step = sb("emb_step", [P, NPOS])
        k.bk_raw = sb("bk_raw", [P, 3, NC])
        k.heads = sb("heads", [P, HG])
        k.t_row32 = sb("t_row32", [P, S + 1])
        k.pick32 = sb("pick32", [P, H])

        k.att = {
            "cross": Attention(wq=k.wq_cross, wk=k.wk_cross, wv=k.wv_cross, wo=k.wo_cross,
                               bq=k.bq_cross, bk=k.bk_cross, bv=k.bv_cross, tbo=k.bo_cross),
            "gated": Attention(wq=k.wq_gated, wk=k.wk_gated, wv=k.wv_gated, wo=k.wo_gated,
                               bq=k.bq_gated, bk=k.bk_gated, bv=k.bv_gated, tbo=k.bo_gated),
        }
        k.x_rows = lambda i, t: x[bass.ds(i, 1), t * P:(t + 1) * P, :].rearrange("a p n -> p (a n)")
        k.ctx_rows = lambda i, t: ctx_in[bass.ds(i, 1), t * P:(t + 1) * P, :].rearrange("a p n -> p (a n)")
        k.out_rows = lambda i, t: out[bass.ds(i, 1), t * P:(t + 1) * P, :].rearrange("a p n -> p (a n)")
        sem = k.sem

        with nc.Block() as block:
            @block.gpsimd
            def _(pool):
                step = stepper(pool, sem["pool_step"])
                exact = dict(channel_multiplier=0, allow_small_or_imprecise_dtypes=True)
                nc.gpsimd.iota(k.cap[:], pattern=[[0, NT], [-1, S + 1]], base=S - NPOS + 1, **exact)\
                    .then_inc(sem["consts"], 1)
                nc.gpsimd.iota(k.t_row32[:], pattern=[[-1, S + 1]], base=S - 1, **exact)
                nc.gpsimd.iota(k.expert_no[:], pattern=[[1, E]], base=0, **exact)
                step(nc.gpsimd.memset(k.ident[:], 0.0))
                nc.gpsimd.affine_select(out=k.ident[:], in_=k.ident[:], compare_op=ALU.not_equal, fill=1.0,
                                        base=0, pattern=[[-1, P]], channel_multiplier=1)\
                    .then_inc(sem["consts"], 1)
                step(nc.gpsimd.memset(k.pick32[:], 0.0))
                for base in range(0, -P, -H):
                    step(nc.gpsimd.affine_select(out=k.pick32[:], in_=k.pick32[:], compare_op=ALU.not_equal,
                                                 fill=1.0, base=base, pattern=[[-1, H]], channel_multiplier=1))
                step(nc.gpsimd.memset(k.heads[:], 1.0))
                step(nc.gpsimd.affine_select(out=k.heads[:], in_=k.heads[:], compare_op=ALU.is_ge, fill=0.0,
                                             base=0, pattern=[[-HD, HG]], channel_multiplier=1))
                nc.gpsimd.affine_select(out=k.heads[:], in_=k.heads[:], compare_op=ALU.is_ge, fill=0.0,
                                        base=HD - 1, pattern=[[HD, HG]], channel_multiplier=-1)\
                    .then_inc(sem["consts"], 1)

            @block.vector
            def _(dve):
                step = stepper(dve, sem["step"])
                dve.wait_ge(sem["consts"], 1)
                step(nc.vector.tensor_scalar(k.cap[:], k.cap[:], TINY, None, ALU.max))
                nc.vector.memset(k.cap[:, :, S:S + 1], TINY)
                nc.vector.memset(k.neghalf[:], -0.5)
                nc.vector.memset(k.half[:], 0.5)
                nc.vector.memset(k.emb[:], 0.0)
                nc.vector.memset(k.small_rows[:], 0.0)
                dve.wait_ge(sem["consts"], 3)
                nc.vector.tensor_copy(k.ident16[:], k.ident[:])
                nc.vector.tensor_copy(k.pick[:], k.pick32[:])
                nc.vector.tensor_copy(k.t_row[:], k.t_row32[:])
                for par in range(2):
                    nc.vector.tensor_reduce(k.parity[:, par:par + 1], k.heads[:, par::2], axis=AX.X, op=ALU.add)
        zero(nc, k)

        def expert_blocks(e, a1, a3, a2, at):
            blocks = []
            for dst, src in ((k.w1, a1), (k.w3, a3)):
                for r in range(2 * F // P):
                    n = P // 2
                    blocks.append((src[r * P:(r + 1) * P, :],
                                   dst[:, at, :, :, r * n:(r + 1) * n].rearrange("p e c t j -> p (e c) t j"),
                                   "parity"))
            for r in range(D // P):
                blocks.append((a2[r * P:(r + 1) * P, :],
                               k.w2[:, at, :, r * P:(r + 1) * P].rearrange("p e f n -> p (e f) n"), "half"))
            return blocks

        flat = "e r n -> (e r) n"
        with nc.Fori(0, E) as e:
            transpose_weights(nc, k, expert_blocks(e, w1[bass.ds(e, 1)].rearrange(flat),
                                                   w3[bass.ds(e, 1)].rearrange(flat),
                                                   w2[bass.ds(e, 1)].rearrange(flat), bass.ds(e, 1)))
        transpose_weights(nc, k, expert_blocks(E, sw1, sw3, sw2, slice(E, NE)))
        for some in (((k.wq_cope, Wq0), (k.wk_cope, Wk0), (k.wv_cope, Wv0), (k.wo_cope, Wo0)),
                     ((k.wq_gated, Wq2), (k.wk_gated, Wk2), (k.wv_gated, Wv2), (k.wo_gated, Wp2))):
            transpose_weights(nc, k, [(src[r * P:(r + 1) * P, :], dst[:, :, r * P:(r + 1) * P], "plain")
                                      for dst, src in some for r in range(D // P)])

        row = lambda a: a.rearrange("(o n) -> o n", o=1)
        columns = lambda dst, a: [(dst[:, g:g + 1], a[g * P:(g + 1) * P].rearrange("(p o) -> p o", o=1))
                                  for g in range(NC)]
        with nc.Block() as block:
            on_sync = [(k.bias_rows[0:E, 0, :], b1), (k.bias_rows[E:NE, 0, :], row(sb1)),
                       (k.bias_rows[0:E, 1, :], b3), (k.bias_rows[E:NE, 1, :], row(sb3)),
                       (k.b2[0:E, :], b2), (k.b2[E:NE, :], row(sb2)),
                       (k.small_rows[0:E, :], gate_w), (k.small_rows[E:E + H - 1, :], Wr),
                       (k.small_rows[E + H - 1:E + NG, :], Ws)]
            for dst, src in ((k.bq_cope, bq0), (k.bq_cross, bq1), (k.bk_raw[:, 0, :], bk0),
                             (k.bk_raw[:, 1, :], bkv1[0:D]), (k.bk_raw[:, 2, :], bk2)):
                on_sync += columns(dst, src)
            for c in range(NC):
                r = slice(c * P, (c + 1) * P)
                on_sync += [(k.wq_cross[:, c, :], wq1[r, :]), (k.wk_cross[:, c, :], wkv1[r, 0:D]),
                            (k.wv_cross[:, c, :], wkv1[r, D:2 * D]), (k.wo_cross[:, c, :], wo1[r, :])]
            on_act = [(dst[:], row(src).broadcast_to([P, src.shape[0]]))
                      for dst, src in ((k.bv_cope, bv0), (k.bo_cope, bo0), (k.bo_cross, bo1),
                                       (k.bq_gated, bq2), (k.bv_gated, bv2), (k.bo_gated, bp2),
                                       (k.gate_b, gate_b))]
            on_act += [(k.bv_cross[:], row(bkv1[D:2 * D]).broadcast_to([P, D])),
                       (k.qe_row[:], query_emb.rearrange("h o d -> o (h d)").broadcast_to([P, D])),
                       (k.temp_row[:], temperature.rearrange("h a b -> (a b) h").broadcast_to([P, H])),
                       (k.brs_row[:, 0:H - 1], row(br).broadcast_to([P, H - 1])),
                       (k.brs_row[:, H - 1:NG], row(bs).broadcast_to([P, 2])),
                       (k.g_raw[:, 0:2], row(g_xattn).broadcast_to([P, 2])),
                       (k.g_raw[:, 2:4], row(g_ffn).broadcast_to([P, 2]))]
            on_act += [(k.emb[HD * j:HD * (j + 1), 0:NPOS], pos_emb) for j in range(HG)]
            all_loads = 16 * (len(on_sync) + len(on_act))

            @block.sync
            def _(sp):
                for dst, src in on_sync:
                    sp.dma_start(dst, src).then_inc(sem["loads"], 16)

            @block.scalar
            def _(act):
                for dst, src in on_act:
                    act.dma_start(dst, src).then_inc(sem["loads"], 16)
                step = stepper(act, sem["dve_side"])
                act.wait_ge(sem["loads"], all_loads)
                step(nc.scalar.activation(k.tanh_g[:], k.g_raw[:], ACT.Tanh))
                act.wait_ge(sem["consts"], 1)
                step(nc.scalar.activation(k.temp_tmp[:, 1, :], k.temp_tmp[:, 0, :], ACT.Exp, scale=-1.0))
                step(nc.scalar.activation(k.temp_tmp[:, 2, :], k.temp_tmp[:, 1, :], ACT.Ln, bias=1.0))

            @block.vector
            def _(dve):
                step = stepper(dve, sem["step"])
                dve.wait_ge(sem["loads"], all_loads)
                nc.vector.scalar_tensor_tensor(k.temp_tmp[:, 0, :], k.temp_row[:], -1.0, k.temp_row[:],
                                               ALU.mult, ALU.max)\
                    .then_inc(sem["consts"], 1)
                for n, dst in enumerate((k.bk_cope, k.bk_cross, k.bk_gated)):
                    for par in range(2):
                        nc.vector.tensor_scalar(dst[:, par, :], k.bk_raw[:, n, :], k.parity[:, par:par + 1],
                                                None, ALU.mult)
                step(nc.vector.tensor_copy(k.emb[:, NPOS:NPOS + 1], k.emb[:, NPOS - 1:NPOS]))
                step(nc.vector.tensor_tensor(k.emb_step[:], k.emb[:, 1:NPOS + 1], k.emb[:, 0:NPOS], ALU.subtract))
                for par in range(2):
                    nc.vector.tensor_scalar(k.table[:, par, :].rearrange("p (r b) -> p r b", b=NPOS),
                                            k.emb_step[:, ::-1].unsqueeze(1).broadcast_to([P, S // NPOS, NPOS]),
                                            k.parity[:, par:par + 1], 1.0 / INV_SQRT_HD, ALU.mult, ALU.mult)
                nc.vector.tensor_scalar(k.first[:], k.heads[:], k.emb[:, 0:1], 1.0 / INV_SQRT_HD,
                                        ALU.mult, ALU.mult)
                dve.wait_ge(sem["dve_side"], 3)
                step(nc.vector.scalar_tensor_tensor(k.temp_row[:], k.temp_row[:], 0.0, k.temp_tmp[:, 2, :],
                                                    ALU.max, ALU.add))
                for n, b in ((0, k.bo_cope), (1, k.bo_cross), (3, k.bo_gated)):
                    nc.vector.tensor_scalar(b[:], b[:], k.tanh_g[:, n:n + 1], None, ALU.mult)
        zero(nc, k)
        with nc.Block() as block:
            @block.tensor
            def _(pe):
                for n in range(2):
                    for par in range(2):
                        for f in range(2):
                            at = (2 * n + par) * 2 + f
                            src = k.bias_rows[:, n, :].rearrange("e (f j t) -> e t f j", f=2, t=2)[:, par, f, :]
                            nc.tensor.transpose(k.bank[0][:, at * 16:at * 16 + NE], src, k.ident[0:NE, 0:NE])
                for c in range(NC):
                    last = nc.tensor.transpose(k.bank[2][:, c * 32:(c + 1) * 32],
                                               k.small_rows[:, c * P:(c + 1) * P], k.ident[0:32, 0:32])
                last.then_inc(sem["transposed"], 1)

            @block.vector
            def _(dve):
                dve.wait_ge(sem["transposed"], 1)
                src = k.bank[0][:, 0:128].rearrange("p (m e) -> p m e", e=16)
                for n, dst in enumerate((k.b1, k.b3)):
                    nc.vector.tensor_copy(dst[:].rearrange("p t f e -> p (t f) e"), src[:, 4 * n:4 * n + 4, 0:NE])
                src = k.bank[2][:, 0:64].rearrange("p (c n) -> p c n", c=NC)
                nc.vector.tensor_copy(k.wgate[:], src[:, :, 0:E])
                nc.vector.tensor_copy(k.wrs[:], src[:, :, E:E + NG])
        zero(nc, k)

        preamble.close()
        k.stack = ctx
        k.core_qT = sb("core_qT", [P, NC, S])
        k.core_kT = sb("core_kT", [P, 2, NC, S])
        k.core_v = sb("core_v", [P, NT, D])
        k.core_o = sb("core_o", [P, NT, D])
        k.core_offset = sb("core_offset", [P, NT * H])
        k.gate = sb("gate", [P, NT, S + 1])
        k.c = sb("c", [P, NT, S + 1])
        k.low = sb("low", [P, NT, S])
        k.diff = sb("diff", [P, NT, S])
        k.shift = sb("shift", [P, NT, S + 1], I16)
        k.mask = sb("mask", [P, NT, S], I16)
        k.shift16 = sb("shift16", [P, NT, S + 1], BF16)
        k.minus_u = sb("minus_u", [P, NT, S + 1], BF16)
        k.neg_rest = sb("neg_rest", [P, NT, S])
        k.rises = sb("rises", [P, NT, S], BF16)
        k.slope = sb("slope", [P, NT, S])
        k.steps = sb("steps", [P, NT, S])
        k.partial = sb("partial", [P, NT, S])
        k.core_scores = sb("core_scores", [P, 2, NT, S])
        k.z = sb("z", [P, 2, NT, S])
        k.rowmax = sb("rowmax", [P, NT])
        k.negmax = sb("negmax", [P, 2, NT])
        k.core_prob = sb("core_prob", [P, NT, S])
        k.core_pT = sb("core_pT", [P, 2, NT, S])
        k.core_sums = sb("core_sums", [P, NT, H])
        k.core_rsum = sb("core_rsum", [P, NT, H])

        def norm(name, x, xn, xT):
            n = Norm()
            n.x, n.xn, n.xT = x, xn, xT
            n.stats = sb(name + "stats", [P, NT, 6])
            n.mean_var = sb(name + "mean_var", [P, NT, 2])
            n.var = sb(name + "var", [P, NT])
            n.rstd = sb(name + "rstd", [P, NT])
            return n

        k.core_ctx, k.core_ctxT = k.z[:, 0], k.core_prob
        k.core_norm = norm("core_", k.core_pT[:, 0], k.z[:, 1], k.steps)

        k.norm = norm("side_", sb("x", [P, NT, D])[:], sb("xn", [P, NT, D])[:], sb("xT", [P, NC, S])[:])
        k.ctxT = sb("ctxT", [P, NC, S])
        k.qT = sb("qT", [P, NC, S])
        k.kT = sb("kT", [P, 2, NC, S])
        k.v = sb("v", [P, NT, H, HD + 1])
        k.o = sb("o", [P, NT, D])
        k.oT = sb("oT", [P, NC, S])
        k.u = sb("u", [P, 2, 2, S])
        k.a = sb("a", [P, 2, 2, S])
        k.cw = sb("cw", [P, NT, NE])
        k.cwT = sb("cwT", [NE, S])
        k.sumsq = sb("sumsq", [P, NT * H])
        k.rnorm = sb("rnorm", [P, NT * H])
        k.row_negmax = sb("row_negmax", [P, NT, H])
        k.max_parts = sb("max_parts", [P, NT, P // HB, 2, H], BF16)
        k.maxT = sb("maxT", [P, S], BF16)
        k.rsum = sb("rsum", [P, NT, H])
        k.glog = sb("glog", [P, NT, NG])
        k.gexp = sb("gexp", [P, NT, NG])
        k.gmax = sb("gmax", [P, 2, NT])
        k.gsum = sb("gsum", [P, 2, NT])
        k.gscale = sb("gscale", [P, 2, NT])
        k.top8 = sb("top8", [P, NT, 8])
        k.escore = sb("escore", [P, NT, E])
        k.ebiased = sb("ebiased", [P, NT, E])
        k.enegmax = sb("enegmax", [P, NT])
        k.esum = sb("esum", [P, NT])
        k.etop = sb("etop", [P, NT, 8])
        k.eidx = sb("eidx", [P, NT, 8], U32)
        k.eidxf = sb("eidxf", [P, NT, 8])
        k.ehot = sb("ehot", [P, E])
        flat2 = "p t s -> p (t s)"
        k.ctx, k.qn, k.qsq, k.pT, k.acc = k.u[:, 0], k.u[:, 0], k.u[:, 1], k.a, k.o
        k.h1 = k.kT
        k.eg, k.el, k.eth = (b.rearrange(flat2) for b in (k.oT[:], k.norm.xn, k.qT[:]))

        with nc.Block() as block:
            @block.vector
            def _(dve):
                nc.vector.memset(k.gate[:, :, S:S + 1], RESET)
                nc.vector.memset(k.shift[:, :, S:S + 1], 0)
                nc.vector.memset(k.v[:, :, :, HD:HD + 1], 1.0)
                nc.vector.memset(k.cw[:, :, E:NE], 1.0)

        run_pass(nc, k, 0, None)
        with nc.Fori(1, B) as i:
            run_pass(nc, k, i, i - 1)
        run_pass(nc, k, None, B - 1)


_INS = ['x', 'ctx_1024', 'g_xattn', 'g_ffn', 'L0_xattn_Wq_w', 'L0_xattn_Wq_b', 'L0_xattn_Wk_w', 'L0_xattn_Wk_b',
        'L0_xattn_Wv_w', 'L0_xattn_Wv_b', 'L0_xattn_Wo_w', 'L0_xattn_Wo_b', 'L0_xattn_pos_emb', 'L0_ffn_gate_w',
        'L0_ffn_gate_b', 'L0_ffn_w1', 'L0_ffn_b1', 'L0_ffn_w3', 'L0_ffn_b3', 'L0_ffn_w2', 'L0_ffn_b2',
        'L0_ffn_sw1', 'L0_ffn_sb1', 'L0_ffn_sw3', 'L0_ffn_sb3', 'L0_ffn_sw2', 'L0_ffn_sb2', 'L1_xattn_w_q',
        'L1_xattn_b_q', 'L1_xattn_w_kv', 'L1_xattn_b_kv', 'L1_xattn_w_out', 'L1_xattn_b_out', 'L1_ffn_Wq',
        'L1_ffn_bq', 'L1_ffn_Wk', 'L1_ffn_bk', 'L1_ffn_Wv', 'L1_ffn_bv', 'L1_ffn_Wp', 'L1_ffn_bp', 'L1_ffn_Wr',
        'L1_ffn_br', 'L1_ffn_Ws', 'L1_ffn_bs', 'L1_ffn_temperature', 'L1_ffn_query_embedding']


def kernel(**inputs):
    import numpy as _np
    import concourse.bacc as _bacc
    from concourse import mybir as _mybir
    from concourse.bass_utils import run_bass_kernel_spmd as _run

    nc = _bacc.Bacc("TRN2", target_bir_lowering=False, num_devices=1)
    arrays, args = {}, []
    for name in _INS:
        a = _np.ascontiguousarray(inputs[name])
        arrays[f"in_{name}"] = a
        args.append(nc.dram_tensor(f"in_{name}", a.shape, _mybir.dt.from_np(a.dtype), kind="ExternalInput").ap())
    out = nc.dram_tensor("out_0", (B, S, D), F32, kind="ExternalOutput").ap()
    build(nc, *args, out)
    return _run(nc, [arrays], core_ids=[0]).results[0]["out_0"]
```

```python
from contextlib import ExitStack

import concourse.bass as bass
from concourse import mybir

F32 = mybir.dt.float32
BF16 = mybir.dt.bfloat16
F16 = mybir.dt.float16
I16 = mybir.dt.int16
U32 = mybir.dt.uint32
ALU = mybir.AluOpType
ACT = mybir.ActivationFunctionType
AX = mybir.AxisListType

P = 128
D = 256
S = 256
B = 16
H = 16
HD = D // H
HB = 2 * HD
HG = P // HD
NC = D // P
NT = S // P
E = 8
NE = E + 1
F = 256
NPOS = 64
EPS = 1e-5
ALPHA = 1.702
LIMIT = 7.0
ROUND = 12582912.0
TINY = 1e-30
SCALE = 64.0
RESET = -1e9
INV_SQRT_HD = HD ** -0.5
MOVES = (32, 16, 8, 4, 2, 1)
TOP = 3
NG = H + 1

STACKS = tuple(a + b for a in ("k_", "q_") for b in ("first", "second", "stack_psum", "stack"))
ATT = ("qT_psum", "k_psum", "v_psum", "v_ready", "q_psum") + STACKS + (
       "scores", "max_ready", "maxT_psum", "maxT_ready", "scoresT", "pT_ready", "pv_done",
       "oH_ready", "heads_psum", "o_ready", "oT_psum", "oT_ready", "y_done")
LN = ("loads", "var_ready", "rstd_ready", "xn_ready", "xT_psum", "xT_ready")
GROUP_LOADS = ("first_loads", "second_loads", "third_loads")
SEMS = (["loads", *GROUP_LOADS, "stores", "transposed", "first", "evacuated", "consts",
         "step", "pool_step", "dve_core", "dve_side"]
        + ["core_" + n for n in LN + STACKS + (
            "ctxT_psum", "ctxT_ready", "k_psum", "v_psum", "v_ready", "q_psum", "q_ready",
            "offset_psum", "offset_ready", "scores", "scores_copied", "gates", "low", "diff", "shift", "shift_copied",
            "pool_shift", "table", "moved", "slope", "steps", "partial", "z_ready", "exp", "pT_psum",
            "pT_ready", "pv_done", "o_ready")]
        + ["tail_" + n for n in ("ctxT_psum", "ctxT_ready", "heads_psum", "o_ready", "oT_psum", "oT_ready", "y_done")]
        + ["ffn_" + n for n in LN[1:] + (
            "x_first", "x_second", "logits", "max_ready", "exp", "cw_ready", "cwT_psum", "cwT_ready", "init", "h1_done",
            "h3_done", "h1_ready", "u_ready", "g_ready", "tanh", "a_ready", "y_done", "acc")]
        + ["cross_" + n for n in LN[1:] + ATT]
        + ["gated_" + n for n in LN[1:] + ATT + ("norm_ready", "rnorm_ready", "q_done", "logits", "glog", "gexp",
                                                 "x_ready")])

PIECE_TIMES = [4] * (4 + 2 * NE) + [2] * 2 + 2 * ([6] * 4 + [0.5] * (H + 1) + [1.2] * (H + 1) + [5] * 3)
EARLY = 2
SLOTS = H + 3
PIECES = [0] * SLOTS
PIECE_TIMES = PIECE_TIMES[EARLY:]
for at in range(len(PIECE_TIMES)):
    PIECES[int((sum(PIECE_TIMES[:at]) + PIECE_TIMES[at] / 2) * SLOTS / sum(PIECE_TIMES))] += 1
FIRST = [(2 * n + 1) // 3 for n in PIECES]


class Kernel:
    pass


class Norm:
    pass


class Attention:

    def __init__(self, wq, wk, wv, wo, bq, bk, bv, tbo):
        self.wq, self.wk, self.wv, self.wo = wq, wk, wv, wo
        self.bq, self.bk, self.bv, self.tbo = bq, bk, bv, tbo


def zero(nc, k):
    nc.gpsimd.sem_clear(range(k.sem[SEMS[0]].num, k.sem[SEMS[-1]].num + 1))
    nc.all_engine_barrier()


def stepper(eng, sem):
    count = [0]

    def step(ins, wait=True):
        count[0] += 1
        ins.then_inc(sem, 1)
        if wait:
            eng.wait_ge(sem, count[0])
        return count[0]
    return step


def transpose_weights(nc, k, groups, small_loads=()):
    sem = k.sem
    blocks, after = [], {}
    for g, group in enumerate(groups):
        after[len(blocks)] = g
        for _, destinations, view in group:
            blocks += [(dst, view) for dst in destinations]
    with nc.Block() as block:
        @block.sync
        def _(sp):
            n = 0
            for g, group in enumerate(groups):
                for src, destinations, _ in group:
                    rows = len(destinations)
                    sp.dma_start(k.stage[:, n:n + rows, :], src.rearrange("(r p) n -> p r n", p=P))\
                        .then_inc(sem[GROUP_LOADS[g]], 16)
                    n += rows
            for dst, src in small_loads:
                sp.dma_start(dst, src).then_inc(sem["loads"], 16)
            if small_loads:
                sp.wait_ge(sem["loads"], 16 * len(small_loads))

        @block.tensor
        def _(pe):
            for n in range(len(blocks)):
                if n in after:
                    pe.wait_ge(sem[GROUP_LOADS[after[n]]], 16 * len(groups[after[n]]))
                if n >= 8:
                    pe.wait_ge(sem["evacuated"], n - 7)
                for c in range(NC):
                    last = nc.tensor.transpose(k.bank[n % 8][:, c * P:(c + 1) * P],
                                               k.stage[:, n, c * P:(c + 1) * P], k.ident[:])
                last.then_inc(sem["transposed"], 1)

        def source(n):
            src = k.bank[n % 8][:, 0:D].rearrange("p (c r) -> p c r", c=NC)
            return src.rearrange("p c (j t) -> p c t j", t=2) if blocks[n][1] == "parity" else src

        @block.scalar
        def _(act):
            for n, (dst, view) in enumerate(blocks):
                if view == "parity":
                    act.wait_ge(sem["transposed"], n + 1)
                    nc.scalar.activation(dst[0], source(n), ACT.Copy, scale=SCALE).then_inc(sem["first"], 1)

        @block.vector
        def _(dve):
            firsts = 0
            for n, (dst, view) in enumerate(blocks):
                src = source(n)
                if view == "parity":
                    firsts += 1
                    dve.wait_ge(sem["first"], firsts)
                    for par in range(2):
                        last = nc.vector.scalar_tensor_tensor(dst[1][:, :, par, :], src[:, :, par, :], SCALE,
                                                              dst[0][:, :, par, :], ALU.mult, ALU.subtract)
                    last.then_inc(sem["evacuated"], 1)
                    continue
                dve.wait_ge(sem["transposed"], n + 1)
                if view == "half":
                    nc.vector.tensor_scalar(dst, src, 0.5, None, ALU.mult).then_inc(sem["evacuated"], 1)
                else:
                    nc.vector.tensor_copy(dst, src).then_inc(sem["evacuated"], 1)
    zero(nc, k)



def norm_vector(nc, k, dve, step, n, p):
    sem = k.sem
    for t in range(NT):
        step(nc.vector.bn_stats(n.stats[:, t, :], n.x[:, t, :]))
        step(nc.vector.bn_aggr(n.mean_var[:, t, :], n.stats[:, t, :]))
    nc.vector.tensor_scalar(n.var[:], n.mean_var[:, :, 1], EPS, None, ALU.add).then_inc(sem[p + "var_ready"], 1)
    dve.wait_ge(sem[p + "rstd_ready"], 1)
    for t in range(NT):
        nc.vector.tensor_scalar(n.xn[:, t, :], n.x[:, t, :], n.mean_var[:, t, 0:1], n.rstd[:, t:t + 1],
                                ALU.subtract, ALU.mult).then_inc(sem[p + "xn_ready"], 1)


def norm_pool(nc, k, pool, n, p):
    pool.wait_ge(k.sem[p + "var_ready"], 1)
    nc.gpsimd.tensor_tensor(n.rstd[:], n.var[:], k.neghalf[:, 0:NT], ALU.pow)\
        .then_inc(k.sem[p + "rstd_ready"], 1)


def transpose_tokens(nc, k, bank, src):
    for c in range(NC):
        for t in range(NT):
            last = nc.tensor.transpose(bank[:, c * S + t * P:c * S + (t + 1) * P],
                                       src[:, t, c * P:(c + 1) * P], k.ident[:])
    return last


def whole(tile):
    return tile[:, :, :].rearrange("p a b -> p (a b)")


def feature_projection(nc, w, src, bank):
    for g in range(NC):
        for c in range(NC):
            last = nc.tensor.matmul(bank[:, g * S:(g + 1) * S], w[:, c, g * P:(g + 1) * P], src[:, c, :],
                                    start=(c == 0), stop=(c == NC - 1))
    return last


def token_projection(nc, w, src, bank):
    for t in range(NT):
        for c in range(NC):
            last = nc.tensor.matmul(bank[:, t * D:(t + 1) * D], src[:, c, t * P:(t + 1) * P], w[:, c, :],
                                    start=(c == 0), stop=(c == NC - 1))
    return last



def first_part(nc, bank, bias, parts, signal):
    for g in range(NC):
        src = bank[:, g * S:(g + 1) * S]
        if bias is None:
            ins = nc.scalar.activation(parts[:, 0, g, :], src, ACT.Copy)
        else:
            ins = nc.scalar.activation(parts[:, 0, g, :], src, ACT.Identity, bias=bias[:, g:g + 1])
        ins.then_inc(signal, 1)


def second_part(nc, bank, bias, parts, signal):
    for g in range(NC):
        src = bank[:, g * S:(g + 1) * S]
        nc.vector.scalar_tensor_tensor(parts[:, 1, g, :], src, 0.0 if bias is None else bias[:, g:g + 1],
                                       parts[:, 0, g, :], ALU.add, ALU.subtract).then_inc(signal, 1)


def stack_pair(nc, k, order, parts, m, bank):
    r = slice(HB * m, HB * (m + 1))
    for c in range(NC):
        for n in range(2):
            last = nc.tensor.matmul(bank[:, c * S:(c + 1) * S], k.select[r, order, n, :], parts[r, n, c, :],
                                    start=(n == 0), stop=(n == 1))
    return last


def copy_stacks(nc, act, m, bank, stack, done, signal):
    act.wait_ge(done, m + 1)
    nc.scalar.activation(stack[:, m::P // HB, :], bank[:].rearrange("p (c s) -> p c s", c=NC), ACT.Copy)\
        .then_inc(signal, 1)


def stack_of(h):
    pair = h % HG // 2
    return h // HG * (P // HB) + pair, slice(64 * (h % 2), 64 * (h % 2 + 1))


def scores(nc, h, queries, keys, bank):
    n, r = stack_of(h)
    for t in range(NT):
        last = nc.tensor.matmul(bank[:, t * S:(t + 1) * S], queries[r, n, t * P:(t + 1) * P], keys[r, n, :],
                                start=True, stop=True)
    return last


def out_rows(h):
    return slice(32 * (h % 4), 32 * (h % 4 + 1)), h // 4


def weigh(nc, v, width, pT, h, bank, group):
    rows, _ = out_rows(h)
    for c in range(NT):
        last = nc.tensor.matmul(bank[rows, group * S:(group + 1) * S], v[:, c, h * width:h * width + 32],
                                pT[:, c, :], start=(c == 0), stop=(c == NT - 1), tile_position=(0, 32 * (h % 4)))
    return last


def heads_to_tokens(nc, k, t, bank, src):
    for g in range(H // 4):
        last = nc.tensor.transpose(bank[:, g * P:(g + 1) * P], src[:, g, t * P:(t + 1) * P], k.ident[:])
    return last



def core_tensor(nc, k, pe, side):
    sem = k.sem
    pe.wait_ge(sem["core_loads"], 16 * 2 * NT)
    transpose_tokens(nc, k, k.bank[0], k.core_ctx).then_inc(sem["core_ctxT_psum"], 1)
    pe.wait_ge(sem["core_ctxT_ready"], 1)
    feature_projection(nc, k.wk_cope, k.core_ctxT, k.bank[2]).then_inc(sem["core_k_psum"], 1)
    token_projection(nc, k.wv_cope, k.core_ctxT, k.bank[0]).then_inc(sem["core_v_psum"], 1)
    pe.wait_ge(sem["core_xn_ready"], NT)
    transpose_tokens(nc, k, k.bank[1], k.core_norm.xn).then_inc(sem["core_xT_psum"], 1)
    pe.wait_ge(sem["core_xT_ready"], 1)
    feature_projection(nc, k.wq_cope, k.core_norm.xT, k.bank[3]).then_inc(sem["core_q_psum"], 1)
    next(side, None)
    pe.wait_ge(sem["core_q_ready"], NC)
    for t in range(NT):
        for g in range(NC):
            last = nc.tensor.matmul(k.bank[1][:, t * H + g * HG:t * H + (g + 1) * HG],
                                    k.core_qT[:, g, t * P:(t + 1) * P], k.first[:], start=True, stop=True)
    last.then_inc(sem["core_offset_psum"], 1)
    pe.wait_ge(sem["core_k_second"], NC)
    pe.wait_ge(sem["core_v_ready"], 1)
    for m in range(P // HB):
        if m >= 2:
            pe.wait_ge(sem["core_k_stack"], m - 1)
        stack_pair(nc, k, 1, k.core_k_parts, m, k.bank[2 - 2 * (m % 2)]).then_inc(sem["core_k_stack_psum"], 1)
    next(side, None)
    pe.wait_ge(sem["core_q_second"], NC)
    pe.wait_ge(sem["core_offset_ready"], 1)
    for m in range(P // HB):
        if m >= 2:
            pe.wait_ge(sem["core_q_stack"], m - 1)
        stack_pair(nc, k, 0, k.core_q_parts, m, k.bank[3 - 2 * (m % 2)]).then_inc(sem["core_q_stack_psum"], 1)

    def raw(h):
        if h == 0:
            pe.wait_ge(sem["core_k_stack"], P // HB)
            pe.wait_ge(sem["core_q_stack"], P // HB)
        else:
            pe.wait_ge(sem["core_scores_copied"], (NT + 1) * h)
        scores(nc, h, k.core_queries, k.core_keys, k.bank[0]).then_inc(sem["core_scores"], 1)

    def table(h):
        if h >= 1:
            pe.wait_ge(sem["core_slope"], h)
        n, r = stack_of(h)
        for t in range(NT):
            last = nc.tensor.matmul(k.bank[1][:, t * S:(t + 1) * S], k.core_queries[r, n, t * P:(t + 1) * P],
                                    k.table[r, :], start=True, stop=True)
        last.then_inc(sem["core_table"], 1)

    raw(0)
    table(0)
    raw(1)
    for s in range(H + 3):
        for _ in range(FIRST[s]):
            next(side, None)
        h = s - 2
        if 0 <= h < H:
            pe.wait_ge(sem["core_exp"], NT * (h + 1))
            if h >= 1:
                pe.wait_ge(sem["core_pT_ready"], h)
            transpose_tokens(nc, k, k.bank[2], k.core_prob).then_inc(sem["core_pT_psum"], 1)
        for _ in range(PIECES[s] - FIRST[s]):
            next(side, None)
        h = s - 3
        if 0 <= h < H:
            pe.wait_ge(sem["core_pT_ready"], h + 1)
            group = out_rows(h)[1]
            if group >= 2 and h % 4 == 0:
                pe.wait_ge(sem["core_o_ready"], group - 1)
            weigh(nc, k.core_v, HD, k.core_pT[:, h % 2], h, k.bank[3], group % 2).then_inc(sem["core_pv_done"], 1)
        if s + 2 < H:
            raw(s + 2)
        if s + 1 < H:
            table(s + 1)


def core_scalar(nc, k, act, side):
    sem = k.sem
    act.wait_ge(sem["core_ctxT_psum"], 1)
    nc.scalar.activation(whole(k.core_ctxT), k.bank[0][:], ACT.Copy).then_inc(sem["core_ctxT_ready"], 1)
    act.wait_ge(sem["core_k_psum"], 1)
    first_part(nc, k.bank[2], k.bk_cope, k.core_k_parts, sem["core_k_first"])
    act.wait_ge(sem["core_xT_psum"], 1)
    nc.scalar.activation(whole(k.core_norm.xT), k.bank[1][:], ACT.Copy).then_inc(sem["core_xT_ready"], 1)
    act.wait_ge(sem["core_q_psum"], 1)
    for g in range(NC):
        nc.scalar.activation(k.core_qT[:, g, :], k.bank[3][:, g * S:(g + 1) * S], ACT.Identity,
                             bias=k.bq_cope[:, g:g + 1]).then_inc(sem["core_q_ready"], 1)
    first_part(nc, k.bank[3], k.bq_cope, k.core_q_parts, sem["core_q_first"])
    next(side, None)
    act.wait_ge(sem["core_offset_psum"], 1)
    nc.scalar.activation(k.core_offset[:], k.bank[1][:, 0:NT * H], ACT.Copy).then_inc(sem["core_offset_ready"], 1)
    act.wait_ge(sem["core_offset_ready"], 1)
    for m in range(P // HB):
        copy_stacks(nc, act, m, k.bank[2 - 2 * (m % 2)], k.core_keys, sem["core_k_stack_psum"],
                    sem["core_k_stack"])
    next(side, None)
    for m in range(P // HB):
        copy_stacks(nc, act, m, k.bank[3 - 2 * (m % 2)], k.core_queries, sem["core_q_stack_psum"],
                    sem["core_q_stack"])

    def gates(h):
        act.wait_ge(sem["core_scores"], h + 1)
        if h >= 1:
            act.wait_ge(sem["core_low"], h)
            act.wait_ge(sem["core_gates"], h)
        gate = k.gate[:, :, 0:S]
        nc.scalar.activation(gate, k.bank[0][:].rearrange("p (t s) -> p t s", t=NT), ACT.Tanh,
                             scale=-0.5 * INV_SQRT_HD).then_inc(sem["core_scores_copied"], 1)
        act.wait_ge(sem["core_scores_copied"], (NT + 1) * h + 1)
        nc.scalar.activation(gate, gate, ACT.Identity, scale=0.5, bias=k.half[:]).then_inc(sem["core_gates"], 1)

    def keep_scores(h):
        if h >= 2:
            act.wait_ge(sem["core_partial"], h - 1)
        for t in range(NT):
            nc.scalar.activation(k.core_scores[:, h % 2, t, :], k.bank[0][:, t * S:(t + 1) * S], ACT.Identity,
                                 bias=k.core_offset[:, t * H + h:t * H + h + 1])\
                .then_inc(sem["core_scores_copied"], 1)

    gates(0)
    keep_scores(0)
    for s in range(H + 3):
        if s < H:
            act.wait_ge(sem["core_shift"], s + 1)
            if s >= 1:
                act.wait_ge(sem["core_pool_shift"], 3 * s)
            nc.scalar.activation(k.shift16[:], k.shift[:], ACT.Copy).then_inc(sem["core_shift_copied"], 1)
        h = s - 2
        if 0 <= h < H:
            act.wait_ge(sem["core_z_ready"], h + 1)
            if h >= 1:
                act.wait_ge(sem["core_pT_psum"], h)
            for t in range(NT):
                nc.scalar.activation(k.core_prob[:, t, :], k.z[:, h % 2, t, :], ACT.Exp,
                                     bias=k.negmax[:, h % 2, t:t + 1], scale=INV_SQRT_HD,
                                     accum_out=k.core_sums[:, t, h:h + 1]).then_inc(sem["core_exp"], 1)
        for _ in range(FIRST[s]):
            next(side, None)
        if s + 1 < H:
            gates(s + 1)
            keep_scores(s + 1)
        if 0 <= h < H:
            act.wait_ge(sem["core_pT_psum"], h + 1)
            if h >= 2:
                act.wait_ge(sem["core_pv_done"], h - 1)
            nc.scalar.activation(whole(k.core_pT[:, h % 2]), k.bank[2][:], ACT.Copy)\
                .then_inc(sem["core_pT_ready"], 1)
        for _ in range(PIECES[s] - FIRST[s]):
            next(side, None)
        h = s - 3
        if h >= 0 and h % 4 == 3:
            act.wait_ge(sem["core_pv_done"], h + 1)
            g = h // 4
            nc.scalar.activation(k.core_oH[:, g, :], k.bank[3][:, g % 2 * S:(g % 2 + 1) * S], ACT.Copy)\
                .then_inc(sem["core_o_ready"], 1)
        if s < H:
            act.wait_ge(sem["core_moved"], s + 1)
            if s >= 1:
                act.wait_ge(sem["core_steps"], 2 * s)
            nc.scalar.activation(whole(k.slope), k.bank[1][:], ACT.Copy).then_inc(sem["core_slope"], 1)


def core_pool(nc, k, pool, side):
    sem = k.sem
    norm_pool(nc, k, pool, k.core_norm, "core_")
    next(side, None)
    next(side, None)

    def diff(h):
        pool.wait_ge(sem["core_low"], h + 1)
        nc.gpsimd.tensor_tensor(k.diff[:], k.c[:, :, 0:S], k.low[:], ALU.subtract)\
            .then_inc(sem["core_diff"], 1)

    diff(0)
    for s in range(H + 3):
        if s < H:
            b = s % 2
            pool.wait_ge(sem["core_shift_copied"], s + 1)
            nc.gpsimd.tensor_tensor(k.minus_u[:], k.shift16[:], k.t_row[:].unsqueeze(1)
                                    .broadcast_to([P, NT, S + 1]), ALU.subtract).then_inc(sem["core_pool_shift"], 1)
            nc.gpsimd.tensor_tensor(k.neg_rest[:], k.shift16[:, :, 0:S], k.c[:, :, 0:S], ALU.subtract)\
                .then_inc(sem["core_pool_shift"], 1)
            pool.wait_ge(sem["core_pool_shift"], 3 * s + 2)
            nc.gpsimd.tensor_tensor(k.rises[:], k.minus_u[:, :, 1:S + 1], k.minus_u[:, :, 0:S], ALU.subtract)\
                .then_inc(sem["core_pool_shift"], 1)
            pool.wait_ge(sem["core_pool_shift"], 3 * s + 3)
        for _ in range(PIECES[s]):
            next(side, None)
        if s + 1 < H:
            diff(s + 1)
        if s < H:
            pool.wait_ge(sem["core_slope"], s + 1)
            if s >= 1:
                pool.wait_ge(sem["core_z_ready"], s)
            nc.gpsimd.tensor_tensor(k.steps[:], k.slope[:], k.rises[:], ALU.mult).then_inc(sem["core_steps"], 1)
            nc.gpsimd.tensor_tensor(k.partial[:], k.slope[:], k.neg_rest[:], ALU.mult).then_inc(sem["core_steps"], 1)
            pool.wait_ge(sem["core_steps"], 2 * s + 2)
            nc.gpsimd.tensor_tensor(k.partial[:], k.partial[:], k.core_scores[:, b], ALU.add)\
                .then_inc(sem["core_partial"], 1)
            pool.wait_ge(sem["core_partial"], s + 1)


def core_vector(nc, k, dve, step, side):
    sem = k.sem
    dve.wait_ge(sem["core_loads"], 16 * 2 * NT)
    norm_vector(nc, k, dve, step, k.core_norm, "core_")
    dve.wait_ge(sem["core_v_psum"], 1)
    nc.vector.tensor_copy(k.core_v[:, :, 0:D], k.bank[0][:].rearrange("p (t n) -> p t n", t=NT))\
        .then_inc(sem["core_v_ready"], 1)
    dve.wait_ge(sem["core_k_first"], NC)
    second_part(nc, k.bank[2], k.bk_cope, k.core_k_parts, sem["core_k_second"])
    dve.wait_ge(sem["core_q_first"], NC)
    second_part(nc, k.bank[3], k.bq_cope, k.core_q_parts, sem["core_q_second"])
    next(side, None)
    next(side, None)
    flat = "p t s -> p (t s)"

    def scan(h):
        dve.wait_ge(sem["core_gates"], h + 1)
        if h >= 1:
            dve.wait_ge(sem["core_pool_shift"], 3 * h - 1)
        step(nc.vector.tensor_tensor_scan(
            k.c[:].rearrange(flat)[:, ::-1], k.gate[:].rearrange(flat)[:, ::-1],
            k.cap[:].rearrange(flat)[:, ::-1], 0.0, ALU.add, ALU.max))
        nc.vector.tensor_scalar(k.low[:], k.c[:, :, 0:S], ROUND, ROUND + 1.0, ALU.add, ALU.subtract)\
            .then_inc(sem["core_low"], 1)

    def some_pieces(s, n):
        for _ in range((n + 1) * PIECES[s] // len(MOVES) - n * PIECES[s] // len(MOVES)):
            next(side, None)

    tab = k.bank[1][:].rearrange("p (t s) -> p t s", t=NT)
    scan(0)
    for s in range(H + 3):
        if s < H:
            dve.wait_ge(sem["core_diff"], s + 1)
            if s >= 1:
                dve.wait_ge(sem["core_shift_copied"], s)
            nc.vector.scalar_tensor_tensor(k.shift[:, :, 0:S], k.diff[:], 1.0, k.low[:], ALU.is_gt,
                                           ALU.add).then_inc(sem["core_shift"], 1)
            dve.wait_ge(sem["core_shift"], s + 1)
            masked = {}

            def mask(n):
                masked[n] = step(nc.vector.tensor_scalar(k.mask[n % 3], k.shift[:, :, 0:S], MOVES[n], None,
                                                         ALU.bitwise_and), wait=False)

            mask(0)
            for n, b in enumerate(MOVES):
                if n + 1 < len(MOVES):
                    mask(n + 1)
                if n == 0:
                    dve.wait_ge(sem["core_table"], s + 1)
                    dve.wait_ge(sem["dve_core"], masked[0])
                else:
                    dve.wait_ge(sem["dve_core"], moved)
                move = nc.vector.copy_predicated(tab[:, :, 0:S - b], k.mask[n % 3][:, :, 0:S - b], tab[:, :, b:S])
                if b > 1:
                    moved = step(move, wait=False)
                    some_pieces(s, n)
                else:
                    move.then_inc(sem["core_moved"], 1)
        else:
            for n in range(len(MOVES) - 1):
                some_pieces(s, n)
        if s + 1 < H:
            scan(s + 1)
        some_pieces(s, len(MOVES) - 1)
        h = s - 1
        if 0 <= h < H:
            dve.wait_ge(sem["core_steps"], 2 * h + 1)
            if h >= 2:
                dve.wait_ge(sem["core_exp"], NT * (h - 1))
            summed = [step(nc.vector.tensor_tensor_scan(k.z[:, h % 2, t, ::-1], k.steps[:, t, ::-1],
                                                        k.steps[:, t, ::-1], 0.0, ALU.add, ALU.bypass),
                           wait=False) for t in range(NT)]
            dve.wait_ge(sem["core_partial"], h + 1)
            for t in range(NT):
                dve.wait_ge(sem["dve_core"], summed[t])
                largest = step(nc.vector.tensor_tensor_reduce(
                    out=k.z[:, h % 2, t, :], in0=k.z[:, h % 2, t, :], in1=k.partial[:, t, :], scale=1.0,
                    scalar=-3e38, op0=ALU.add, op1=ALU.max, accum_out=k.rowmax[:, t:t + 1]), wait=False)
            dve.wait_ge(sem["dve_core"], largest)
            nc.vector.tensor_scalar(k.negmax[:, h % 2], k.rowmax[:], -INV_SQRT_HD, None, ALU.mult)\
                .then_inc(sem["core_z_ready"], 1)
            dve.wait_ge(sem["core_z_ready"], h + 1)


def core_tail(nc, k, dve, step):
    dve.wait_ge(k.sem["core_exp"], NT * H)
    step(nc.vector.reciprocal(k.core_rsum[:], k.core_sums[:]))



def side_tensor(nc, k, pe):
    sem = k.sem
    n = k.norm
    pe.wait_ge(sem["loads"], 16 * 2 * NT)
    transpose_tokens(nc, k, k.bank[4], k.ctx).then_inc(sem["tail_ctxT_psum"], 1)
    for t in range(NT):
        heads_to_tokens(nc, k, t, k.bank[6 + t], k.core_oH).then_inc(sem["tail_heads_psum"], 1)
    yield
    pe.wait_ge(sem["tail_o_ready"], NT)
    transpose_tokens(nc, k, k.bank[5], k.o).then_inc(sem["tail_oT_psum"], 1)
    pe.wait_ge(sem["tail_oT_ready"], 1)
    token_projection(nc, k.wo_cope, k.oT, k.bank[6]).then_inc(sem["tail_y_done"], 1)
    yield
    yield
    pe.wait_ge(sem["ffn_xn_ready"], NT)
    pe.wait_ge(sem["tail_ctxT_ready"], 1)
    transpose_tokens(nc, k, k.bank[4], n.xn).then_inc(sem["ffn_xT_psum"], 1)
    pe.wait_ge(sem["ffn_xT_ready"], 1)
    for t in range(NT):
        for c in range(NC):
            last = nc.tensor.matmul(k.bank[7][:, t * E:(t + 1) * E], n.xT[:, c, t * P:(t + 1) * P],
                                    k.wgate[:, c, :], start=(c == 0), stop=(c == NC - 1))
    last.then_inc(sem["ffn_logits"], 1)

    products = [(c, a, b) for c in range(NC) for a, b in ((0, 0), (0, 1), (1, 0))]

    def up(m):
        e, par = divmod(m, 2)
        if m == 0:
            pe.wait_ge(sem["ffn_x_second"], NC)
        for w, bank, signal in ((k.w1, 4, "ffn_h1_done"), (k.w3, 5 + m % 2, "ffn_h3_done")):
            if bank == 4 and m >= 1:
                pe.wait_ge(sem["ffn_h1_ready"], 2 * m)
            if bank != 4 and m >= 2:
                pe.wait_ge(sem["ffn_u_ready"], 2 * (m - 1))
            for f in range(2):
                for n, (c, a, b) in enumerate(products):
                    last = nc.tensor.matmul(k.bank[bank][:, f * S:(f + 1) * S],
                                            w[:, e, a, c, par, f * P:(f + 1) * P], k.x_parts[:, b, c, :],
                                            start=(n == 0), stop=(n == len(products) - 1))
            last.then_inc(sem[signal], 1)

    def down(e):
        pe.wait_ge(sem["ffn_a_ready"], e + 1)
        if e == 0:
            pe.wait_ge(sem["ffn_init"], 2)
        else:
            pe.wait_ge(sem["ffn_acc"], 2 * e)
        for t in range(NT):
            for f in range(2):
                last = nc.tensor.matmul(k.bank[7][:, t * D:(t + 1) * D], k.a[:, e % 2, f, t * P:(t + 1) * P],
                                        k.w2[:, e, f, :], start=(f == 0), stop=(f == 1))
        last.then_inc(sem["ffn_y_done"], 1)

    yield
    up(0)
    yield
    up(1)
    pe.wait_ge(sem["ffn_cw_ready"], 1)
    for t in range(NT):
        last = nc.tensor.transpose(k.bank[7][0:NE, t * P:(t + 1) * P], k.cw[:, t, :], k.ident[:])
    last.then_inc(sem["ffn_cwT_psum"], 1)
    yield
    up(2)
    pe.wait_ge(sem["ffn_cwT_ready"], 1)
    for t in range(NT):
        last = nc.tensor.matmul(k.bank[7][:, t * D:(t + 1) * D], k.cwT[0:NE, t * P:(t + 1) * P],
                                k.b2[0:NE, :], start=True, stop=True)
    last.then_inc(sem["ffn_init"], 1)
    yield
    up(3)
    down(0)
    yield
    for e in range(2, NE):
        up(2 * e)
        yield
        up(2 * e + 1)
        down(e - 1)
        yield
    down(NE - 1)
    yield
    yield
    yield from attention_tensor(nc, k, pe, "cross")
    yield from attention_tensor(nc, k, pe, "gated")


def side_scalar(nc, k, act):
    sem = k.sem
    n = k.norm
    act.wait_ge(sem["tail_ctxT_psum"], 1)
    nc.scalar.activation(whole(k.ctxT), k.bank[4][:], ACT.Copy).then_inc(sem["tail_ctxT_ready"], 1)
    yield
    act.wait_ge(sem["tail_oT_psum"], 1)
    nc.scalar.activation(whole(k.oT), k.bank[5][:], ACT.Copy).then_inc(sem["tail_oT_ready"], 1)
    yield
    yield
    act.wait_ge(sem["ffn_xT_psum"], 1)
    nc.scalar.activation(whole(n.xT), k.bank[4][:], ACT.Copy).then_inc(sem["ffn_xT_ready"], 1)
    first_part(nc, k.bank[4], None, k.x_parts, sem["ffn_x_first"])
    yield

    def first_linear(m):
        e, par = divmod(m, 2)
        act.wait_ge(sem["ffn_h1_done"], m + 1)
        if m >= 2:
            act.wait_ge(sem["ffn_u_ready"], 2 * (m - 1))
        for f in range(2):
            nc.scalar.activation(k.h1[:, m % 2, f, :], k.bank[4][:, f * S:(f + 1) * S], ACT.Identity,
                                 bias=k.b1[:, par, f, e:e + 1], scale=SCALE ** -2)\
                .then_inc(sem["ffn_h1_ready"], 1)

    act.wait_ge(sem["ffn_max_ready"], 1)
    for t in range(NT):
        nc.scalar.activation(k.escore[:, t, :], k.bank[7][:, t * E:(t + 1) * E], ACT.Exp,
                             bias=k.enegmax[:, t:t + 1], accum_out=k.esum[:, t:t + 1])\
            .then_inc(sem["ffn_exp"], 1)
    first_linear(0)
    yield
    for e in range(NE):
        if e >= 1:
            first_linear(2 * e)
            if e == 1:
                act.wait_ge(sem["ffn_cwT_psum"], 1)
                nc.scalar.activation(k.cwT[0:NE, :], k.bank[7][0:NE, 0:S], ACT.Copy)\
                    .then_inc(sem["ffn_cwT_ready"], 1)
            yield
        act.wait_ge(sem["ffn_g_ready"], e + 1)
        nc.scalar.activation(k.eth, k.eg, ACT.Tanh, scale=0.5 * ALPHA).then_inc(sem["ffn_tanh"], 1)
        first_linear(2 * e + 1)
        yield
    yield
    yield
    yield from attention_scalar(nc, k, act, "cross")
    yield from attention_scalar(nc, k, act, "gated")


def side_pool(nc, k, pool):
    yield
    yield
    norm_pool(nc, k, pool, k.norm, "ffn_")
    for _ in range(2 + 2 * NE + 2):
        yield
    for kind in ("cross", "gated"):
        p = kind + "_"
        norm_pool(nc, k, pool, k.norm, p)
        yield
        if kind == "gated":
            pool.wait_ge(k.sem[p + "norm_ready"], 1)
            nc.gpsimd.tensor_tensor(k.rnorm[:], k.sumsq[:], k.neghalf[:], ALU.pow)\
                .then_inc(k.sem[p + "rnorm_ready"], 1)
        for _ in range(3 + 2 * H + 5):
            yield


def side_vector(nc, k, dve):
    sem = k.sem
    step = stepper(dve, sem["dve_side"])
    for t in range(NT):
        dve.wait_ge(sem["tail_heads_psum"], t + 1)
        head = k.bank[6 + t][:].rearrange("p (h d) -> p h d", h=H)
        nc.vector.tensor_tensor(k.o[:, t, :].rearrange("p (h d) -> p h d", d=HD), head[:, :, 0:HD],
                                k.core_rsum[:, t, :].unsqueeze(2).broadcast_to([P, H, HD]), ALU.mult)\
            .then_inc(sem["tail_o_ready"], 1)
    yield
    dve.wait_ge(sem["tail_y_done"], 1)
    add_to_x(nc, k, step, k.bank[6], k.tanh_g[:, 0:1], k.bo_cope)
    yield
    norm_vector(nc, k, dve, step, k.norm, "ffn_")
    yield
    dve.wait_ge(sem["ffn_x_first"], NC)
    second_part(nc, k.bank[4], None, k.x_parts, sem["ffn_x_second"])
    yield
    dve.wait_ge(sem["ffn_logits"], 1)
    logits = k.bank[7][:, 0:NT * E].rearrange("p (t e) -> p t e", t=NT)
    nc.vector.tensor_reduce(k.enegmax[:], logits, axis=AX.X, op=ALU.max, negate=True)\
        .then_inc(sem["ffn_max_ready"], 1)

    def hidden(m):
        e, par = divmod(m, 2)
        dve.wait_ge(sem["ffn_h3_done"], m + 1)
        for f in range(2):
            dve.wait_ge(sem["ffn_h1_ready"], 2 * m + f + 1)
            nc.vector.scalar_tensor_tensor(k.u[:, par, f, :], k.bank[5 + m % 2][:, f * S:(f + 1) * S],
                                           k.b3[:, par, f, e:e + 1], k.h1[:, m % 2, f, :],
                                           ALU.add, ALU.mult).then_inc(sem["ffn_u_ready"], 1)
        dve.wait_ge(sem["ffn_u_ready"], 2 * m + 2)

    both = "p f s -> p (f s)"

    def gate_part(e):
        hidden(2 * e)
        if e >= 1:
            dve.wait_ge(sem["ffn_a_ready"], e)
        nc.vector.tensor_scalar(k.eg, k.u[:, 0].rearrange(both), LIMIT, None, ALU.min)\
            .then_inc(sem["ffn_g_ready"], 1)

    def linear_part(e):
        hidden(2 * e + 1)
        step(nc.vector.tensor_scalar(k.el, k.u[:, 1].rearrange(both), -LIMIT, LIMIT, ALU.max, ALU.min), wait=False)
        dve.wait_ge(sem["ffn_tanh"], e + 1)
        step(nc.vector.scalar_tensor_tensor(k.eg, k.eth, 1.0, k.eg, ALU.add, ALU.mult))
        if e >= 2:
            dve.wait_ge(sem["ffn_y_done"], e - 1)
        nc.vector.scalar_tensor_tensor(k.a[:, e % 2].rearrange(both), k.el, 1.0, k.eg,
                                       ALU.add, ALU.mult).then_inc(sem["ffn_a_ready"], 1)

    def accumulate(e):
        dve.wait_ge(sem["ffn_y_done"], e + 1)
        for t in range(NT):
            nc.vector.scalar_tensor_tensor(k.acc[:, t, :], k.bank[7][:, t * D:(t + 1) * D],
                                           k.cw[:, t, e:e + 1], k.acc[:, t, :], ALU.mult, ALU.add)\
                .then_inc(sem["ffn_acc"], 1)
        dve.wait_ge(sem["ffn_acc"], 2 * e + 2)

    dve.wait_ge(sem["ffn_exp"], NT)
    step(nc.vector.reciprocal(k.esum[:], k.esum[:]))
    step(nc.vector.tensor_tensor(k.escore[:], k.escore[:],
                                 k.esum[:].unsqueeze(2).broadcast_to([P, NT, E]), ALU.mult))
    step(nc.vector.tensor_tensor(k.ebiased[:], k.escore[:],
                                 k.gate_b[:].unsqueeze(1).broadcast_to([P, NT, E]), ALU.add))
    for t in range(NT):
        step(nc.vector.max(k.etop[:, t, :], k.ebiased[:, t, :]))
        step(nc.vector.max_index(k.eidx[:, t, :], k.etop[:, t, :], k.ebiased[:, t, :]))
        step(nc.vector.tensor_copy(k.eidxf[:, t, :], k.eidx[:, t, :]))
        step(nc.vector.tensor_scalar(k.ehot[:], k.expert_no[:], k.eidxf[:, t, 1:2], None, ALU.is_equal))
        step(nc.vector.scalar_tensor_tensor(k.ehot[:], k.expert_no[:], k.eidxf[:, t, 0:1], k.ehot[:],
                                            ALU.is_equal, ALU.add))
        last = nc.vector.tensor_tensor(k.cw[:, t, 0:E], k.escore[:, t, :], k.ehot[:], ALU.mult)
        if t < NT - 1:
            step(last)
    last.then_inc(sem["ffn_cw_ready"], 1)
    gate_part(0)
    yield
    linear_part(0)
    yield
    gate_part(1)
    dve.wait_ge(sem["ffn_init"], 1)
    nc.vector.tensor_copy(whole(k.acc), k.bank[7][:]).then_inc(sem["ffn_init"], 1)
    dve.wait_ge(sem["ffn_init"], 2)
    yield
    linear_part(1)
    accumulate(0)
    yield
    for e in range(2, NE):
        gate_part(e)
        yield
        linear_part(e)
        accumulate(e - 1)
        yield
    accumulate(NE - 1)
    step(nc.vector.scalar_tensor_tensor(whole(k.norm.x), whole(k.acc), k.tanh_g[:, 2:3], whole(k.norm.x),
                                        ALU.mult, ALU.add))
    yield
    yield
    yield from attention_vector(nc, k, dve, step, "cross")
    yield from attention_vector(nc, k, dve, step, "gated")


def add_to_x(nc, k, step, bank, scale, bias_row):
    x = k.norm.x
    step(nc.vector.scalar_tensor_tensor(whole(x), bank[:], scale, whole(x), ALU.mult, ALU.add))
    step(nc.vector.tensor_tensor(x[:], x[:], bias_row[:].unsqueeze(1).broadcast_to([P, NT, D]), ALU.add))



def attention_tensor(nc, k, pe, kind):
    sem = k.sem
    p = kind + "_"
    w = k.att[kind]
    n = k.norm
    def keys_and_values(src):
        feature_projection(nc, w.wk, src, k.bank[5]).then_inc(sem[p + "k_psum"], 1)
        token_projection(nc, w.wv, src, k.bank[6]).then_inc(sem[p + "v_psum"], 1)

    if kind == "cross":
        keys_and_values(k.ctxT)
    pe.wait_ge(sem[p + "xn_ready"], NT)
    transpose_tokens(nc, k, k.bank[4], n.xn).then_inc(sem[p + "xT_psum"], 1)
    yield
    pe.wait_ge(sem[p + "xT_ready"], 1)
    if kind == "gated":
        token_projection(nc, w.wq, n.xT, k.bank[7]).then_inc(sem[p + "q_psum"], 1)
        keys_and_values(n.xT)
    else:
        feature_projection(nc, w.wq, n.xT, k.bank[7]).then_inc(sem[p + "q_psum"], 1)
    yield
    pe.wait_ge(sem[p + "k_second"], NC)
    pe.wait_ge(sem[p + "v_ready"], 1)
    for m in range(P // HB):
        if m >= 2:
            pe.wait_ge(sem[p + "k_stack"], m - 1)
        stack_pair(nc, k, 1, k.k_parts, m, k.bank[5 + m % 2]).then_inc(sem[p + "k_stack_psum"], 1)
    if kind == "gated":
        pe.wait_ge(sem[p + "q_done"], 1)
        transpose_tokens(nc, k, k.bank[4], k.qn).then_inc(sem[p + "qT_psum"], 1)
    yield
    pe.wait_ge(sem[p + "q_second"], NC)
    for m in range(P // HB):
        if m >= 2:
            pe.wait_ge(sem[p + "q_stack"], m - 1)
        stack_pair(nc, k, 0, k.q_parts, m, k.bank[7 - 3 * (m % 2)]).then_inc(sem[p + "q_stack_psum"], 1)
    yield
    pe.wait_ge(sem[p + "k_stack"], P // HB)
    pe.wait_ge(sem[p + "q_stack"], P // HB)
    for h in range(H):
        if h >= 2:
            pe.wait_ge(sem[p + "max_ready"], h - 1)
        scores(nc, h, k.queries, k.keys, k.bank[6 + h % 2]).then_inc(sem[p + "scores"], 1)
        yield
    pe.wait_ge(sem[p + "max_ready"], H + 1)
    maxT = k.bank[6].bitcast(BF16)
    for t in range(NT):
        last = nc.tensor.transpose(maxT[:, t * P:(t + 1) * P],
                                   k.max_parts[:, t].rearrange("p r m h -> p (r m h)"), k.ident16[:])
    last.then_inc(sem[p + "maxT_psum"], 1)
    yield

    def weigh_values(h):
        pe.wait_ge(sem[p + "pT_ready"], h + 1)
        group = out_rows(h)[1]
        weigh(nc, k.v, HD + 1, k.pT[:, h % 2], h, k.bank[4 + group // 2], group % 2)\
            .then_inc(sem[p + "pv_done"], 1)

    pe.wait_ge(sem[p + "maxT_ready"], 1)
    for h in range(H):
        if h >= 2:
            pe.wait_ge(sem[p + "pT_ready"], h - 1)
        n, r = stack_of(h)
        for c in range(NT):
            out = k.bank[6 + h % 2][:, c * S:(c + 1) * S]
            nc.tensor.matmul(out, k.keys[r, n, c * P:(c + 1) * P], k.queries[r, n, :], start=True, stop=False)
            last = nc.tensor.matmul(out, k.pick[r, h:h + 1].broadcast_to([64, P]), k.maxT[r, :],
                                    start=False, stop=True)
        last.then_inc(sem[p + "scoresT"], 1)
        if h >= 1:
            weigh_values(h - 1)
        yield
    weigh_values(H - 1)
    yield
    pe.wait_ge(sem[p + "oH_ready"], 2)
    for t in range(NT):
        heads_to_tokens(nc, k, t, k.bank[6 + t], k.oH).then_inc(sem[p + "heads_psum"], 1)
    yield
    pe.wait_ge(sem[p + "o_ready"], NT)
    transpose_tokens(nc, k, k.bank[4], k.o).then_inc(sem[p + "oT_psum"], 1)
    pe.wait_ge(sem[p + "oT_ready"], 1)
    if kind == "gated":
        for t in range(NT):
            for c in range(NC):
                last = nc.tensor.matmul(k.bank[5][:, t * NG:(t + 1) * NG], k.oT[:, c, t * P:(t + 1) * P],
                                        k.wrs[:, c, :], start=(c == 0), stop=(c == NC - 1))
        last.then_inc(sem[p + "logits"], 1)
    token_projection(nc, w.wo, k.oT, k.bank[7]).then_inc(sem[p + "y_done"], 1)
    yield
    yield


def attention_scalar(nc, k, act, kind):
    sem = k.sem
    p = kind + "_"
    w = k.att[kind]
    def keys():
        act.wait_ge(sem[p + "k_psum"], 1)
        first_part(nc, k.bank[5], w.bk, k.k_parts, sem[p + "k_first"])

    if kind == "cross":
        keys()
    act.wait_ge(sem[p + "xT_psum"], 1)
    nc.scalar.activation(whole(k.norm.xT), k.bank[4][:], ACT.Copy).then_inc(sem[p + "xT_ready"], 1)
    yield
    if kind == "gated":
        keys()
    else:
        act.wait_ge(sem[p + "q_psum"], 1)
        first_part(nc, k.bank[7], w.bq, k.q_parts, sem[p + "q_first"])
    yield
    for m in range(P // HB):
        copy_stacks(nc, act, m, k.bank[5 + m % 2], k.keys, sem[p + "k_stack_psum"], sem[p + "k_stack"])
    if kind == "gated":
        act.wait_ge(sem[p + "qT_psum"], 1)
        first_part(nc, k.bank[4], None, k.q_parts, sem[p + "q_first"])
    yield
    for m in range(P // HB):
        copy_stacks(nc, act, m, k.bank[7 - 3 * (m % 2)], k.queries, sem[p + "q_stack_psum"],
                    sem[p + "q_stack"])
    yield
    for h in range(H):
        yield
    act.wait_ge(sem[p + "maxT_psum"], 1)
    nc.scalar.activation(k.maxT[:], k.bank[6].bitcast(BF16)[:, 0:S], ACT.Copy)\
        .then_inc(sem[p + "maxT_ready"], 1)
    yield
    for h in range(H):
        act.wait_ge(sem[p + "scoresT"], h + 1)
        if h >= 2:
            act.wait_ge(sem[p + "pv_done"], h - 1)
        nc.scalar.activation(whole(k.pT[:, h % 2]), k.bank[6 + h % 2][:], ACT.Exp, scale=INV_SQRT_HD)\
            .then_inc(sem[p + "pT_ready"], 1)
        yield
    for n in range(2):
        act.wait_ge(sem[p + "pv_done"], (n + 1) * H // 2)
        nc.scalar.activation(whole(k.oH[:, 2 * n:2 * n + 2]), k.bank[4 + n][:], ACT.Copy)\
            .then_inc(sem[p + "oH_ready"], 1)
    yield
    yield
    act.wait_ge(sem[p + "oT_psum"], 1)
    nc.scalar.activation(whole(k.oT), k.bank[4][:], ACT.Copy).then_inc(sem[p + "oT_ready"], 1)
    if kind == "gated":
        act.wait_ge(sem[p + "glog"], 1)
        nc.scalar.activation(whole(k.gexp), whole(k.glog), ACT.Exp).then_inc(sem[p + "gexp"], 1)
    yield
    yield


def attention_vector(nc, k, dve, step, kind):
    sem = k.sem
    p = kind + "_"
    w = k.att[kind]
    norm_vector(nc, k, dve, step, k.norm, p)
    yield
    if kind == "gated":
        dve.wait_ge(sem[p + "q_psum"], 1)
        q = whole(k.qn)
        step(nc.vector.tensor_tensor(k.qn, k.bank[7][:].rearrange("p (t n) -> p t n", t=NT),
                                     w.bq[:].unsqueeze(1).broadcast_to([P, NT, D]), ALU.add))
        step(nc.vector.tensor_tensor(whole(k.qsq), q, q, ALU.mult))
        nc.vector.tensor_reduce(k.sumsq[:], whole(k.qsq).rearrange("p (m d) -> p m d", d=HD),
                                axis=AX.X, op=ALU.add).then_inc(sem[p + "norm_ready"], 1)
    dve.wait_ge(sem[p + "k_first"], NC)
    second_part(nc, k.bank[5], w.bk, k.k_parts, sem[p + "k_second"])
    dve.wait_ge(sem[p + "v_psum"], 1)
    v = k.bank[6][:].rearrange("p (t h d) -> p t h d", t=NT, h=H)
    if kind == "gated":
        last = nc.vector.tensor_tensor(k.v_heads, v, w.bv[:].rearrange("p (h d) -> p h d", h=H).unsqueeze(1)
                                       .broadcast_to([P, NT, H, HD]), ALU.add)
    else:
        last = nc.vector.tensor_copy(k.v_heads, v)
    last.then_inc(sem[p + "v_ready"], 1)
    if kind == "cross":
        dve.wait_ge(sem[p + "q_first"], NC)
        second_part(nc, k.bank[7], w.bq, k.q_parts, sem[p + "q_second"])
    yield
    if kind == "gated":
        heads = k.qn.rearrange("p t (h d) -> p (t h) d", d=HD)
        dve.wait_ge(sem[p + "rnorm_ready"], 1)
        step(nc.vector.tensor_tensor(heads, heads, k.rnorm[:].unsqueeze(2).broadcast_to([P, NT * H, HD]),
                                     ALU.mult))
        step(nc.vector.tensor_tensor(k.qn, k.qn, k.qe_row[:].unsqueeze(1).broadcast_to([P, NT, D]), ALU.add))
        nc.vector.tensor_tensor(k.qn.rearrange("p t (h d) -> p t h d", d=HD),
                                k.qn.rearrange("p t (h d) -> p t h d", d=HD),
                                k.temp_row[:].unsqueeze(2).unsqueeze(1).broadcast_to([P, NT, H, HD]),
                                ALU.mult).then_inc(sem[p + "q_done"], 1)
        dve.wait_ge(sem[p + "q_first"], NC)
        second_part(nc, k.bank[4], None, k.q_parts, sem[p + "q_second"])
    yield
    yield
    for h in range(H):
        dve.wait_ge(sem[p + "scores"], h + 1)
        nc.vector.tensor_reduce(k.row_negmax[:, :, h], k.bank[6 + h % 2][:].rearrange("p (t s) -> p t s", t=NT),
                                axis=AX.X, op=ALU.max, negate=True).then_inc(sem[p + "max_ready"], 1)
        yield
    dve.wait_ge(sem[p + "max_ready"], H)
    for t in range(NT):
        negmax = k.row_negmax[:, t, :].unsqueeze(1).broadcast_to([P, P // HB, H])
        step(nc.vector.tensor_copy(k.max_parts[:, t, :, 0, :], negmax))
        last = nc.vector.tensor_tensor(k.max_parts[:, t, :, 1, :], negmax, k.max_parts[:, t, :, 0, :],
                                       ALU.subtract)
        if t < NT - 1:
            step(last)
    last.then_inc(sem[p + "max_ready"], 1)
    yield
    for h in range(H):
        yield
    yield
    for t in range(NT):
        dve.wait_ge(sem[p + "heads_psum"], t + 1)
        ov = k.bank[6 + t][:].rearrange("p (h d) -> p h d", h=H)
        step(nc.vector.reciprocal(k.rsum[:, t, :], ov[:, :, HD]))
        nc.vector.tensor_tensor(k.o[:, t, :].rearrange("p (h d) -> p h d", d=HD), ov[:, :, 0:HD],
                                k.rsum[:, t, :].unsqueeze(2).broadcast_to([P, H, HD]), ALU.mult)\
            .then_inc(sem[p + "o_ready"], 1)
    yield
    if kind == "cross":
        dve.wait_ge(sem[p + "y_done"], 1)
        add_to_x(nc, k, step, k.bank[7], k.tanh_g[:, 1:2], w.tbo)
        yield
        yield
        return
    dve.wait_ge(sem[p + "logits"], 1)
    step(nc.vector.tensor_tensor(k.glog[:], k.bank[5][:, 0:NT * NG].rearrange("p (t n) -> p t n", t=NT),
                                 k.brs_row[:].unsqueeze(1).broadcast_to([P, NT, NG]), ALU.add))
    parts = ((0, H - 1), (H - 1, NG))
    for m, (a, b) in enumerate(parts):
        step(nc.vector.tensor_reduce(k.gmax[:, m, :], k.glog[:, :, a:b], axis=AX.X, op=ALU.max))
    for m, (a, b) in enumerate(parts):
        last = nc.vector.tensor_tensor(k.glog[:, :, a:b], k.glog[:, :, a:b],
                                       k.gmax[:, m, :].unsqueeze(2).broadcast_to([P, NT, b - a]), ALU.subtract)
        if m == 0:
            step(last)
    last.then_inc(sem[p + "glog"], 1)
    yield
    dve.wait_ge(sem[p + "gexp"], 1)
    for m, (a, b) in enumerate(parts):
        step(nc.vector.tensor_reduce(k.gsum[:, m, :], k.gexp[:, :, a:b], axis=AX.X, op=ALU.add))
    step(nc.vector.reciprocal(k.gsum[:], k.gsum[:]))
    for m, (a, b) in enumerate(parts):
        step(nc.vector.tensor_tensor(k.gexp[:, :, a:b], k.gexp[:, :, a:b],
                                     k.gsum[:, m, :].unsqueeze(2).broadcast_to([P, NT, b - a]), ALU.mult))
    for t in range(NT):
        step(nc.vector.max(k.top8[:, t, :], k.gexp[:, t, 0:H - 1]))
    step(nc.vector.tensor_reduce(k.gscale[:, 0, :], k.top8[:, :, 0:TOP], axis=AX.X, op=ALU.add))
    step(nc.vector.tensor_reduce(k.gscale[:, 1, :], k.gexp[:, :, H - 1:NG], axis=AX.X, op=ALU.add))
    step(nc.vector.scalar_tensor_tensor(k.gscale[:, 0, :], k.gscale[:, 0, :], 2.0 * TOP,
                                        k.gexp[:, :, NG - 1], ALU.mult, ALU.mult))
    step(nc.vector.scalar_tensor_tensor(k.gscale[:, 1, :], k.gscale[:, 1, :], 2.0,
                                        k.gexp[:, :, NG - 2], ALU.mult, ALU.mult))
    step(nc.vector.tensor_tensor(k.gscale[:, 0, :], k.gscale[:, 0, :], k.gscale[:, 1, :], ALU.add))
    step(nc.vector.tensor_scalar(k.gscale[:, 0, :], k.gscale[:, 0, :], k.tanh_g[:, 3:4], None, ALU.mult))
    dve.wait_ge(sem[p + "y_done"], 1)
    x = k.norm.x
    for t in range(NT):
        step(nc.vector.scalar_tensor_tensor(x[:, t, :], k.bank[7][:, t * D:(t + 1) * D],
                                            k.gscale[:, 0, t:t + 1], x[:, t, :], ALU.mult, ALU.add))
    nc.vector.tensor_tensor(x[:], x[:], w.tbo[:].unsqueeze(1).broadcast_to([P, NT, D]), ALU.add)\
        .then_inc(sem[p + "x_ready"], 1)
    yield


def run_pass(nc, k, core, rest):
    sem = k.sem
    with nc.Block() as block:
        @block.sync
        def _(sp):
            if rest is not None:
                for t in range(NT):
                    sp.dma_start(k.ctx[:, t, :], k.ctx_rows(rest, t)).then_inc(sem["loads"], 16)
                    sp.dma_start(k.norm.x[:, t, :], k.x_rows(rest, t)).then_inc(sem["loads"], 16)
                sp.wait_ge(sem["gated_x_ready"], 1)
                for t in range(NT):
                    sp.dma_start(k.out_rows(rest, t), k.norm.x[:, t, :]).then_inc(sem["stores"], 16)
                sp.wait_ge(sem["stores"], 16 * NT)

        @block.gpsimd
        def _(pool):
            side = side_pool(nc, k, pool) if rest is not None else iter(())
            if core is not None:
                core_pool(nc, k, pool, side)
            for _ in side:
                pass

        @block.tensor
        def _(pe):
            side = side_tensor(nc, k, pe) if rest is not None else iter(())
            if core is not None:
                core_tensor(nc, k, pe, side)
            for _ in side:
                pass

        @block.scalar
        def _(act):
            if core is not None:
                for t in range(NT):
                    act.dma_start(k.core_ctx[:, t, :], k.ctx_rows(core, t)).then_inc(sem["core_loads"], 16)
                    act.dma_start(k.core_norm.x[:, t, :], k.x_rows(core, t)).then_inc(sem["core_loads"], 16)
            side = side_scalar(nc, k, act) if rest is not None else iter(())
            if core is not None:
                core_scalar(nc, k, act, side)
            for _ in side:
                pass

        @block.vector
        def _(dve):
            side = side_vector(nc, k, dve) if rest is not None else iter(())
            if core is not None:
                step = stepper(dve, sem["dve_core"])
                core_vector(nc, k, dve, step, side)
            for _ in side:
                pass
            if core is not None:
                core_tail(nc, k, dve, step)
    zero(nc, k)


def build(nc, x, ctx_in, g_xattn, g_ffn, Wq0, bq0, Wk0, bk0, Wv0, bv0, Wo0, bo0, pos_emb,
          gate_w, gate_b, w1, b1, w3, b3, w2, b2, sw1, sb1, sw3, sb3, sw2, sb2,
          wq1, bq1, wkv1, bkv1, wo1, bo1, Wq2, bq2, Wk2, bk2, Wv2, bv2, Wp2, bp2, Wr, br, Ws, bs,
          temperature, query_emb, out):
    with ExitStack() as ctx:
        k = Kernel()
        k.stack = ctx

        def sb(name, shape, dt=F32):
            return k.stack.enter_context(nc.sbuf_tensor(name, shape, dt))

        k.sem = {name: ctx.enter_context(nc.semaphore(name)) for name in SEMS}
        k.banks = ctx.enter_context(nc.psum_tensor("banks", [P, 8, 512], F32))
        k.bank = [k.banks[:, n, :] for n in range(8)]

        k.wq_cope = sb("wq_cope", [P, NC, D])
        k.wk_cope = sb("wk_cope", [P, NC, D])
        k.wv_cope = sb("wv_cope", [P, NC, D])
        k.wo_cope = sb("wo_cope", [P, NC, D])
        k.wq_cross = sb("wq_cross", [P, NC, D])
        k.wk_cross = sb("wk_cross", [P, NC, D])
        k.wv_cross = sb("wv_cross", [P, NC, D])
        k.wo_cross = sb("wo_cross", [P, NC, D])
        k.wq_gated = sb("wq_gated", [P, NC, D])
        k.wk_gated = sb("wk_gated", [P, NC, D])
        k.wv_gated = sb("wv_gated", [P, NC, D])
        k.wo_gated = sb("wo_gated", [P, NC, D])
        k.w1 = sb("w1", [P, NE, 2, NC, 2, F], F16)
        k.w3 = sb("w3", [P, NE, 2, NC, 2, F], F16)
        k.w2 = sb("w2", [P, NE, 2, D])
        k.b1 = sb("b1", [P, 2, 2, NE])
        k.b3 = sb("b3", [P, 2, 2, NE])
        k.b2 = sb("b2", [NE, D])
        k.wgate = sb("wgate", [P, NC, E])
        k.wrs = sb("wrs", [P, NC, NG])
        k.table = sb("table", [P, S], F16)
        k.first = sb("first", [P, HG])
        k.select = sb("select", [P, 2, 2, P], F16)
        k.bq_cope = sb("bq_cope", [P, NC])
        k.bk_cope = sb("bk_cope", [P, NC])
        k.bq_cross = sb("bq_cross", [P, NC])
        k.bk_cross = sb("bk_cross", [P, NC])
        k.bk_gated = sb("bk_gated", [P, NC])
        k.bo_cope = sb("bo_cope", [P, D])
        k.bo_cross = sb("bo_cross", [P, D])
        k.bq_gated = sb("bq_gated", [P, D])
        k.bv_gated = sb("bv_gated", [P, D])
        k.bo_gated = sb("bo_gated", [P, D])
        k.qe_row = sb("qe_row", [P, D])
        k.temp_row = sb("temp_row", [P, H])
        k.gate_b = sb("gate_b", [P, E])
        k.brs_row = sb("brs_row", [P, NG])
        k.g_raw = sb("g_raw", [P, 4])
        k.tanh_g = sb("tanh_g", [P, 4])
        k.ident = sb("ident", [P, P])
        k.ident16 = sb("ident16", [P, P], BF16)
        k.pick = sb("pick", [P, H], BF16)
        k.neghalf = sb("neghalf", [P, NT * H])
        k.half = sb("half", [P, 1])
        k.cap = sb("cap", [P, NT, S + 1])
        k.t_row = sb("t_row", [P, S + 1], BF16)
        k.expert_no = sb("expert_no", [P, E])
        preamble = ctx.enter_context(ExitStack())
        k.stack = preamble
        k.temp_tmp = sb("temp_tmp", [P, 3, H])
        k.stage = sb("stage", [P, 26, D])
        k.bias_rows = sb("bias_rows", [NE, 2, 2 * F])
        k.small_rows = sb("small_rows", [32, D])
        k.emb = sb("emb", [P, NPOS + 1])
        k.emb_step = sb("emb_step", [P, NPOS])
        k.odd = sb("odd", [P, 1])
        k.table32 = sb("table32", [P, S])
        k.table16 = sb("table16", [P, S], F16)
        k.pair = sb("pair", [P, 2, HD])
        k.bv_raw = sb("bv_raw", [P, 2, NC])
        k.heads = sb("heads", [P, HG])
        k.t_row32 = sb("t_row32", [P, S + 1])
        k.pick32 = sb("pick32", [P, H])

        k.att = {
            "cross": Attention(wq=k.wq_cross, wk=k.wk_cross, wv=k.wv_cross, wo=k.wo_cross,
                               bq=k.bq_cross, bk=k.bk_cross, bv=None, tbo=k.bo_cross),
            "gated": Attention(wq=k.wq_gated, wk=k.wk_gated, wv=k.wv_gated, wo=k.wo_gated,
                               bq=k.bq_gated, bk=k.bk_gated, bv=k.bv_gated, tbo=k.bo_gated),
        }
        k.x_rows = lambda i, t: x[bass.ds(i, 1), t * P:(t + 1) * P, :].rearrange("a p n -> p (a n)")
        k.ctx_rows = lambda i, t: ctx_in[bass.ds(i, 1), t * P:(t + 1) * P, :].rearrange("a p n -> p (a n)")
        k.out_rows = lambda i, t: out[bass.ds(i, 1), t * P:(t + 1) * P, :].rearrange("a p n -> p (a n)")
        sem = k.sem

        with nc.Block() as block:
            @block.gpsimd
            def _(pool):
                step = stepper(pool, sem["pool_step"])
                exact = dict(channel_multiplier=0, allow_small_or_imprecise_dtypes=True)
                nc.gpsimd.iota(k.cap[:], pattern=[[0, NT], [-1, S + 1]], base=S - NPOS + 1, **exact)\
                    .then_inc(sem["consts"], 1)
                nc.gpsimd.iota(k.t_row32[:], pattern=[[-1, S + 1]], base=S - 1, **exact)
                nc.gpsimd.iota(k.expert_no[:], pattern=[[1, E]], base=0, **exact)
                step(nc.gpsimd.memset(k.ident[:], 0.0))
                nc.gpsimd.affine_select(out=k.ident[:], in_=k.ident[:], compare_op=ALU.not_equal, fill=1.0,
                                        base=0, pattern=[[-1, P]], channel_multiplier=1)\
                    .then_inc(sem["consts"], 1)
                step(nc.gpsimd.memset(k.pick32[:], 0.0))
                for base in (0, -H, -64, -64 - H):
                    step(nc.gpsimd.affine_select(out=k.pick32[:], in_=k.pick32[:], compare_op=ALU.not_equal,
                                                 fill=1.0, base=base, pattern=[[-1, H]], channel_multiplier=1))
                step(nc.gpsimd.memset(k.pair[:], 0.0))
                for base in range(0, -P, -HB):
                    step(nc.gpsimd.affine_select(out=k.pair[:], in_=k.pair[:], compare_op=ALU.not_equal,
                                                 fill=1.0, base=base, pattern=[[-HD, 2], [-1, HD]],
                                                 channel_multiplier=1))
                step(nc.gpsimd.memset(k.heads[:], 1.0))
                step(nc.gpsimd.affine_select(out=k.heads[:], in_=k.heads[:], compare_op=ALU.is_ge, fill=0.0,
                                             base=0, pattern=[[-HD, HG]], channel_multiplier=1))
                nc.gpsimd.affine_select(out=k.heads[:], in_=k.heads[:], compare_op=ALU.is_ge, fill=0.0,
                                        base=HD - 1, pattern=[[HD, HG]], channel_multiplier=-1)\
                    .then_inc(sem["consts"], 1)

            @block.vector
            def _(dve):
                step = stepper(dve, sem["step"])
                dve.wait_ge(sem["consts"], 1)
                step(nc.vector.tensor_scalar(k.cap[:], k.cap[:], TINY, None, ALU.max))
                nc.vector.memset(k.cap[:, :, S:S + 1], TINY)
                nc.vector.memset(k.half[:], 0.5)
                nc.vector.memset(k.neghalf[:], -0.5)
                nc.vector.memset(k.emb[:], 0.0)
                nc.vector.memset(k.small_rows[:], 0.0)
                dve.wait_ge(sem["consts"], 3)
                nc.vector.tensor_copy(k.ident16[:], k.ident[:])
                nc.vector.tensor_copy(k.pick[:], k.pick32[:])
                nc.vector.tensor_copy(k.t_row[:], k.t_row32[:])
                nc.vector.tensor_reduce(k.odd[:], k.heads[:, 1::2], axis=AX.X, op=ALU.add)
                step(nc.vector.memset(k.select[:], 0.0))
                copies = "p (a c d) -> p a c d"
                for order, part, which in ((0, 0, slice(0, 2)), (0, 1, slice(2, 4)),
                                           (1, 0, slice(0, 4, 2)), (1, 1, slice(1, 4, 2))):
                    nc.vector.tensor_copy(k.select[:, order, part, :].rearrange(copies, a=2, c=4)[:, :, which, :],
                                          k.pair[:].unsqueeze(2).broadcast_to([P, 2, 2, HD]))
        zero(nc, k)

        def expert_group(a1, a3, a2, at):
            half = P // 2
            group = []
            for dst, src in ((k.w1, a1), (k.w3, a3)):
                group.append((src, [[dst[:, at, part, :, :, r * half:(r + 1) * half]
                                     .rearrange("p e c t j -> p (e c) t j") for part in range(2)]
                                    for r in range(2 * F // P)], "parity"))
            group.append((a2, [k.w2[:, at, :, r * P:(r + 1) * P].rearrange("p e f n -> p (e f) n")
                               for r in range(D // P)], "half"))
            return group

        flat = "e r n -> (e r) n"
        with nc.Fori(0, E // 2) as e:
            transpose_weights(nc, k, [expert_group(w1[bass.ds(i, 1)].rearrange(flat),
                                                   w3[bass.ds(i, 1)].rearrange(flat),
                                                   w2[bass.ds(i, 1)].rearrange(flat), bass.ds(i, 1))
                                      for i in (e * 2, e * 2 + 1)])

        row = lambda a: a.rearrange("(o n) -> o n", o=1)
        columns = lambda dst, a: [(dst[:, g:g + 1], a[g * P:(g + 1) * P].rearrange("(p o) -> p o", o=1))
                                  for g in range(NC)]
        small = [(k.bias_rows[0:E, 0, :], b1), (k.bias_rows[E:NE, 0, :], row(sb1)),
                 (k.bias_rows[0:E, 1, :], b3), (k.bias_rows[E:NE, 1, :], row(sb3)),
                 (k.b2[0:E, :], b2), (k.b2[E:NE, :], row(sb2)),
                 (k.small_rows[0:E, :], gate_w), (k.small_rows[E:E + H - 1, :], Wr),
                 (k.small_rows[E + H - 1:E + NG, :], Ws)]
        for dst, src in ((k.bq_cope, bq0), (k.bq_cross, bq1), (k.bk_cope, bk0),
                         (k.bk_cross, bkv1[0:D]), (k.bk_gated, bk2),
                         (k.bv_raw[:, 0, :], bv0), (k.bv_raw[:, 1, :], bkv1[D:2 * D])):
            small += columns(dst, src)
        chunks = "(c p) n -> p c n"
        small += [(k.wq_cross[:], wq1.rearrange(chunks, p=P)), (k.wk_cross[:], wkv1[:, 0:D].rearrange(chunks, p=P)),
                  (k.wv_cross[:], wkv1[:, D:2 * D].rearrange(chunks, p=P)),
                  (k.wo_cross[:], wo1.rearrange(chunks, p=P))]
        small += [(dst[:], row(src).broadcast_to([P, src.shape[0]]))
                  for dst, src in ((k.bo_cope, bo0), (k.bo_cross, bo1),
                                   (k.bq_gated, bq2), (k.bv_gated, bv2), (k.bo_gated, bp2),
                                   (k.gate_b, gate_b))]
        small += [(k.qe_row[:], query_emb.rearrange("h o d -> o (h d)").broadcast_to([P, D])),
                  (k.temp_row[:], temperature.rearrange("h a b -> (a b) h").broadcast_to([P, H])),
                  (k.brs_row[:, 0:H - 1], row(br).broadcast_to([P, H - 1])),
                  (k.brs_row[:, H - 1:NG], row(bs).broadcast_to([P, 2])),
                  (k.g_raw[:, 0:2], row(g_xattn).broadcast_to([P, 2])),
                  (k.g_raw[:, 2:4], row(g_ffn).broadcast_to([P, 2]))]
        small += [(k.emb[HD * j:HD * (j + 1), 0:NPOS], pos_emb) for j in range(HG)]
        plain = [[(src, [dst[:, :, r * P:(r + 1) * P] for r in range(D // P)], "plain") for dst, src in some]
                 for some in (((k.wq_cope, Wq0), (k.wk_cope, Wk0), (k.wv_cope, Wv0), (k.wo_cope, Wo0)),
                              ((k.wq_gated, Wq2), (k.wk_gated, Wk2), (k.wv_gated, Wv2), (k.wo_gated, Wp2)))]
        transpose_weights(nc, k, [expert_group(sw1, sw3, sw2, slice(E, NE))] + plain, small)
        with nc.Block() as block:
            @block.scalar
            def _(act):
                step = stepper(act, sem["dve_side"])
                step(nc.scalar.activation(k.tanh_g[:], k.g_raw[:], ACT.Tanh))
                act.wait_ge(sem["consts"], 1)
                step(nc.scalar.activation(k.temp_tmp[:, 1, :], k.temp_tmp[:, 0, :], ACT.Exp, scale=-1.0))
                step(nc.scalar.activation(k.temp_tmp[:, 2, :], k.temp_tmp[:, 1, :], ACT.Ln, bias=1.0))

            @block.tensor
            def _(pe):
                for n, w in enumerate((k.wo_cope, k.wo_cross)):
                    for c in range(NC):
                        last = nc.tensor.matmul(k.bank[n][:, 0:D], k.bv_raw[:, n, c:c + 1].broadcast_to([P, P]),
                                                w[:, c, :], start=(c == 0), stop=(c == NC - 1))
                last.then_inc(sem["transposed"], 1)

            @block.vector
            def _(dve):
                step = stepper(dve, sem["step"])
                nc.vector.scalar_tensor_tensor(k.temp_tmp[:, 0, :], k.temp_row[:], -1.0, k.temp_row[:],
                                               ALU.mult, ALU.max)\
                    .then_inc(sem["consts"], 1)
                step(nc.vector.tensor_copy(k.emb[:, NPOS:NPOS + 1], k.emb[:, NPOS - 1:NPOS]))
                step(nc.vector.tensor_tensor(k.emb_step[:], k.emb[:, 1:NPOS + 1], k.emb[:, 0:NPOS], ALU.subtract))
                step(nc.vector.tensor_scalar(k.table32[:].rearrange("p (r b) -> p r b", b=NPOS),
                                             k.emb_step[:, ::-1].unsqueeze(1).broadcast_to([P, S // NPOS, NPOS]),
                                             1.0 / INV_SQRT_HD, None, ALU.mult))
                step(nc.vector.tensor_copy(k.table16[:], k.table32[:]))
                step(nc.vector.tensor_scalar(k.table16[:], k.table16[:], k.odd[:], None, ALU.mult))
                step(nc.vector.tensor_tensor(k.table[:], k.table32[:], k.table16[:], ALU.subtract))
                nc.vector.tensor_scalar(k.first[:], k.heads[:], k.emb[:, 0:1], 1.0 / INV_SQRT_HD,
                                        ALU.mult, ALU.mult)
                dve.wait_ge(sem["dve_side"], 3)
                step(nc.vector.scalar_tensor_tensor(k.temp_row[:], k.temp_row[:], 0.0, k.temp_tmp[:, 2, :],
                                                    ALU.max, ALU.add))
                dve.wait_ge(sem["transposed"], 1)
                for n, b in enumerate((k.bo_cope, k.bo_cross)):
                    step(nc.vector.tensor_tensor(b[:], b[:], k.bank[n][:, 0:D], ALU.add))
                for n, b in ((0, k.bo_cope), (1, k.bo_cross), (3, k.bo_gated)):
                    nc.vector.tensor_scalar(b[:], b[:], k.tanh_g[:, n:n + 1], None, ALU.mult)
        zero(nc, k)
        with nc.Block() as block:
            @block.tensor
            def _(pe):
                for n in range(2):
                    for par in range(2):
                        for f in range(2):
                            at = (2 * n + par) * 2 + f
                            src = k.bias_rows[:, n, :].rearrange("e (f j t) -> e t f j", f=2, t=2)[:, par, f, :]
                            nc.tensor.transpose(k.bank[0][:, at * 16:at * 16 + NE], src, k.ident[0:NE, 0:NE])
                for c in range(NC):
                    last = nc.tensor.transpose(k.bank[2][:, c * 32:(c + 1) * 32],
                                               k.small_rows[:, c * P:(c + 1) * P], k.ident[0:32, 0:32])
                last.then_inc(sem["transposed"], 1)

            @block.vector
            def _(dve):
                dve.wait_ge(sem["transposed"], 1)
                src = k.bank[0][:, 0:128].rearrange("p (m e) -> p m e", e=16)
                for n, (dst, scale) in enumerate(((k.b1, 1.0 / SCALE), (k.b3, SCALE))):
                    nc.vector.tensor_scalar(dst[:].rearrange("p t f e -> p (t f) e"),
                                            src[:, 4 * n:4 * n + 4, 0:NE], scale, None, ALU.mult)
                src = k.bank[2][:, 0:64].rearrange("p (c n) -> p c n", c=NC)
                nc.vector.tensor_copy(k.wgate[:], src[:, :, 0:E])
                nc.vector.tensor_copy(k.wrs[:], src[:, :, E:E + NG])
        zero(nc, k)

        preamble.close()
        k.stack = ctx
        k.core_queries = sb("core_queries", [P, H // 2, S], F16)
        k.core_keys = sb("core_keys", [P, H // 2, S], F16)
        k.core_v = sb("core_v", [P, NT, D + HD])
        k.core_oH = sb("core_oH", [P, H // 4, S])
        k.core_offset = sb("core_offset", [P, NT * H])
        k.gate = sb("gate", [P, NT, S + 1])
        k.c = sb("c", [P, NT, S + 1])
        k.low = sb("low", [P, NT, S])
        k.diff = sb("diff", [P, NT, S])
        k.shift = sb("shift", [P, NT, S + 1], I16)
        mask = sb("mask", [P, NT, S], I16)
        masks = k.diff[:].rearrange("p t s -> p (t s)").bitcast(I16).rearrange("p (n t s) -> p n t s", n=2, t=NT)
        k.mask = [masks[:, 0], masks[:, 1], mask[:]]
        k.shift16 = sb("shift16", [P, NT, S + 1], BF16)
        k.minus_u = sb("minus_u", [P, NT, S + 1], BF16)
        k.neg_rest = sb("neg_rest", [P, NT, S])
        k.rises = sb("rises", [P, NT, S], BF16)
        k.slope = sb("slope", [P, NT, S])
        k.steps = sb("steps", [P, NT, S])
        k.partial = sb("partial", [P, NT, S])
        k.core_scores = sb("core_scores", [P, 2, NT, S])
        k.z = sb("z", [P, 2, NT, S])
        k.rowmax = sb("rowmax", [P, NT])
        k.negmax = sb("negmax", [P, 2, NT])
        k.core_prob = sb("core_prob", [P, NT, S])
        k.core_pT = sb("core_pT", [P, 2, NT, S])
        k.core_sums = sb("core_sums", [P, NT, H])
        k.core_rsum = sb("core_rsum", [P, NT, H])

        def norm(name, x, xn, xT):
            n = Norm()
            n.x, n.xn, n.xT = x, xn, xT
            n.stats = sb(name + "stats", [P, NT, 6])
            n.mean_var = sb(name + "mean_var", [P, NT, 2])
            n.var = sb(name + "var", [P, NT])
            n.rstd = sb(name + "rstd", [P, NT])
            return n

        k.core_ctx, k.core_ctxT = k.z[:, 0], k.core_prob
        k.core_norm = norm("core_", k.core_pT[:, 0], k.z[:, 1], k.steps)

        k.core_qT = k.partial
        halves = lambda b: b.rearrange("p a s -> p (a s)").bitcast(F16).rearrange("p (n c s) -> p n c s", n=2, c=NC)
        k.core_k_parts, k.core_q_parts = halves(k.core_pT[:, 1]), halves(k.slope[:])

        k.norm = norm("side_", sb("x", [P, NT, D])[:], sb("xn", [P, NT, D])[:], sb("xT", [P, NC, S])[:])
        k.ctxT = sb("ctxT", [P, NC, S])
        k.h1 = sb("h1", [P, 2, 2, S])
        k.eg_eth = sb("eg_eth", [P, 2, NT, S])
        k.v = sb("v", [P, NT, H * (HD + 1) + HD])
        v_heads = k.v[:, :, 0:H * (HD + 1)].rearrange("p t (h d) -> p t h d", h=H)
        k.v_heads = v_heads[:, :, :, 0:HD]
        k.o = sb("o", [P, NT, D])
        k.u = sb("u", [P, 2, 2, S])
        k.a = sb("a", [P, 2, 2, S])
        k.cw = sb("cw", [P, NT, NE])
        small = sb("small", [P, S])
        small16 = small[:].bitcast(BF16)
        k.sumsq = sb("sumsq", [P, NT * H])
        k.rnorm = sb("rnorm", [P, NT * H])
        k.row_negmax = sb("row_negmax", [P, NT, H])
        k.rsum = sb("rsum", [P, NT, H])
        k.glog = sb("glog", [P, NT, NG])
        k.gexp = sb("gexp", [P, NT, NG])
        k.gmax = sb("gmax", [P, 2, NT])
        k.gsum = sb("gsum", [P, 2, NT])
        k.gscale = sb("gscale", [P, 2, NT])
        k.top8 = sb("top8", [P, NT, 8])
        k.escore = sb("escore", [P, NT, E])
        k.ebiased = sb("ebiased", [P, NT, E])
        k.enegmax = sb("enegmax", [P, NT])
        k.esum = sb("esum", [P, NT])
        k.etop = sb("etop", [P, NT, 8])
        k.eidx = sb("eidx", [P, NT, 8], U32)
        k.eidxf = sb("eidxf", [P, NT, 8])
        k.ehot = sb("ehot", [P, E])
        flat2 = "p t s -> p (t s)"
        k.ctx, k.qn, k.qsq, k.pT, k.acc, k.oH = k.u[:, 0], k.u[:, 0], k.u[:, 1], k.a, k.o, k.u[:].rearrange("p a b s -> p (a b) s")
        stacks = lambda b: b[:].rearrange("p a b s -> p (a b s)").bitcast(F16).rearrange("p (n s) -> p n s", s=S)
        k.cwT, k.maxT, k.oT = small[0:NE, :], small16[:, 0:S], k.h1[:, 0]
        k.max_parts = small16[:, S:2 * S].rearrange("p (t r m h) -> p t r m h", t=NT, m=2, h=H)
        k.keys, k.queries = stacks(k.h1), stacks(k.eg_eth)
        k.k_parts, k.q_parts = halves(k.a[:, 0]), halves(k.a[:, 1])
        k.eg, k.el, k.eth = (b.rearrange(flat2) for b in (k.eg_eth[:, 0], k.norm.xT, k.eg_eth[:, 1]))
        k.x_parts = halves(k.norm.xn)

        with nc.Block() as block:
            @block.vector
            def _(dve):
                nc.vector.memset(k.gate[:, :, S:S + 1], RESET)
                nc.vector.memset(k.shift[:, :, S:S + 1], 0)
                nc.vector.memset(v_heads[:, :, :, HD:HD + 1], 1.0)
                nc.vector.memset(k.v[:, :, H * (HD + 1):], 0.0)
                nc.vector.memset(k.core_v[:, :, D:], 0.0)
                nc.vector.memset(k.cw[:, :, E:NE], 1.0)

        run_pass(nc, k, 0, None)
        with nc.Fori(1, B) as i:
            run_pass(nc, k, i, i - 1)
        run_pass(nc, k, None, B - 1)


_INS = ['x', 'ctx_1024', 'g_xattn', 'g_ffn', 'L0_xattn_Wq_w', 'L0_xattn_Wq_b', 'L0_xattn_Wk_w', 'L0_xattn_Wk_b',
        'L0_xattn_Wv_w', 'L0_xattn_Wv_b', 'L0_xattn_Wo_w', 'L0_xattn_Wo_b', 'L0_xattn_pos_emb', 'L0_ffn_gate_w',
        'L0_ffn_gate_b', 'L0_ffn_w1', 'L0_ffn_b1', 'L0_ffn_w3', 'L0_ffn_b3', 'L0_ffn_w2', 'L0_ffn_b2',
        'L0_ffn_sw1', 'L0_ffn_sb1', 'L0_ffn_sw3', 'L0_ffn_sb3', 'L0_ffn_sw2', 'L0_ffn_sb2', 'L1_xattn_w_q',
        'L1_xattn_b_q', 'L1_xattn_w_kv', 'L1_xattn_b_kv', 'L1_xattn_w_out', 'L1_xattn_b_out', 'L1_ffn_Wq',
        'L1_ffn_bq', 'L1_ffn_Wk', 'L1_ffn_bk', 'L1_ffn_Wv', 'L1_ffn_bv', 'L1_ffn_Wp', 'L1_ffn_bp', 'L1_ffn_Wr',
        'L1_ffn_br', 'L1_ffn_Ws', 'L1_ffn_bs', 'L1_ffn_temperature', 'L1_ffn_query_embedding']


def kernel(**inputs):
    import numpy as _np
    import concourse.bacc as _bacc
    from concourse import mybir as _mybir
    from concourse.bass_utils import run_bass_kernel_spmd as _run

    nc = _bacc.Bacc("TRN2", target_bir_lowering=False, num_devices=1)
    arrays, args = {}, []
    for name in _INS:
        a = _np.ascontiguousarray(inputs[name])
        arrays[f"in_{name}"] = a
        args.append(nc.dram_tensor(f"in_{name}", a.shape, _mybir.dt.from_np(a.dtype), kind="ExternalInput").ap())
    out = nc.dram_tensor("out_0", (B, S, D), F32, kind="ExternalOutput").ap()
    build(nc, *args, out)
    return _run(nc, [arrays], core_ids=[0]).results[0]["out_0"]
```
